# Optimizing a Trainium2 kernel written in Bass

```python
import numpy as np
import jax
import jax.numpy as jnp

def _softmax(x, axis=-1):
    return jax.nn.softmax(x, axis=axis)

def _gelu(x):
    return jax.nn.gelu(x, approximate=True)

def _silu(x):
    return jax.nn.silu(x)

def _sigmoid(x):
    return jax.nn.sigmoid(x)

def _layernorm(x, axis=-1, eps=1e-05):
    m = jnp.mean(x, axis=axis, keepdims=True)
    v = jnp.var(x, axis=axis, keepdims=True)
    return (x - m) / jnp.sqrt(v + eps)

def _scatter_add(tgt, idx, src, axis=0):
    return tgt.at[idx].add(src)

def _segment_sum(src, seg, n):
    return jax.ops.segment_sum(src, seg, n)
kernel_name = 'mk_gnn_preln_d4_gnn_r32_01146f'

def setup_inputs(seed: int=0):
    np.random.seed(seed)
    _w = jnp.asarray

    def _rec_inputs():
        import jax
        import jax.numpy as jnp
        _gk = jax.random.key(seed)
        x = -8.776e-05 + 1 * jax.random.normal(jax.random.fold_in(_gk, 1), (10000, 512), jnp.float32)
        src = jax.random.randint(jax.random.fold_in(_gk, 2), (10000,), 0, 10000, jnp.int32)
        dst = jnp.minimum((10000 * jax.random.uniform(jax.random.fold_in(_gk, 3), (10000,)) ** 2.0).astype(jnp.int32), 9999)
        _o = jnp.argsort(dst, stable=True)
        src = src[_o]
        dst = dst[_o]
        return (x, src, dst)
    x, src, dst = _rec_inputs()

    def _L0_gnn_setup():
        import jax, jax.numpy as jnp
        import numpy as np
        N_NODES = 10000

        def gnn_layer(x, W, b, src, dst):
            h = x @ W.T + b
            msgs = h[src]
            agg = jax.ops.segment_sum(msgs, dst, num_segments=N_NODES)
            return jax.nn.relu(agg)
        key = jax.random.key(seed)
        ks = jax.random.split(key, 6)
        d_in, d_hid, d_out = (512, 512, 512)
        E = 5000
        x = jax.random.normal(ks[0], (N_NODES, d_in), dtype=jnp.float32)
        edge_index = jax.random.randint(ks[1], (2, E), 0, N_NODES, dtype=jnp.int64)
        s_in = 1.0 / np.sqrt(d_in)
        s_hid = 1.0 / np.sqrt(d_hid)
        W1 = jax.random.uniform(ks[2], (d_hid, d_in), jnp.float32, -s_in, s_in)
        b1 = jax.random.uniform(ks[3], (d_hid,), jnp.float32, -s_in, s_in)
        W2 = jax.random.uniform(ks[4], (d_out, d_hid), jnp.float32, -s_hid, s_hid)
        b2 = jax.random.uniform(ks[5], (d_out,), jnp.float32, -s_hid, s_hid)
        return {'x': x, 'edge_index': edge_index, 'W1': W1, 'b1': b1, 'W2': W2, 'b2': b2}
    _L0_gnn_all = _L0_gnn_setup()
    _L0_gnn_in = {k: v for k, v in _L0_gnn_all.items() if k in ('W1', 'b1', 'W2', 'b2')}
    del _L0_gnn_all

    def _L1_gnn_setup():
        import jax, jax.numpy as jnp
        import numpy as np
        N, D, E = (50000, 512, 12500)
        LN_EPS = 1e-05
        key = jax.random.key(seed)
        ks = jax.random.split(key, 8)
        x = jax.random.normal(ks[0], (N, D), dtype=jnp.float32)
        edge_index = jax.random.randint(ks[1], (2, E), 0, N, dtype=jnp.int64)
        s = 1.0 / np.sqrt(D)
        W1 = jax.random.uniform(ks[2], (D, D), jnp.float32, -s, s)
        b1 = jax.random.uniform(ks[3], (D,), jnp.float32, -s, s)
        W2 = jax.random.uniform(ks[4], (D, D), jnp.float32, -s, s)
        b2 = jax.random.uniform(ks[5], (D,), jnp.float32, -s, s)
        eps = jnp.zeros((), dtype=jnp.float32)
        gamma = jnp.ones((D,), dtype=jnp.float32)
        beta = jnp.zeros((D,), dtype=jnp.float32)
        return {'x': x, 'edge_index': edge_index, 'eps': eps, 'W1': W1, 'b1': b1, 'W2': W2, 'b2': b2, 'gamma': gamma, 'beta': beta}
    _L1_gnn_all = _L1_gnn_setup()
    _L1_gnn_in = {k: v for k, v in _L1_gnn_all.items() if k in ('eps', 'W1', 'b1', 'W2', 'b2', 'gamma', 'beta')}
    del _L1_gnn_all

    def _L2_gnn_setup():
        import jax, jax.numpy as jnp
        import numpy as np
        N_NODES = 10000
        N_EDGES = 5000
        DIM = 512
        LN_EPS = 1e-05
        key = jax.random.key(seed)
        ks = jax.random.split(key, 6)
        scale = 1.0 / np.sqrt(DIM)
        h = jax.random.normal(ks[0], (N_NODES, DIM), dtype=jnp.float32)
        edge_index = jax.random.randint(ks[1], (2, N_EDGES), 0, N_NODES, dtype=jnp.int32)
        W_self = jax.random.normal(ks[2], (DIM, DIM), dtype=jnp.float32) * scale
        b_self = jnp.zeros((DIM,), dtype=jnp.float32)
        W_neigh = jax.random.normal(ks[3], (DIM, DIM), dtype=jnp.float32) * scale
        b_neigh = jnp.zeros((DIM,), dtype=jnp.float32)
        ln_gamma = jnp.ones((DIM,), dtype=jnp.float32)
        ln_beta = jnp.zeros((DIM,), dtype=jnp.float32)
        return {'h': h, 'edge_index': edge_index, 'W_self': W_self, 'b_self': b_self, 'W_neigh': W_neigh, 'b_neigh': b_neigh, 'ln_gamma': ln_gamma, 'ln_beta': ln_beta}
    _L2_gnn_all = _L2_gnn_setup()
    _L2_gnn_in = {k: v for k, v in _L2_gnn_all.items() if k in ('W_self', 'b_self', 'W_neigh', 'b_neigh', 'ln_gamma', 'ln_beta')}
    del _L2_gnn_all

    def _L3_gnn_setup():
        import jax, jax.numpy as jnp
        import numpy as np
        N_NODES = 10000
        N_EDGES = 5000
        D_FEAT = 512
        OUT_CH = 512
        key = jax.random.key(seed)
        k1, k2, k3, k4 = jax.random.split(key, 4)
        x = jax.random.normal(k1, (N_NODES, D_FEAT), dtype=jnp.float32)
        edge_index = jax.random.randint(k2, (N_EDGES, 2), 0, N_NODES, dtype=jnp.int64)
        W = jax.random.normal(k3, (OUT_CH, 2 * D_FEAT), dtype=jnp.float32) / np.sqrt(2 * D_FEAT)
        b = jax.random.normal(k4, (OUT_CH,), dtype=jnp.float32) * 0.01
        return {'x': x, 'edge_index': edge_index, 'num_local_nodes': N_NODES, 'W': W, 'b': b}
    _L3_gnn_all = _L3_gnn_setup()
    _L3_gnn_in = {k: v for k, v in _L3_gnn_all.items() if k in ('W', 'b')}
    del _L3_gnn_all
    return {'x': x, 'src': src, 'dst': dst, 'L0_gnn_W1': _L0_gnn_in['W1'], 'L0_gnn_b1': _L0_gnn_in['b1'], 'L0_gnn_W2': _L0_gnn_in['W2'], 'L0_gnn_b2': _L0_gnn_in['b2'], 'L1_gnn_eps': _L1_gnn_in['eps'], 'L1_gnn_W1': _L1_gnn_in['W1'], 'L1_gnn_b1': _L1_gnn_in['b1'], 'L1_gnn_W2': _L1_gnn_in['W2'], 'L1_gnn_b2': _L1_gnn_in['b2'], 'L1_gnn_gamma': _L1_gnn_in['gamma'], 'L1_gnn_beta': _L1_gnn_in['beta'], 'L2_gnn_W_self': _L2_gnn_in['W_self'], 'L2_gnn_b_self': _L2_gnn_in['b_self'], 'L2_gnn_W_neigh': _L2_gnn_in['W_neigh'], 'L2_gnn_b_neigh': _L2_gnn_in['b_neigh'], 'L2_gnn_ln_gamma': _L2_gnn_in['ln_gamma'], 'L2_gnn_ln_beta': _L2_gnn_in['ln_beta'], 'L3_gnn_W': _L3_gnn_in['W'], 'L3_gnn_b': _L3_gnn_in['b']}

def reference(x, src, dst, L0_gnn_W1, L0_gnn_b1, L0_gnn_W2, L0_gnn_b2, L1_gnn_eps, L1_gnn_W1, L1_gnn_b1, L1_gnn_W2, L1_gnn_b2, L1_gnn_gamma, L1_gnn_beta, L2_gnn_W_self, L2_gnn_b_self, L2_gnn_W_neigh, L2_gnn_b_neigh, L2_gnn_ln_gamma, L2_gnn_ln_beta, L3_gnn_W, L3_gnn_b):
    import jax
    import jax.numpy as jnp

    def _L0_gnn_ref(x, edge_index, W1, b1, W2, b2):
        import jax, jax.numpy as jnp
        import numpy as np
        N_NODES = 10000

        def gnn_layer(x, W, b, src, dst):
            h = x @ W.T + b
            msgs = h[src]
            agg = jax.ops.segment_sum(msgs, dst, num_segments=N_NODES)
            return jax.nn.relu(agg)
        src, dst = (edge_index[0], edge_index[1])
        h = gnn_layer(x, W1, b1, src, dst)
        out = gnn_layer(h, W2, b2, src, dst)
        return out

    def _L1_gnn_ref(x, edge_index, eps, W1, b1, W2, b2, gamma, beta):
        import jax, jax.numpy as jnp
        import numpy as np
        N, D, E = (50000, 512, 12500)
        LN_EPS = 1e-05
        i, j = (edge_index[0], edge_index[1])
        agg = jax.ops.segment_sum(x[j], i, num_segments=x.shape[0])
        h = (1.0 + eps) * x + agg
        h = jax.nn.relu(h @ W1.T + b1)
        h = h @ W2.T + b2
        mu = jnp.mean(h, axis=-1, keepdims=True)
        var = jnp.var(h, axis=-1, keepdims=True)
        out = (h - mu) * jax.lax.rsqrt(var + LN_EPS) * gamma + beta
        return out

    def _L2_gnn_ref(h, edge_index, W_self, b_self, W_neigh, b_neigh, ln_gamma, ln_beta):
        import jax, jax.numpy as jnp
        import numpy as np
        N_NODES = 10000
        N_EDGES = 5000
        DIM = 512
        LN_EPS = 1e-05
        n = h.shape[0]
        src = edge_index[0]
        dst = edge_index[1]
        msg = h[dst] @ W_neigh.T + b_neigh
        neigh = jax.ops.segment_sum(msg, src, num_segments=n)
        deg = jax.ops.segment_sum(jnp.ones(src.shape, h.dtype), src, num_segments=n)
        deg = jnp.maximum(deg, 1.0)
        neigh = neigh / deg[:, None]
        out = jax.nn.relu(h @ W_self.T + b_self + neigh)
        x = h + out
        mean = jnp.mean(x, axis=-1, keepdims=True)
        var = jnp.mean(jnp.square(x - mean), axis=-1, keepdims=True)
        return (x - mean) * jax.lax.rsqrt(var + LN_EPS) * ln_gamma + ln_beta

    def _L3_gnn_ref(x, edge_index, num_local_nodes, W, b):
        import jax, jax.numpy as jnp
        import numpy as np
        N_NODES = 10000
        N_EDGES = 5000
        D_FEAT = 512
        OUT_CH = 512
        src = edge_index[:, 0]
        tgt = edge_index[:, 1]
        x_i = x[src]
        x_j = x[tgt]
        x_ij = jnp.concatenate([x_i, x_j], axis=1)
        m_ij = jax.nn.relu(x_ij @ W.T + b)
        out = jax.ops.segment_sum(m_ij, src, num_segments=num_local_nodes)
        return out
    edge_index = jnp.stack([src, dst])
    edge_index_t = jnp.stack([src, dst], axis=1)
    h = jnp.maximum(_layernorm(x, axis=-1), 0.0)
    x = x + _L0_gnn_ref(h, edge_index, L0_gnn_W1, L0_gnn_b1, L0_gnn_W2, L0_gnn_b2)
    h = jnp.maximum(_layernorm(x, axis=-1), 0.0)
    x = x + _L1_gnn_ref(h, edge_index, L1_gnn_eps, L1_gnn_W1, L1_gnn_b1, L1_gnn_W2, L1_gnn_b2, L1_gnn_gamma, L1_gnn_beta)
    h = jnp.maximum(_layernorm(x, axis=-1), 0.0)
    x = x + _L2_gnn_ref(h, edge_index, L2_gnn_W_self, L2_gnn_b_self, L2_gnn_W_neigh, L2_gnn_b_neigh, L2_gnn_ln_gamma, L2_gnn_ln_beta)
    h = jnp.maximum(_layernorm(x, axis=-1), 0.0)
    x = x + _L3_gnn_ref(h, edge_index_t, 10000, L3_gnn_W, L3_gnn_b)
    return x

_drawn_inputs = setup_inputs


def setup_inputs(seed=0):
    import zlib

    import numpy as np

    out = dict(_drawn_inputs(seed))
    spreads = {'L1_gnn_gamma': (1.0, 0.2),
     'L1_gnn_beta': (0.0, 0.1),
     'L2_gnn_b_self': (0.0, 0.1),
     'L2_gnn_b_neigh': (0.0, 0.273),
     'L2_gnn_ln_gamma': (1.0, 0.2),
     'L2_gnn_ln_beta': (0.0, 0.1)}
    factors = {'L0_gnn_b1': 3.186, 'L3_gnn_b': 8.0}
    for name, (base, spread) in spreads.items():
        noise = np.random.default_rng([zlib.crc32(name.encode()), seed]).standard_normal(out[name].shape)
        drawn = base * np.exp(spread * noise) if base else spread * noise
        out[name] = jnp.asarray(drawn.astype(out[name].dtype))
    for name, factor in factors.items():
        out[name] = (out[name] * factor).astype(out[name].dtype)
    return out
```

```python
from contextlib import ExitStack, contextmanager

import concourse.bass as bass
from concourse import mybir

P = 128
D = 512
C = D // P
EXT = 520
SCALE, BIAS = D, D + 1
SEL = P + 2
LN_EPS = 1e-5
NOWHERE = 1 << 20

F32, F32R, BF16 = mybir.dt.float32, mybir.dt.float32r, mybir.dt.bfloat16
I32, I16 = mybir.dt.int32, mybir.dt.int16
ALU = mybir.AluOpType
ACT = mybir.ActivationFunctionType
AX = mybir.AxisListType


class Tile:

    def __init__(self, k, j, unroll):
        self.k, self.j, self.unroll = k, j, unroll
        self.t = k * unroll + j if j else k * unroll

    def slot(self, ring):
        return self.j % ring

    def use(self, ring):
        each = self.unroll // ring
        n = self.k * each if each > 1 else self.k
        return n + self.j // ring if self.j // ring else n


def at(i, u, off, unroll, tiles, stage):
    tile = Tile(i + (u + off) // unroll, (u + off) % unroll, unroll)
    if not isinstance(i, int) or 0 <= tile.t < tiles:
        stage(tile)


def pipeline(eng, groups, lead, drain, body, ahead=2, between=None):
    first, last = 2, groups - ahead
    for i in range(-lead, first):
        body(i)
        if between and i >= 0:
            between(i)
    with eng.Fori(first, last) as i:
        body(i)
    for i in range(last, groups + drain):
        body(i)


def pairs(eng, groups, lead, drain, body, between=None):
    for i in range(-lead, 2):
        body(i, i % 2)
        if between and i >= 0:
            between(i)
    with eng.Fori(1, groups // 2 - 2) as n:
        body(2 * n, 0)
        body(2 * n + 1, 1)
    for i in range(groups - 4, groups + drain):
        body(i, i % 2)


class Pair:

    def __init__(self, t, slot):
        self.t, self.ring_slot = t, slot

    def slot(self, ring):
        return self.ring_slot


def wait(eng, sem, value):
    if not isinstance(value, int) or value > 0:
        eng.wait_ge(sem, value)


class Env:

    def __init__(self, nc, ctx, prefix):
        self.nc, self.ctx, self.prefix = nc, ctx, prefix
        self.semaphores = []

    def sb(self, name, shape, dt):
        return self.ctx.enter_context(self.nc.sbuf_tensor(self.prefix + name, shape, dt))

    def ring(self, name, n, shape, dt):
        return [self.sb(f"{name}{i}", shape, dt) for i in range(n)]

    def ps(self, name, shape, dt=F32):
        return self.ctx.enter_context(self.nc.psum_tensor(self.prefix + name, shape, dt))

    def sem(self, name):
        self.semaphores.append(self.nc.alloc_semaphore(self.prefix + name))
        return self.semaphores[-1]

    @contextmanager
    def block(self):
        with self.nc.Block() as block:
            yield block
        self.nc.clear_and_free_semaphores(self.semaphores)
        self.nc.all_engine_barrier()
        self.semaphores = []

    def sems(self, name, n):
        return [self.sem(f"{name}{i}") for i in range(n)]


def row_of(vector):
    return vector.rearrange("(a n) -> a n", a=1)



def prepare_orders(nc, io, g):
    NT, N = g.NT, g.N
    KEYS = ("D", "S")
    G4 = NT // 4
    with ExitStack() as ctx:
        e = Env(nc, ctx, "p_")
        sb, ps, sem = e.sb, e.ps, e.sem

        key_i = {k: sb("keyi" + k, [P, NT], I32) for k in KEYS}
        tmp_i = sb("tmpi", [P, NT], I32)
        key_f = {k: sb("keyf" + k, [P, NT], F32) for k in KEYS}
        hi_f = {k: sb("hif" + k, [P, NT], F32) for k in KEYS}
        lo_f = {k: sb("lof" + k, [P, NT], F32) for k in KEYS}
        hirow = {k: g.selrows[k][:, :, :].rearrange("p t c -> p (t c)")[0:NT, 0:N] for k in KEYS}
        iota_i = sb("iotai", [P, P], I32)
        iota_b = sb("iotab", [P, P], BF16)
        iota_f = sb("iotaf", [P, P], F32)
        pidx_i = sb("pidxi", [P, 1], I32)
        pidx = sb("pidx", [P, 1], F32)
        node_i = sb("nodei", [P, NT], I32)
        node_f = sb("nodef", [P, NT], F32)
        ones_f = sb("onesf", [P, P], F32)
        ones_b = sb("onesb", [P, 2], BF16)
        before_f = sb("beforef", [P, P], F32)
        before_b = sb("beforeb", [P, P], BF16)
        neg_half = sb("neghalf", [P, 1], F32)
        count = {k: sb("count" + k, [NT, P], F32) for k in KEYS}
        start = {k: sb("start" + k, [NT, P], F32) for k in KEYS}
        colform = sb("colform", [P, NT], F32)
        total = sb("total", [NT, 1], F32)
        totals = sb("totals", [NT, P], F32)

        pos = {k: sb("pos" + k, [P, NT], F32) for k in KEYS}
        deg = {k: sb("deg" + k, [P, NT], F32) for k in KEYS}
        intile = {k: sb("intile" + k, [P, NT], F32) for k in KEYS}

        c12 = ctx.enter_context(ExitStack())
        first = Env(nc, c12, "q_")
        keyrow = {k: first.sb("keyrow" + k, [P, N], I16) for k in KEYS}
        zero_row = first.sb("zerorow", [P, D], F32)
        spare = g.parts.bitcast(BF16)
        words = NT * P
        OHlo = {k: spare[:, m * words:(m + 1) * words].rearrange("p (t n) -> p t n", n=P)
                for m, k in enumerate(KEYS)}
        OHhi = {"D": spare[:, 2 * words:2 * words + NT * NT].rearrange("p (t n) -> p t n", n=NT),
                "S": first.sb("ohhiS", [P, NT, NT], BF16)}

        s_load = sem("s_load")
        s_rowload = {k: sem("s_rowload" + k) for k in KEYS}
        s_iota = sem("s_iota")
        s_v = sem("s_v")
        s_one = sem("s_one")
        s_cnt = sem("s_cnt")
        s_pe = sem("s_pe")

        with ExitStack() as c1:
            pcount = {k: c1.enter_context(nc.psum_tensor("p_pcount" + k, [P, 512], F32)) for k in KEYS}
            ptr = c1.enter_context(nc.psum_tensor("p_ptr", [P, 512], F32))
            pstart = c1.enter_context(nc.psum_tensor("p_pstart", [P, 512], F32))
            block = c1.enter_context(e.block())

            @block.sync
            def _(sp):
                sp.dma_start(key_i["D"][:, :], io.dst_col).then_inc(s_load, 16)
                sp.dma_start(key_i["S"][:, :], io.src_col).then_inc(s_load, 16)

            @block.gpsimd
            def _(pool):
                pool.dma_start(keyrow["D"][:, :], io.dst.partition_broadcast(P)).then_inc(s_rowload["D"], 16)
                pool.dma_start(keyrow["S"][:, :], io.src.partition_broadcast(P)).then_inc(s_rowload["S"], 16)
                pool.iota(iota_i[:, :], pattern=[[1, P]], base=0, channel_multiplier=0).then_inc(s_iota, 1)
                pool.iota(pidx_i[:, :], pattern=[[0, 1]], base=0, channel_multiplier=1).then_inc(s_iota, 1)
                pool.iota(node_i[:, :], pattern=[[P, NT]], base=0, channel_multiplier=1).then_inc(s_iota, 1)
                pool.memset(g.ident[:, :], 0.0).then_inc(s_iota, 1)
                pool.memset(ones_f[:, :], 1.0)
                pool.memset(ones_b[:, :], 1.0)
                pool.memset(zero_row[:, :], 0.0)
                pool.memset(neg_half[:, :], -0.5)
                pool.wait_ge(s_iota, 4)
                pool.affine_select(out=g.ident[:, :], in_=g.ident[:, :], compare_op=ALU.not_equal, fill=1.0,
                                   base=0, pattern=[[-1, P]], channel_multiplier=1).then_inc(s_iota, 1)

            @block.vector
            def _(dve):
                n = [0]

                def step(ins):
                    ins.then_inc(s_v, 1)
                    n[0] += 1
                    dve.wait_ge(s_v, n[0])

                dve.wait_ge(s_iota, 5)
                step(dve.tensor_copy(iota_b[:, :], iota_i[:, :]))
                step(dve.tensor_copy(iota_f[:, :], iota_i[:, :]))
                step(dve.tensor_copy(pidx[:, :], pidx_i[:, :]))
                step(dve.tensor_copy(node_f[:, :], node_i[:, :]))
                step(dve.tensor_scalar(before_f[:, :], iota_f[:, :], pidx[:, 0:1], None, ALU.is_gt))
                step(dve.tensor_scalar(before_b[:, :], iota_f[:, :], pidx[:, 0:1], None, ALU.is_gt))
                dve.wait_ge(s_load, 32)
                for k in KEYS:
                    step(dve.tensor_copy(key_f[k][:, :], key_i[k][:, :]))
                    step(dve.tensor_scalar(tmp_i[:, :], key_i[k][:, :], 7, None, ALU.logical_shift_right))
                    step(dve.tensor_copy(hi_f[k][:, :], tmp_i[:, :]))
                    step(dve.tensor_scalar(tmp_i[:, :], key_i[k][:, :], P - 1, None, ALU.bitwise_and))
                    step(dve.tensor_copy(lo_f[k][:, :], tmp_i[:, :]))
                with dve.Fori(0, NT) as t:
                    for k in KEYS:
                        dve.tensor_scalar(OHhi[k][:, bass.ds(t, 1), :], iota_b[:, 0:NT],
                                          hi_f[k][:, bass.ds(t, 1)], None, ALU.is_equal)
                        dve.tensor_scalar(OHlo[k][:, bass.ds(t, 1), :], iota_b[:, :],
                                          lo_f[k][:, bass.ds(t, 1)], None, ALU.is_equal).then_inc(s_one, 1)
                for k in KEYS:
                    dve.wait_ge(s_rowload[k], 16)
                    step(dve.tensor_scalar(hirow[k][:, :], keyrow[k][0:NT, :], 7, None, ALU.logical_shift_right))
                for m, k in enumerate(KEYS):
                    dve.wait_ge(s_cnt, m + 1)
                    step(dve.tensor_copy(count[k][:, :], pcount[k][0:NT, 0:P]))
                for m, k in enumerate(KEYS):
                    dve.wait_ge(s_pe, 2 * m + 1)
                    step(dve.tensor_copy(colform[:, :], ptr[:, 0:NT]))
                    step(dve.tensor_reduce(total[:, :], count[k][:, :], AX.X, ALU.add))
                    step(dve.tensor_scalar(totals[:, :], ones_f[0:NT, :], total[:, 0:1], None, ALU.mult))
                    dve.wait_ge(s_pe, 2 * m + 2)
                    step(dve.tensor_copy(start[k][:, :], pstart[0:NT, 0:P]))

            @block.tensor
            def _(pe):
                pe.wait_ge(s_one, 2)
                for k in KEYS:
                    pe.matmul(pcount[k][0:NT, 0:P], OHhi[k][:, 0, :], OHlo[k][:, 0, :], start=True, stop=False)
                with pe.Fori(1, NT - 1) as t:
                    pe.wait_ge(s_one, 2 * t + 2)
                    for k in KEYS:
                        pe.matmul(pcount[k][0:NT, 0:P], OHhi[k][:, bass.ds(t, 1), :], OHlo[k][:, bass.ds(t, 1), :],
                                  start=False, stop=False)
                pe.wait_ge(s_one, 2 * NT)
                for k in KEYS:
                    pe.matmul(pcount[k][0:NT, 0:P], OHhi[k][:, NT - 1, :], OHlo[k][:, NT - 1, :],
                              start=False, stop=True).then_inc(s_cnt, 1)
                pe.wait_ge(s_iota, 5)
                for m, k in enumerate(KEYS):
                    base = 6 + 10 + 2
                    pe.wait_ge(s_v, base + m + 1 if m == 0 else base + 2 + 4)
                    pe.transpose(ptr[:, 0:NT], count[k][:, :], g.ident[0:NT, 0:NT]).then_inc(s_pe, 1)
                    pe.wait_ge(s_v, base + 2 + 4 * m + 3)
                    pe.matmul(pstart[0:NT, 0:P], colform[:, :], before_f[:, :], start=True, stop=False)
                    pe.matmul(pstart[0:NT, 0:P], before_f[0:NT, 0:NT], totals[:, :], start=False, stop=True)\
                        .then_inc(s_pe, 1)

        U = 4
        with ExitStack() as c2:
            f = Env(nc, c2, "r_")
            OHhiT = {k: f.ring("ohhit" + k, 2, [NT, P], F32) for k in KEYS}
            same = {k: f.ring("same" + k, 2, [P, P], BF16) for k in KEYS}
            earlier = {k: f.ring("earlier" + k, 2, [P, P], BF16) for k in KEYS}
            table = {k: f.ring("table" + k, 2, [NT, 2, P], F32) for k in KEYS}
            picked = f.sb("picked", [P, 2, P], F32)
            pair = f.sb("pair", [P, 2], F32)
            xt = f.ring("xt", U, [P, EXT], F32)
            h0 = f.ring("h0", 2, [P, D], F32)
            st = f.ring("st", 2, [P, 6], F32)
            mv = f.ring("mv", 2, [P, 2], F32)
            va = f.ring("va", 2, [P, 1], F32)
            pbase = {k: f.ps("pbase" + k, [P, 512]) for k in KEYS}
            plook = {k: [f.ps(f"plook{k}{j}", [P, 2, P]) for j in range(2)] for k in KEYS}
            pin = f.ps("pin", [P, 512])
            q_tab, q_acc, q_hot, q_eq, q_early, q_look, q_in, q_pick, q_red = (
                {k: f.sem(n + k) for k in KEYS} for n in
                ("q_tab", "q_acc", "q_hot", "q_eq", "q_early", "q_look", "q_in", "q_pick", "q_red"))
            q_x = f.sems("q_x", U)
            q_st, q_mv, q_var, q_a, q_b, q_h = (f.sem(n) for n in ("q_st", "q_mv", "q_var", "q_a", "q_b", "q_h"))
            q_out = f.sems("q_out", 2)
            q_ext = f.sems("q_ext", U)
            q_zero = f.sem("q_zero")
            q_tick = f.sem("q_tick")
            q_done = f.sem("q_done")
            block = c2.enter_context(f.block())
            GR = NT // U

            @block.sync
            def _(sp):
                def load(T):
                    s = T.slot(U)
                    wait(sp, q_h, T.t - U + 1)
                    sp.sem_inc(q_tick, 1)
                    wait(sp, q_ext[s], 16 * T.use(U))
                    sp.sem_inc(q_tick, 1)
                    sp.dma_start(xt[s][:, 0:D], io.x[bass.ds(T.t * P, P), :]).then_inc(q_x[s], 16)

                def store(T):
                    s = T.slot(2)
                    sp.wait_ge(q_h, T.t + 1)
                    sp.sem_inc(q_tick, 1)
                    sp.dma_start(g.h0[bass.ds(T.t * P, P), :], h0[s][:, :]).then_inc(q_out[s], 16)
                    sp.dma_start(g.xs[0][bass.ds(T.t * P, P), :], xt[T.slot(U)][:, :]).then_inc(q_ext[T.slot(U)], 16)
                    sp.dma_start(g.h1[bass.ds(T.t * P, P), :], zero_row[:, :]).then_inc(q_zero, 16)

                def body(i):
                    for u in range(U):
                        at(i, u, 0, U, NT, store)
                        at(i, u, 3, U, NT, load)

                pipeline(sp, GR, 1, 0, body)
                for s in range(2):
                    sp.wait_ge(q_out[s], 16 * (NT // 2))
                for s in range(U):
                    sp.wait_ge(q_ext[s], 16 * GR)
                sp.wait_ge(q_zero, 16 * NT)

            @block.vector
            def _(dve):
                def hot(T):
                    s = T.slot(2)
                    for k in KEYS:
                        wait(dve, q_look[k], T.t - 1)
                        dve.tensor_scalar(OHhiT[k][s][:, :], hirow[k][:, bass.ds(T.t * P, P)], pidx[0:NT, 0:1],
                                          None, ALU.is_equal).then_inc(q_hot[k], 1)
                        wait(dve, q_early[k], T.t - 1)
                        dve.tensor_scalar(same[k][s][:, :], keyrow[k][:, bass.ds(T.t * P, P)],
                                          key_f[k][:, bass.ds(T.t, 1)], None, ALU.is_equal).then_inc(q_eq[k], 1)
                    for k in KEYS:
                        dve.wait_ge(q_eq[k], T.t + 1)
                        wait(dve, q_in[k], T.t - 1)
                        dve.tensor_tensor(earlier[k][s][:, :], same[k][s][:, :], before_b[:, :], ALU.mult)\
                            .then_inc(q_early[k], 1)

                def pick(T):
                    s = T.slot(2)
                    for k in KEYS:
                        dve.wait_ge(q_look[k], T.t + 1)
                        if k == "D":
                            wait(dve, q_red["S"], T.t)
                        else:
                            dve.wait_ge(q_red["D"], T.t + 1)
                        dve.tensor_tensor(picked[:, :, :], plook[k][s][:, :, :],
                                          OHlo[k][:, bass.ds(T.t, 1), :].broadcast_to([P, 2, P]), ALU.mult)\
                            .then_inc(q_pick[k], 1)
                        dve.wait_ge(q_pick[k], T.t + 1)
                        dve.tensor_reduce(pos[k][:, bass.ds(T.t, 1)], picked[:, 0, :], AX.X, ALU.add)
                        dve.tensor_reduce(deg[k][:, bass.ds(T.t, 1)], picked[:, 1, :], AX.X, ALU.add)\
                            .then_inc(q_red[k], 1)

                def norm_x(T):
                    s = T.slot(2)
                    dve.wait_ge(q_x[T.slot(U)], 16 * (T.use(U) + 1))
                    dve.bn_stats(st[s][:, :], xt[T.slot(U)][:, 0:D]).then_inc(q_st, 1)
                    dve.wait_ge(q_st, T.t + 1)
                    wait(dve, q_b, T.t - 1)
                    dve.sem_inc(q_tick, 1)
                    dve.bn_aggr(mv[s][:, :], st[s][:, :]).then_inc(q_mv, 1)

                def body(i):
                    for u in range(U):
                        at(i, u, 1, U, NT, hot)
                        at(i, u, 1, U, NT, norm_x)
                        at(i, u, 0, U, NT, pick)

                pipeline(dve, GR, 1, 0, body)
                for k in KEYS:
                    dve.wait_ge(q_red[k], NT)
                    dve.wait_ge(q_in[k], NT)
                for m, k in enumerate(KEYS):
                    dve.tensor_copy(intile[k][:, :], pin[:, m * P:m * P + NT]).then_inc(q_done, 1)
                    dve.wait_ge(q_done, 2 * m + 1)
                    dve.tensor_tensor(pos[k][:, :], pos[k][:, :], intile[k][:, :], ALU.add).then_inc(q_done, 1)

            @block.gpsimd
            def _(pool):
                def scale(T):
                    s, x = T.slot(2), xt[T.slot(U)]
                    pool.wait_ge(q_mv, T.t + 1)
                    pool.sem_inc(q_tick, 1)
                    pool.tensor_scalar(va[s][:, 0:1], mv[s][:, 1:2], 1.0, LN_EPS, ALU.mult, ALU.add)\
                        .then_inc(q_var, 1)
                    pool.wait_ge(q_var, T.t + 1)
                    pool.tensor_tensor(x[:, SCALE:SCALE + 1], va[s][:, 0:1], neg_half[:, :], ALU.pow).then_inc(q_a, 1)
                    pool.wait_ge(q_a, T.t + 1)
                    pool.sem_inc(q_tick, 1)
                    pool.tensor_scalar(x[:, BIAS:BIAS + 1], mv[s][:, 0:1], x[:, SCALE:SCALE + 1], -1.0,
                                       ALU.mult, ALU.mult)\
                        .then_inc(q_b, 1)

                def body(i):
                    for u in range(U):
                        at(i, u, 0, U, NT, scale)

                for s in range(U):
                    pool.memset(xt[s][:, BIAS + 1:EXT], 0.0)
                pipeline(pool, GR, 0, 0, body)

            @block.scalar
            def _(act):
                def table_of(T):
                    s = T.slot(2)
                    for k in KEYS:
                        act.wait_ge(q_acc[k], T.t + 1)
                        wait(act, q_look[k], T.t - 1)
                        nc.scalar.copy(table[k][s][:, 0, :], pbase[k][0:NT, 0:P]).then_inc(q_tab[k], 1)

                def relu(T):
                    s, x = T.slot(2), xt[T.slot(U)]
                    act.wait_ge(q_b, T.t + 1)
                    wait(act, q_out[s], 16 * T.use(2))
                    nc.scalar.activation(h0[s][:, :], x[:, 0:D], ACT.Relu, bias=x[:, BIAS:BIAS + 1],
                                         scale=x[:, SCALE:SCALE + 1]).then_inc(q_h, 1)

                def body(i):
                    for u in range(U):
                        at(i, u, 0, U, NT, table_of)
                        at(i, u, 0, U, NT, relu)

                for k in KEYS:
                    for s in range(2):
                        nc.scalar.copy(table[k][s][:, 1, :], count[k][:, :])
                pipeline(act, GR, 0, 0, body)

            @block.tensor
            def _(pe):
                for k in KEYS:
                    pe.matmul(pbase[k][0:NT, 0:P], g.ident[0:NT, 0:NT], start[k][:, :], start=True, stop=True,
                              skip_group_check=True).then_inc(q_acc[k], 1)

                def look(T):
                    s = T.slot(2)
                    for m, k in enumerate(KEYS):
                        pe.wait_ge(q_tab[k], T.t + 1)
                        pe.matmul(pbase[k][0:NT, 0:P], OHhi[k][:, bass.ds(T.t, 1), :], OHlo[k][:, bass.ds(T.t, 1), :],
                                  start=False, stop=True, skip_group_check=True).then_inc(q_acc[k], 1)
                        pe.wait_ge(q_hot[k], T.t + 1)
                        wait(pe, q_pick[k], T.t - 1)
                        pe.matmul(plook[k][s][:, :, :], OHhiT[k][s][:, :], table[k][s][:, :, :],
                                  start=True, stop=True).then_inc(q_look[k], 1)
                        pe.wait_ge(q_early[k], T.t + 1)
                        pe.matmul(pin[:, bass.ds(T.t + m * P, 1)], earlier[k][s][:, :], ones_b[:, 0:1],
                                  start=True, stop=True, skip_group_check=True).then_inc(q_in[k], 1)

                def body(i):
                    for u in range(U):
                        at(i, u, 0, U, NT, look)

                pipeline(pe, GR, 0, 0, body)

        c12.close()
        other_f = {"D": key_f["S"], "S": key_f["D"]}
        scol = {k: sb("scol" + k, [P, 3, NT], F32) for k in KEYS}
        with ExitStack() as c3:
            f = Env(nc, c3, "m_")
            pos_i = f.sb("posi", [P, NT], I32)
            row = {k: f.sb("row" + k, [P, NT], F32) for k in KEYS}
            lane = {k: f.sb("lane" + k, [P, NT], F32) for k in KEYS}
            OHlane = {k: f.ring("ohlane" + k, 2, [P, P], F32) for k in KEYS}
            cargo = {k: f.ring("cargo" + k, 2, [P, 3, NT], F32) for k in KEYS}
            pmove = {k: f.ps("pmove" + k, [P, 512]) for k in KEYS}
            m_v, m_made, m_moved, m_out = (f.sem(n) for n in ("m_v", "m_made", "m_moved", "m_out"))
            W = Weights(nc, f, g, [(0, io.L0_W1), (1, io.L0_W2)])
            block = c3.enter_context(f.block())
            GR = NT // 2

            @block.sync
            def _(sp):
                W.load(sp)

            @block.scalar
            def _(act):
                for m in range(2):
                    W.split_high(act, m)

            @block.gpsimd
            def _(pool):
                for m in range(2):
                    W.split_low(pool, m)

            @block.vector
            def _(dve):
                n = [0]

                def step(ins):
                    ins.then_inc(m_v, 1)
                    n[0] += 1
                    dve.wait_ge(m_v, n[0])

                for k in KEYS:
                    step(dve.tensor_copy(pos_i[:, :], pos[k][:, :]))
                    step(dve.tensor_scalar(tmp_i[:, :], pos_i[:, :], 7, None, ALU.logical_shift_right))
                    step(dve.tensor_copy(row[k][:, :], tmp_i[:, :]))
                    step(dve.tensor_scalar(tmp_i[:, :], pos_i[:, :], P - 1, None, ALU.bitwise_and))
                    step(dve.tensor_copy(lane[k][:, :], tmp_i[:, :]))

                def make(T):
                    s = T.slot(2)
                    wait(dve, m_moved, T.t - 1)
                    for k in KEYS:
                        one = bass.ds(T.t, 1)
                        dve.tensor_scalar(OHlane[k][s][:, :], iota_f[:, :], lane[k][:, one], None, ALU.is_equal)
                        for q, value in enumerate((key_f[k], other_f[k], deg[k])):
                            ins = dve.tensor_scalar(cargo[k][s][:, q, :], iota_f[:, 0:NT], row[k][:, one],
                                                    value[:, one], ALU.is_equal, ALU.mult)
                    ins.then_inc(m_made, 1)

                def body(i):
                    for u in range(2):
                        at(i, u, 0, 2, NT, make)

                pipeline(dve, GR, 0, 0, body)
                dve.wait_ge(m_moved, NT)
                for k in KEYS:
                    dve.tensor_copy(scol[k][:, :, :], pmove[k][:, 0:3 * NT]).then_inc(m_out, 1)

            @block.tensor
            def _(pe):
                def move(T):
                    s = T.slot(2)
                    pe.wait_ge(m_made, T.t + 1)
                    for k in KEYS:
                        ins = pe.matmul(pmove[k][:, 0:3 * NT], OHlane[k][s][:, :],
                                        cargo[k][s][:, :, :].rearrange("p a t -> p (a t)"),
                                        start=isinstance(T.t, int) and T.t == 0,
                                        stop=isinstance(T.t, int) and T.t == NT - 1)
                    ins.then_inc(m_moved, 1)

                def body(i):
                    for u in range(2):
                        at(i, u, 0, 2, NT, move)

                pipeline(pe, GR, 0, 0, body)

        rowT = {k: sb("rowT" + k, [NT, P + 1], F32) for k in KEYS}
        last = {k: sb("last" + k, [NT, P], F32) for k in KEYS}
        lastc = {k: sb("lastc" + k, [P, NT], F32) for k in KEYS}
        selrow = {k: sb("selrow" + k, [NT, SEL], I16) for k in KEYS}
        tmp_t = sb("tmpt", [NT, P], F32)
        tmp_c = sb("tmpc", [P, NT], F32)
        tmp_c2 = sb("tmpc2", [P, NT], F32)
        empty = sb("empty", [NT, P], F32)
        free = sb("free", [NT, P], F32)
        emptyc = sb("emptyc", [P, NT], F32)
        zrow = sb("zrow", [NT, P], F32)
        qrow = sb("qrow", [NT, P], F32)
        rank_c = {n: sb("rankc" + n, [P, NT], F32) for n in "zq"}
        rank_hi = {n: sb("rankhi" + n, [P, NT], F32) for n in "zq"}
        rank_lo = {n: sb("ranklo" + n, [P, NT], F32) for n in "zq"}
        qi = sb("qi", [NT, P], I32)
        qhi16 = sb("qhi16", [NT, P], I16)
        sentinel = sb("sentinel", [1, 1], F32)
        with ExitStack() as c4:
            f = Env(nc, c4, "o_")
            ptr = {k: f.ps("ptr" + k, [P, 512]) for k in KEYS}
            plast = {k: f.ps("plast" + k, [P, 512]) for k in KEYS}
            pflag, prank = f.ps("pflag", [P, 512]), f.ps("prank", [P, 512])
            psum = f.ps("psum", [P, 512])
            o_v, o_pe, o_st, o_ld, o_sel, o_bc, o_q = (f.sem(n) for n in ("o_v", "o_pe", "o_st", "o_ld", "o_sel", "o_bc", "o_q"))
            block = c4.enter_context(f.block())
            marks = {}

            @block.vector
            def _(dve):
                n = [0]

                def step(ins, mark=None):
                    ins.then_inc(o_v, 1)
                    n[0] += 1
                    if mark:
                        marks[mark] = n[0]
                    dve.wait_ge(o_v, n[0])

                step(dve.memset(sentinel[:, :], -1.0), "sentinel")
                for m, k in enumerate(KEYS):
                    dve.wait_ge(o_pe, m + 1)
                    step(dve.tensor_copy(rowT[k][:, 0:P], ptr[k][0:NT, 0:P]), "rowT" + k)
                for m, k in enumerate(KEYS):
                    dve.wait_ge(o_ld, 16 * (m + 1))
                    step(dve.tensor_tensor(last[k][:, :], rowT[k][:, 0:P], rowT[k][:, 1:P + 1], ALU.not_equal),
                         "last" + k)
                    step(dve.scalar_tensor_tensor(tmp_t[:, :], rowT[k][:, 0:P], 1.0, last[k][:, :],
                                                  ALU.add, ALU.mult))
                    step(dve.memset(selrow[k][:, P + 1:SEL], -1.0))
                    step(dve.tensor_copy(selrow[k][:, P:P + 1], rowT[k][:, P - 1:P]))
                    step(dve.tensor_scalar(selrow[k][:, 0:P], tmp_t[:, :], -1.0, None, ALU.add), "sel" + k)
                for m, k in enumerate(KEYS):
                    dve.wait_ge(o_pe, 3 + m)
                    step(dve.tensor_copy(lastc[k][:, :], plast[k][:, 0:NT]))
                    step(dve.tensor_copy(g.index[k][:, :, 0], scol[k][:, 1, :]))
                    step(dve.tensor_copy(g.index[k][:, :, 1], scol[k][:, 0, :]))
                    step(dve.tensor_scalar(tmp_c[:, :], lastc[k][:, :], float(-NOWHERE), float(NOWHERE),
                                           ALU.mult, ALU.add))
                    step(dve.tensor_tensor(tmp_c2[:, :], scol[k][:, 0, :], lastc[k][:, :], ALU.mult))
                    step(dve.tensor_tensor(g.index[k][:, :, 2], tmp_c[:, :], tmp_c2[:, :], ALU.add))
                    step(dve.tensor_copy(g.keycol[k][:, :], scol[k][:, 0, :]))
                step(dve.tensor_copy(g.degcol[:, :], scol["D"][:, 2, :]))
                step(dve.tensor_scalar(tmp_c[:, :], scol["S"][:, 2, :], 1.0, None, ALU.max))
                step(dve.reciprocal(g.rdeg[:, :], tmp_c[:, :]))
                for m, k in enumerate(KEYS):
                    dve.wait_ge(o_bc, 16 * (m + 1))
                    step(dve.tensor_copy(g.keylast[k][:, :], g.selrows[k][:, :, P]))
                    step(dve.memset(g.keyprev[k][:, 0:1], -2.0))
                    step(dve.tensor_copy(g.keyprev[k][:, 1:NT], g.keylast[k][:, 0:NT - 1]))
                step(dve.tensor_tensor(g.same_last[:, :], g.keylast["S"][:, :], g.keyprev["S"][:, :], ALU.is_equal))
                step(dve.tensor_tensor(tmp_c[:, :], g.keycol["S"][:, :], g.keyprev["S"][:, :], ALU.is_equal))
                step(dve.tensor_tensor(g.takes[:, :], tmp_c[:, :], lastc["S"][:, :], ALU.mult))
                step(dve.tensor_tensor(g.in_last[:, :], g.keycol["S"][:, :], g.keylast["S"][:, :], ALU.is_equal))
                step(dve.tensor_scalar(empty[:, :], count["S"][:, :], 0.0, None, ALU.is_equal), "empty")
                step(dve.tensor_scalar(free[:, :], last["S"][:, :], -1.0, 1.0, ALU.mult, ALU.add), "free")
                for m, (rows, out_row, name) in enumerate(((empty, zrow, "z"), (free, qrow, "q"))):
                    dve.wait_ge(o_pe, 5 + 3 * m)
                    step(dve.tensor_copy(colform[:, :], pflag[:, 0:NT]))
                    if name == "z":
                        step(dve.tensor_copy(emptyc[:, :], colform[:, :]))
                    step(dve.tensor_reduce(total[:, :], rows[:, :], AX.X, ALU.add))
                    step(dve.tensor_scalar(totals[:, :], ones_f[0:NT, :], total[:, 0:1], None, ALU.mult),
                         "totals" + name)
                    dve.wait_ge(o_pe, 6 + 3 * m)
                    step(dve.tensor_copy(out_row[:, :], psum[0:NT, 0:P]), "row" + name)
                    dve.wait_ge(o_pe, 7 + 3 * m)
                    step(dve.tensor_copy(rank_c[name][:, :], prank[:, 0:NT]), "col" + name)
                    step(dve.tensor_copy(tmp_i[:, :], rank_c[name][:, :]))
                    step(dve.tensor_scalar(node_i[:, :], tmp_i[:, :], 7, None, ALU.logical_shift_right))
                    step(dve.tensor_copy(rank_hi[name][:, :], node_i[:, :]))
                    step(dve.tensor_scalar(node_i[:, :], tmp_i[:, :], P - 1, None, ALU.bitwise_and))
                    step(dve.tensor_copy(rank_lo[name][:, :], node_i[:, :]))
                step(dve.tensor_scalar(tmp_c[:, :], emptyc[:, :], 200.0, -200.0, ALU.mult, ALU.add))
                step(dve.tensor_tensor(rank_hi["z"][:, :], rank_hi["z"][:, :], tmp_c[:, :], ALU.add))
                step(dve.tensor_copy(qi[:, :], qrow[:, :]))
                step(dve.tensor_scalar(qi[:, :], qi[:, :], 7, None, ALU.logical_shift_right))
                step(dve.tensor_copy(qhi16[:, :], qi[:, :]), "qhi16")

            @block.tensor
            def _(pe):
                for k in KEYS:
                    pe.transpose(ptr[k][0:NT, 0:P], scol[k][:, 0, :], g.ident[:, :]).then_inc(o_pe, 1)
                for m, k in enumerate(KEYS):
                    pe.wait_ge(o_v, marks["last" + k])
                    pe.transpose(plast[k][:, 0:NT], last[k][:, :], g.ident[0:NT, 0:NT]).then_inc(o_pe, 1)
                for rows, out_row, name, mark in ((empty, zrow, "z", "empty"), (free, qrow, "q", "colz")):
                    pe.wait_ge(o_v, marks["free"])
                    pe.wait_ge(o_v, marks[mark])
                    pe.transpose(pflag[:, 0:NT], rows[:, :], g.ident[0:NT, 0:NT]).then_inc(o_pe, 1)
                    pe.wait_ge(o_v, marks["totals" + name])
                    pe.matmul(psum[0:NT, 0:P], colform[:, :], before_f[:, :], start=True, stop=False)
                    pe.matmul(psum[0:NT, 0:P], before_f[0:NT, 0:NT], totals[:, :], start=False, stop=True)\
                        .then_inc(o_pe, 1)
                    pe.wait_ge(o_v, marks["row" + name])
                    pe.transpose(prank[:, 0:NT], out_row[:, :], g.ident[0:NT, 0:NT]).then_inc(o_pe, 1)

            @block.sync
            def _(sp):
                sp.wait_ge(o_v, marks["sentinel"])
                for k in KEYS:
                    sp.wait_ge(o_v, marks["rowT" + k])
                    sp.dma_start(g.seq[k][0:N].rearrange("(t j) -> t j", j=P), rowT[k][:, 0:P]).then_inc(o_st, 16)
                    sp.dma_start(row_of(g.seq[k][N:N + 1]), sentinel[:, :]).then_inc(o_st, 16)
                sp.wait_ge(o_st, 64)
                for k in KEYS:
                    sp.dma_start(rowT[k][:, P:P + 1], g.seq[k][1:N + 1].rearrange("(t j) -> t j", j=P)[:, P - 1:P],
                                 allow_slow_non_contiguous=True).then_inc(o_ld, 16)
                    sp.wait_ge(o_ld, 16 if k == "D" else 32)
                for m, k in enumerate(KEYS):
                    sp.wait_ge(o_v, marks["sel" + k])
                    sp.dma_start(g.seldram[k], selrow[k][:, :]).then_inc(o_sel, 16)
                    sp.wait_ge(o_sel, 16 * (m + 1))
                    sp.dma_start(g.selrows[k][:, :, :], g.seldram[k].partition_broadcast(P)).then_inc(o_bc, 16)
                    sp.wait_ge(o_bc, 16 * (m + 1))
                sp.dma_start(g.lastdram, last["S"][:, :]).then_inc(o_q, 16)
                sp.wait_ge(o_v, marks["qhi16"])
                sp.dma_start(g.qdram, qhi16[:, :]).then_inc(o_q, 16)
                sp.wait_ge(o_q, 32)

        with ExitStack() as c5:
            f = Env(nc, c5, "e_")
            qrow16 = f.sb("qrow16", [NT, N], I16)
            hot_hi = f.ring("hothi", 2, [P, NT], F32)
            hot_lo = f.ring("hotlo", 2, [P, P], F32)
            listed = f.sb("listed", [NT, P], F32)
            hotT = f.ring("hott", 2, [NT, P], F32)
            hotq = f.ring("hotq", 2, [P, P], F32)
            picked = f.ring("picked", 2, [P, P], F32)
            found = f.sb("found", [P, NT], F32)
            plist = f.ps("plist", [P, 512])
            pl = [f.ps(f"pl{i}", [P, 512]) for i in range(2)]
            e_ld, e_made, e_put, e_list, e_hot, e_look, e_pick, e_red, e_fin = (
                f.sem(n) for n in ("e_ld", "e_made", "e_put", "e_list", "e_hot", "e_look", "e_pick", "e_red", "e_fin"))
            block = c5.enter_context(f.block())
            GR = NT // 2

            @block.sync
            def _(sp):
                sp.dma_start(qrow16[:, :], g.qdram.rearrange("t j -> (t j)").partition_broadcast(NT)).then_inc(e_ld, 16)
                sp.wait_ge(e_ld, 16)

            @block.vector
            def _(dve):
                def make(T):
                    s = T.slot(2)
                    one = bass.ds(T.t, 1)
                    wait(dve, e_put, T.t - 1)
                    dve.tensor_scalar(hot_hi[s][:, :], iota_f[:, 0:NT], rank_hi["z"][:, one], None, ALU.is_equal)
                    dve.tensor_scalar(hot_lo[s][:, :], iota_f[:, :], rank_lo["z"][:, one], node_f[:, one],
                                      ALU.is_equal, ALU.mult).then_inc(e_made, 1)

                def body(i):
                    for u in range(2):
                        at(i, u, 0, 2, NT, make)

                pipeline(dve, GR, 0, 0, body)
                dve.wait_ge(e_put, NT)
                dve.tensor_copy(listed[:, :], plist[0:NT, 0:P]).then_inc(e_list, 1)
                dve.wait_ge(e_ld, 16)

                def hot(T):
                    s = T.slot(2)
                    wait(dve, e_look, T.t - 1)
                    dve.tensor_scalar(hotT[s][:, :], qrow16[:, bass.ds(T.t * P, P)], pidx[0:NT, 0:1], None,
                                      ALU.is_equal).then_inc(e_hot, 1)
                    wait(dve, e_pick, T.t - 1)
                    dve.tensor_scalar(hotq[s][:, :], iota_f[:, :], rank_lo["q"][:, bass.ds(T.t, 1)], None,
                                      ALU.is_equal).then_inc(e_hot, 1)

                def pick(T):
                    s = T.slot(2)
                    dve.wait_ge(e_look, T.t + 1)
                    dve.wait_ge(e_hot, 2 * T.t + 2)
                    wait(dve, e_red, T.t - 1)
                    dve.tensor_tensor(picked[s][:, :], pl[s][:, 0:P], hotq[s][:, :], ALU.mult).then_inc(e_pick, 1)
                    dve.wait_ge(e_pick, T.t + 1)
                    dve.tensor_reduce(found[:, bass.ds(T.t, 1)], picked[s][:, :], AX.X, ALU.add).then_inc(e_red, 1)

                def body2(i):
                    for u in range(2):
                        at(i, u, 1, 2, NT, hot)
                        at(i, u, 0, 2, NT, pick)

                pipeline(dve, GR, 1, 0, body2)
                dve.wait_ge(e_red, NT)
                n = [0]

                def step(ins):
                    ins.then_inc(e_fin, 1)
                    n[0] += 1
                    dve.wait_ge(e_fin, n[0])

                step(dve.tensor_tensor(tmp_c[:, :], scol["S"][:, 0, :], found[:, :], ALU.subtract))
                step(dve.tensor_tensor(tmp_c[:, :], tmp_c[:, :], lastc["S"][:, :], ALU.mult))
                step(dve.tensor_tensor(g.index["S"][:, :, 2], tmp_c[:, :], found[:, :], ALU.add))

            @block.tensor
            def _(pe):
                def put(T):
                    s = T.slot(2)
                    pe.wait_ge(e_made, T.t + 1)
                    pe.matmul(plist[0:NT, 0:P], hot_hi[s][:, :], hot_lo[s][:, :],
                              start=isinstance(T.t, int) and T.t == 0,
                              stop=isinstance(T.t, int) and T.t == NT - 1).then_inc(e_put, 1)

                def look(T):
                    s = T.slot(2)
                    pe.wait_ge(e_hot, 2 * T.t + 1)
                    wait(pe, e_pick, T.t - 1)
                    pe.matmul(pl[s][:, 0:P], hotT[s][:, :], listed[:, :], start=True, stop=True).then_inc(e_look, 1)

                def body(i):
                    for u in range(2):
                        at(i, u, 0, 2, NT, put)

                def body2(i):
                    for u in range(2):
                        at(i, u, 0, 2, NT, look)

                pipeline(pe, GR, 0, 0, body)
                pe.wait_ge(e_list, 1)
                pipeline(pe, GR, 0, 0, body2)



class Weights:

    def __init__(self, nc, e, g, sources):
        self.nc, self.g, self.sources = nc, g, sources
        self.stage = e.sb("wstage", [P, C, D], F32)
        self.loaded, self.high, self.low = e.sem("w_loaded"), e.sem("w_high"), e.sem("w_low")

    def load(self, sp):
        for n in range(len(self.sources)):
            self.load_one(sp, n)

    def load_one(self, sp, n):
        wait(sp, self.low, n)
        sp.dma_start(self.stage[:, :, :], self.sources[n][1].rearrange("(c p) n -> p c n", p=P))\
            .then_inc(self.loaded, 16)

    def split_high(self, act, n):
        slot = self.sources[n][0]
        act.wait_ge(self.loaded, 16 * (n + 1))
        self.nc.scalar.copy(self.g.Whi[slot][:, :, :], self.stage[:, :, :]).then_inc(self.high, 1)

    def split_low(self, pool, n):
        slot = self.sources[n][0]
        pool.wait_ge(self.high, n + 1)
        pool.tensor_tensor(self.g.Wlo[slot][:, :, :], self.stage[:, :, :],
                           self.g.Whi[slot][:, :, :].bitcast(F32), ALU.subtract).then_inc(self.low, 1)


def selection(dve, g, k, T, sel, mask, sel_sem, mask_sem, sel_free, mask_done):
    s = T.slot(2)
    rows = g.selrows[k][:, bass.ds(T.t, 1), :]
    wait(dve, sel_free, T.t - 1)
    dve.tensor_scalar(sel[s][:, :], rows, g.keycol[k][:, bass.ds(T.t, 1)], None, ALU.is_equal).then_inc(sel_sem, 1)
    if mask is not None:
        wait(dve, mask_done, T.t - 1)
        dve.tensor_scalar(mask[s][:, :], rows, g.keyprev[k][:, bass.ds(T.t, 1)], None, ALU.is_equal)\
            .then_inc(mask_sem, 1)


def chunk(psum, c, cols):
    return psum[:, c // 2, (c % 2) * SEL:(c % 2) * SEL + cols]


def all_chunks(psum, first, cols):
    return psum[:, :, 0:2 * SEL].rearrange("p b (h w) -> p b h w", w=SEL)[:, :, :, first:first + cols]


def chunks_of(t):
    return t.rearrange("p (b h) n -> p b h n", b=2)


def carry_in(dve, T, psum, mask, carry, summed, mask_sem, done, copied):
    s, before = T.slot(2), (T.j - 1) % 2
    dve.wait_ge(summed, T.t + 1)
    dve.wait_ge(mask_sem, T.t + 1)
    wait(dve, copied, T.t)
    for c in range(C):
        ins = dve.scalar_tensor_tensor(chunk(psum[s], c, SEL), mask[s][:, :], carry[before][:, c:c + 1],
                                       chunk(psum[s], c, SEL), ALU.mult, ALU.add)
    ins.then_inc(done, 1)
    dve.wait_ge(done, T.t + 1)
    dve.tensor_copy(carry[s][:, :], all_chunks(psum[s], P, 1)).then_inc(copied, 1)


def product(pe, out, hi, lo, whi, wlo, start, stop):
    for c in range(C):
        ins = pe.matmul(out, hi[:, c, :], whi[:, c, :], start=start and c == 0, stop=False)
        ins = pe.matmul(out, hi[:, c, :], wlo[:, c, :], start=False, stop=False)
        ins = pe.matmul(out, lo[:, c, :], whi[:, c, :], start=False, stop=stop and c == C - 1)
    return ins


def indices(pool, g, k, T, col, n, tick, copied):
    s = T.slot(2)
    pool.sem_inc(tick, 1)
    pool.tensor_copy(col[s][:, 0:n], g.index[k][:, bass.ds(T.t, 1), 0:n]).then_inc(copied, 1)


def fetch(pool, out, table, index):
    return pool.indirect_dma_start(out, None, table, bass.IndirectOffsetOnAxis(ap=index, axis=0))


def put_rows(pool, table, index, rows, last_row):
    return pool.indirect_dma_start(table, bass.IndirectOffsetOnAxis(ap=index, axis=0), rows, None,
                                   bounds_check=last_row, oob_is_err=False)


class Norm:

    def __init__(self, e, name):
        self.stats = e.ring(name + "stats", 2, [P, 6], F32)
        self.mean_var = e.ring(name + "mv", 2, [P, 2], F32)
        self.var = e.ring(name + "var", 2, [P, 1], F32)
        self.s_stats, self.s_mean, self.s_var, self.s_scale, self.s_bias = (
            e.sem(name + n) for n in ("_stats", "_mean", "_var", "_scale", "_bias"))

    def statistics(self, dve, tick, T, rows, used):
        s = T.slot(2)
        dve.bn_stats(self.stats[s][:, :], rows).then_inc(self.s_stats, 1)
        wait(dve, used, T.t - 1)
        dve.wait_ge(self.s_stats, T.t + 1)
        dve.sem_inc(tick, 1)
        dve.bn_aggr(self.mean_var[s][:, :], self.stats[s][:, :]).then_inc(self.s_mean, 1)

    def finish(self, pool, tick, T, neg_half, scale, bias=None):
        s = T.slot(2)
        pool.wait_ge(self.s_mean, T.t + 1)
        pool.sem_inc(tick, 1)
        pool.tensor_scalar(self.var[s][:, :], self.mean_var[s][:, 1:2], 1.0, LN_EPS, ALU.mult, ALU.add)\
            .then_inc(self.s_var, 1)
        pool.wait_ge(self.s_var, T.t + 1)
        pool.tensor_tensor(scale, self.var[s][:, :], neg_half[:, :], ALU.pow).then_inc(self.s_scale, 1)
        if bias is not None:
            pool.wait_ge(self.s_scale, T.t + 1)
            pool.sem_inc(tick, 1)
            pool.tensor_scalar(bias, self.mean_var[s][:, 0:1], scale, -1.0, ALU.mult, ALU.mult)\
                .then_inc(self.s_bias, 1)



def layer0(nc, io, g, second):
    NT, N = g.NT, g.N
    GR = NT // 2
    with ExitStack() as ctx:
        e = Env(nc, ctx, "b_" if second else "a_")
        src, slot, bias = (g.h1, 1, io.L0_b2) if second else (g.h0, 0, io.L0_b1)
        brow = e.sb("brow", [P, D], F32)
        neg_half = e.sb("neghalf", [P, 1], F32)
        col = e.ring("col", 2, [P, 3], I32)
        colx = e.ring("colx", 2, [P, 3], I32)
        G = e.ring("G", 2, [P, D], F32)
        Ghi, Glo = e.ring("Ghi", 2, [P, D], F32R), e.ring("Glo", 2, [P, D], F32R)
        sel, mask = e.ring("sel", 2, [P, SEL], F32R), e.ring("mask", 2, [P, SEL], F32)
        carry = e.ring("carry", 2, [P, C], F32)
        Thi, Tlo = e.ring("Thi", 2, [P, C, P], F32R), e.ring("Tlo", 2, [P, C, P], F32R)
        rows = e.ring("rows", 2, [P, EXT if second else D], F32)
        xr = e.ring("xr", 2, [P, D], F32) if second else None
        ln = Norm(e, "ln") if second else None
        W = None if second else Weights(nc, e, g, [(2, io.L1_W1), (3, io.L1_W2)])
        psum_t = [e.ps(f"pt{i}", [P, 2, 512]) for i in range(2)]
        psum_o = [e.ps(f"po{i}", [P, D]) for i in range(2)]

        s_brow, s_const = e.sem("s_brow"), e.sem("s_const")
        s_col, s_colx = e.sem("s_col"), e.sem("s_colx")
        s_G, s_x, s_put = e.sems("s_G", 2), e.sems("s_x", 2), e.sems("s_put", 2)
        s_Ghi, s_Glo = e.sem("s_Ghi"), e.sem("s_Glo")
        s_sel, s_mask = e.sem("s_sel"), e.sem("s_mask")
        s_summed, s_carried, s_copied = e.sem("s_summed"), e.sem("s_carried"), e.sem("s_copied")
        s_Thi, s_Tlo = e.sem("s_Thi"), e.sem("s_Tlo")
        s_prod, s_biased, s_rows = e.sem("s_prod"), e.sem("s_biased"), e.sem("s_rows")
        tick = e.sem("tick")
        block = ctx.enter_context(e.block())

        @block.sync
        def _(sp):
            sp.dma_start(brow[:, :], bias.partition_broadcast(P)).then_inc(s_brow, 16)
            if W:
                W.load(sp)
            sp.wait_ge(s_brow, 16)

        @block.gpsimd
        def _(pool):
            def start_fetch(T):
                s = T.slot(2)
                wait(pool, s_Glo, T.t - 1)
                indices(pool, g, "D", T, col, 1, tick, s_col)
                pool.wait_ge(s_col, T.t + 1)
                pool.sem_inc(tick, 1)
                fetch(pool, G[s][:, :], src, col[s][:, 0:1]).then_inc(s_G[s], 16)

            def low(T):
                s = T.slot(2)
                wait(pool, s_summed, T.t - 1)
                pool.wait_ge(s_Ghi, T.t + 1)
                pool.tensor_tensor(Glo[s][:, :], G[s][:, :], Ghi[s][:, :].bitcast(F32), ALU.subtract)\
                    .then_inc(s_Glo, 1)

            def residual(T):
                s = T.slot(2)
                wait(pool, s_rows, T.t - 1)
                wait(pool, s_put[s], 16 * T.use(2))
                indices(pool, g, "D", T, colx, 3, tick, s_colx)
                if second:
                    pool.wait_ge(s_colx, T.t + 1)
                    pool.sem_inc(tick, 1)
                    fetch(pool, xr[s][:, :], io.x, colx[s][:, 1:2]).then_inc(s_x[s], 16)

            def store(T):
                s = T.slot(2)
                pool.wait_ge(s_colx, T.t + 1)
                if second:
                    ln.finish(pool, tick, T, neg_half, rows[s][:, SCALE:SCALE + 1], rows[s][:, BIAS:BIAS + 1])
                    pool.wait_ge(ln.s_bias, T.t + 1)
                else:
                    pool.wait_ge(s_rows, T.t + 1)
                pool.sem_inc(tick, 1)
                put_rows(pool, g.xs[0] if second else g.h1, colx[s][:, 2:3], rows[s][:, :], N - 1)\
                    .then_inc(s_put[s], 16)

            def body(i):
                for u in range(2):
                    at(i, u, 0, 2, NT, residual)
                    at(i, u, -1, 2, NT, store)
                    at(i, u, 2, 2, NT, low)
                    at(i, u, 4, 2, NT, start_fetch)

            pool.memset(neg_half[:, :], -0.5).then_inc(s_const, 1)
            for s in range(2):
                pool.memset(carry[s][:, :], 0.0).then_inc(s_const, 1)
                if second:
                    pool.memset(rows[s][:, BIAS + 1:EXT], 0.0).then_inc(s_const, 1)
            pool.wait_ge(s_const, 5 if second else 3)
            pipeline(pool, GR, 2, 1, body, between=W and (lambda n: W.split_low(pool, n)))
            for s in range(2):
                pool.wait_ge(s_put[s], 16 * GR)

        @block.scalar
        def _(act):
            def high(T):
                s = T.slot(2)
                act.wait_ge(s_G[s], 16 * (T.use(2) + 1))
                wait(act, s_summed, T.t - 1)
                nc.scalar.copy(Ghi[s][:, :], G[s][:, :]).then_inc(s_Ghi, 1)

            def high_sum(T):
                s = T.slot(2)
                act.wait_ge(s_copied, T.t + 1)
                wait(act, s_prod, T.t - 1)
                nc.scalar.copy(chunks_of(Thi[s]), all_chunks(psum_t[s], 0, P)).then_inc(s_Thi, 1)

            def relu(T):
                s = T.slot(2)
                act.wait_ge(s_biased, T.t + 1)
                wait(act, s_put[s], 16 * T.use(2))
                nc.scalar.activation(rows[s][:, :], psum_o[s][:, :], ACT.Relu).then_inc(s_rows, 1)

            def body(i):
                for u in range(2):
                    at(i, u, 2, 2, NT, high)
                    at(i, u, 1, 2, NT, high_sum)
                    if not second:
                        at(i, u, 0, 2, NT, relu)

            pipeline(act, GR, 1, 0, body, between=W and (lambda n: W.split_high(act, n)))

        @block.vector
        def _(dve):
            def select(T):
                selection(dve, g, "D", T, sel, mask, s_sel, s_mask, s_summed, s_carried)

            def carried(T):
                carry_in(dve, T, psum_t, mask, carry, s_summed, s_mask, s_carried, s_copied)

            def low_sum(T):
                s = T.slot(2)
                dve.wait_ge(s_Thi, T.t + 1)
                dve.tensor_tensor(chunks_of(Tlo[s]), all_chunks(psum_t[s], 0, P), chunks_of(Thi[s]).bitcast(F32),
                                  ALU.subtract).then_inc(s_Tlo, 1)

            def add_bias(T):
                s = T.slot(2)
                dve.wait_ge(s_prod, T.t + 1)
                dve.scalar_tensor_tensor(psum_o[s][:, :], brow[:, :], g.degcol[:, bass.ds(T.t, 1)], psum_o[s][:, :],
                                         ALU.mult, ALU.add).then_inc(s_biased, 1)

            def add_x(T):
                s = T.slot(2)
                dve.wait_ge(s_biased, T.t + 1)
                dve.wait_ge(s_x[s], 16 * (T.use(2) + 1))
                wait(dve, s_put[s], 16 * T.use(2))
                dve.scalar_tensor_tensor(rows[s][:, 0:D], psum_o[s][:, :], 0.0, xr[s][:, :], ALU.max, ALU.add)\
                    .then_inc(s_rows, 1)
                dve.wait_ge(s_rows, T.t + 1)
                ln.statistics(dve, tick, T, rows[s][:, 0:D], ln.s_bias)

            def body(i):
                for u in range(2):
                    at(i, u, 1, 2, NT, carried)
                    at(i, u, 1, 2, NT, low_sum)
                    at(i, u, 2, 2, NT, select)
                    at(i, u, 0, 2, NT, add_bias)
                    if second:
                        at(i, u, 0, 2, NT, add_x)

            dve.wait_ge(s_brow, 16)
            dve.wait_ge(s_const, 5 if second else 3)
            pipeline(dve, GR, 1, 0, body)

        @block.tensor
        def _(pe):
            def sum_edges(T):
                s = T.slot(2)
                pe.wait_ge(s_sel, T.t + 1)
                pe.wait_ge(s_Glo, T.t + 1)
                wait(pe, s_Tlo, T.t - 1)
                for c in range(C):
                    pe.matmul(chunk(psum_t[s], c, SEL), Ghi[s][:, c * P:(c + 1) * P], sel[s][:, :],
                              start=True, stop=False)
                    ins = pe.matmul(chunk(psum_t[s], c, SEL), Glo[s][:, c * P:(c + 1) * P], sel[s][:, :],
                                    start=False, stop=True)
                ins.then_inc(s_summed, 1)

            def multiply(T):
                s = T.slot(2)
                pe.wait_ge(s_Tlo, T.t + 1)
                wait(pe, s_rows, T.t - 1)
                product(pe, psum_o[s][:, :], Thi[s], Tlo[s], g.Whi[slot], g.Wlo[slot], True, True)\
                    .then_inc(s_prod, 1)

            def body(i):
                for u in range(2):
                    at(i, u, 1, 2, NT, sum_edges)
                    at(i, u, 0, 2, NT, multiply)

            pipeline(pe, GR, 1, 0, body)



def layer1(nc, io, g):
    NT, N = g.NT, g.N
    GR = NT // 2
    RX = 8
    with ExitStack() as ctx:
        e = Env(nc, ctx, "c_")
        src, out = g.xs[0], g.xs[1]
        W = Weights(nc, e, g, [(0, io.L2_Wn), (1, io.L2_Ws)])
        gamma, beta = e.sb("gamma", [P, D], F32), e.sb("beta", [P, D], F32)
        b1col = e.sb("b1col", [P, C], F32)
        b2f, b2hi, b2lo = e.sb("b2f", [1, D], F32), e.sb("b2hi", [1, D], F32R), e.sb("b2lo", [1, D], F32R)
        ones1 = e.sb("ones1", [1, P], F32R)
        ones_f = e.sb("onesf", [1, P], F32)
        eps1 = e.sb("eps1", [P, 1], F32)
        eye = e.sb("eye", [P, P], F32)
        neg_half = e.sb("neghalf", [P, 1], F32)
        col, colx = e.ring("col", 2, [P, 3], I32), e.ring("colx", 2, [P, 3], I32)
        G, X = e.ring("G", 2, [P, EXT], F32), e.ring("X", 2, [P, EXT], F32)
        H = e.ring("H", 2, [P, D], F32)
        XB = e.sb("XB", [P, RX, D], F32)
        Ghi, Glo = e.ring("Ghi", 2, [P, D], F32R), e.ring("Glo", 2, [P, D], F32R)
        sel, mask = e.ring("sel", 2, [P, SEL], F32R), e.ring("mask", 2, [P, SEL], F32)
        carry = e.ring("carry", 2, [P, C], F32)
        Zhi, Zlo = e.sb("Zhi", [P, C, 2 * P], F32R), e.sb("Zlo", [P, C, 2 * P], F32R)
        Uhi, Ulo = e.ring("Uhi", 2, [P, C, 2 * P], F32R), e.ring("Ulo", 2, [P, C, 2 * P], F32R)
        rows = e.ring("rows", 2, [P, EXT], F32)
        ylen = e.ring("ylen", 2, [P, 1], F32)
        ln_y, ln_x = Norm(e, "lny"), Norm(e, "lnx")
        psum_t = [e.ps(f"pt{i}", [P, 2, 512]) for i in range(2)]
        psum_u = e.ps("pu", [P, C, 2 * P])
        psum_o = [e.ps(f"po{i}", [P, D]) for i in range(2)]

        s_load, s_const, s_prep = e.sem("s_load"), e.sem("s_const"), e.sem("s_prep")
        s_col, s_colx = e.sem("s_col"), e.sem("s_colx")
        s_G, s_X, s_put = e.sems("s_G", 2), e.sems("s_X", 2), e.sems("s_put", 2)
        s_Gn, s_H, s_Ghi, s_Glo, s_XB = (e.sem(n) for n in ("s_Gn", "s_H", "s_Ghi", "s_Glo", "s_XB"))
        s_sel, s_mask = e.sem("s_sel"), e.sem("s_mask")
        s_summed, s_carried, s_copied = e.sem("s_summed"), e.sem("s_carried"), e.sem("s_copied")
        s_Zhi, s_Zlo = e.sem("s_Zhi"), e.sem("s_Zlo")
        s_u, s_relu, s_Uhi, s_Ulo = (e.sem(n) for n in ("s_u", "s_relu", "s_Uhi", "s_Ulo"))
        s_prod, s_cent, s_rows = e.sem("s_prod"), e.sem("s_cent"), e.sem("s_rows")
        tick = e.sem("tick")
        block = ctx.enter_context(e.block())

        @block.sync
        def _(sp):
            sp.dma_start(gamma[:, :], io.L1_gamma.partition_broadcast(P)).then_inc(s_load, 16)
            sp.dma_start(beta[:, :], io.L1_beta.partition_broadcast(P)).then_inc(s_load, 16)
            sp.dma_start(b1col[:, :], io.L1_b1col).then_inc(s_load, 16)
            sp.dma_start(b2f[:, :], row_of(io.L1_b2)).then_inc(s_load, 16)
            sp.dma_start(eps1[:, :], io.eps.partition_broadcast(P)).then_inc(s_load, 16)
            W.load(sp)
            sp.wait_ge(s_load, 80)

        @block.gpsimd
        def _(pool):
            def start_fetch(T):
                s = T.slot(2)
                wait(pool, s_Glo, T.t - 1)
                wait(pool, s_H, T.t - 1)
                wait(pool, s_XB, T.t - 1)
                wait(pool, s_X[s], 16 * T.use(2))
                indices(pool, g, "S", T, col, 3, tick, s_col)
                pool.wait_ge(s_col, T.t + 1)
                pool.sem_inc(tick, 1)
                fetch(pool, G[s][:, :], src, col[s][:, 0:1]).then_inc(s_G[s], 16)
                fetch(pool, X[s][:, :], src, col[s][:, 2:3]).then_inc(s_X[s], 16)

            def keep_x(T):
                s = T.slot(2)
                pool.wait_ge(s_X[s], 16 * (T.use(2) + 1))
                wait(pool, s_rows, T.t - RX + 1)
                pool.sem_inc(tick, 1)
                pool.tensor_tensor(XB[:, bass.ds(T.t % RX, 1), :], X[s][:, 0:D], beta[:, :], ALU.add)\
                    .then_inc(s_XB, 1)

            def low(T):
                s = T.slot(2)
                wait(pool, s_summed, T.t - 1)
                pool.wait_ge(s_Ghi, T.t + 1)
                pool.tensor_tensor(Glo[s][:, :], G[s][:, 0:D], Ghi[s][:, :].bitcast(F32), ALU.subtract)\
                    .then_inc(s_Glo, 1)

            def norm_y(T):
                wait(pool, s_rows, T.t - 1)
                ln_y.finish(pool, tick, T, neg_half, ylen[T.slot(2)][:, :])

            def store(T):
                s = T.slot(2)
                wait(pool, s_put[s], 16 * T.use(2))
                indices(pool, g, "S", T, colx, 3, tick, s_colx)
                ln_x.finish(pool, tick, T, neg_half, rows[s][:, SCALE:SCALE + 1], rows[s][:, BIAS:BIAS + 1])
                pool.wait_ge(s_colx, T.t + 1)
                pool.wait_ge(ln_x.s_bias, T.t + 1)
                pool.sem_inc(tick, 1)
                put_rows(pool, out, colx[s][:, 2:3], rows[s][:, :], N - 1).then_inc(s_put[s], 16)

            def body(i):
                for u in range(2):
                    at(i, u, 6, 2, NT, keep_x)
                    at(i, u, 6, 2, NT, low)
                    at(i, u, 8, 2, NT, start_fetch)
                for u in range(2):
                    at(i, u, 0, 2, NT, norm_y)
                for u in range(2):
                    at(i, u, 0, 2, NT, store)

            pool.memset(neg_half[:, :], -0.5).then_inc(s_const, 1)
            pool.memset(ones_f[:, :], 1.0).then_inc(s_const, 1)
            for s in range(2):
                pool.memset(carry[s][:, :], 0.0).then_inc(s_const, 1)
                pool.memset(rows[s][:, BIAS + 1:EXT], 0.0).then_inc(s_const, 1)
            pool.wait_ge(s_const, 6)
            pool.wait_ge(s_load, 80)
            pipeline(pool, GR, 4, 0, body, ahead=4, between=lambda n: W.split_low(pool, n))
            for s in range(2):
                pool.wait_ge(s_put[s], 16 * GR)

        @block.scalar
        def _(act):
            def norm_in(T):
                s = T.slot(2)
                act.wait_ge(s_G[s], 16 * (T.use(2) + 1))
                nc.scalar.activation(G[s][:, 0:D], G[s][:, 0:D], ACT.Relu, bias=G[s][:, BIAS:BIAS + 1],
                                     scale=G[s][:, SCALE:SCALE + 1]).then_inc(s_Gn, 1)
                act.wait_ge(s_X[s], 16 * (T.use(2) + 1))
                wait(act, s_summed, T.t - 1)
                nc.scalar.activation(H[s][:, :], X[s][:, 0:D], ACT.Relu, bias=X[s][:, BIAS:BIAS + 1],
                                     scale=X[s][:, SCALE:SCALE + 1]).then_inc(s_H, 1)
                act.wait_ge(s_Gn, T.t + 1)
                nc.scalar.copy(Ghi[s][:, :], G[s][:, 0:D]).then_inc(s_Ghi, 1)

            def high_sum(T):
                s = T.slot(2)
                act.wait_ge(s_copied, T.t + 1)
                wait(act, s_u, T.k)
                nc.scalar.copy(chunks_of(Zhi[:, :, s * P:(s + 1) * P]), all_chunks(psum_t[s], 0, P))\
                    .then_inc(s_Zhi, 1)

            def relu(T):
                act.wait_ge(s_u, T.t + 1)
                for c in range(C):
                    ins = nc.scalar.activation(psum_u[:, c, :], psum_u[:, c, :], ACT.Relu, bias=b1col[:, c:c + 1])
                ins.then_inc(s_relu, 1)
                act.wait_ge(s_relu, T.t + 1)
                wait(act, s_prod, 2 * (T.t - 1))
                nc.scalar.copy(Uhi[T.slot(2)][:, :, :], psum_u[:, :, :]).then_inc(s_Uhi, 1)

            def body(i, odd):
                at(i, 0, 1, 1, GR, lambda T: relu(Pair(T.t, (odd + 1) % 2)))
                for u in range(2):
                    at(i, u, 4, 2, NT, high_sum)
                    at(i, u, 6, 2, NT, norm_in)

            act.wait_ge(s_load, 80)
            nc.scalar.copy(b2hi[:, :], b2f[:, :]).then_inc(s_prep, 1)
            act.wait_ge(s_const, 2)
            nc.scalar.copy(ones1[:, :], ones_f[:, :]).then_inc(s_prep, 1)
            pairs(act, GR, 3, 0, body, between=lambda n: W.split_high(act, n))

        @block.vector
        def _(dve):
            def low_u(T):
                dve.wait_ge(s_Uhi, T.t + 1)
                dve.tensor_tensor(Ulo[T.slot(2)][:, :, :], psum_u[:, :, :], Uhi[T.slot(2)][:, :, :].bitcast(F32),
                                  ALU.subtract).then_inc(s_Ulo, 1)

            def carried(T):
                carry_in(dve, T, psum_t, mask, carry, s_summed, s_mask, s_carried, s_copied)

            def low_sum(T):
                s = T.slot(2)
                dve.wait_ge(s_Zhi, T.t + 1)
                half = slice(s * P, (s + 1) * P)
                dve.tensor_tensor(chunks_of(Zlo[:, :, half]), all_chunks(psum_t[s], 0, P),
                                  chunks_of(Zhi[:, :, half]).bitcast(F32), ALU.subtract).then_inc(s_Zlo, 1)

            def select(T):
                selection(dve, g, "S", T, sel, mask, s_sel, s_mask, s_summed, s_carried)

            def center(T):
                s = T.slot(2)
                dve.wait_ge(s_prod, T.t + 1)
                ln_y.statistics(dve, tick, T, psum_o[s][:, :], ln_y.s_scale)
                dve.wait_ge(ln_y.s_mean, T.t + 1)
                dve.scalar_tensor_tensor(psum_o[s][:, :], psum_o[s][:, :], ln_y.mean_var[s][:, 0:1], gamma[:, :],
                                         ALU.subtract, ALU.mult).then_inc(s_cent, 1)

            def new_rows(T):
                s = T.slot(2)
                dve.wait_ge(s_cent, T.t + 1)
                dve.wait_ge(ln_y.s_scale, T.t + 1)
                dve.wait_ge(s_XB, T.t + 1)
                wait(dve, s_put[s], 16 * T.use(2))
                dve.scalar_tensor_tensor(rows[s][:, 0:D], psum_o[s][:, :], ylen[s][:, 0:1],
                                         XB[:, bass.ds(T.t % RX, 1), :], ALU.mult, ALU.add).then_inc(s_rows, 1)
                dve.wait_ge(s_rows, T.t + 1)
                ln_x.statistics(dve, tick, T, rows[s][:, 0:D], ln_x.s_bias)

            def body(i, odd):
                at(i, 0, 1, 1, GR, lambda T: low_u(Pair(T.t, (odd + 1) % 2)))
                for u in range(2):
                    at(i, u, 4, 2, NT, carried)
                    at(i, u, 4, 2, NT, low_sum)
                    at(i, u, 6, 2, NT, select)
                for u in range(2):
                    at(i, u, 0, 2, NT, center)
                for u in range(2):
                    at(i, u, 0, 2, NT, new_rows)

            dve.wait_ge(s_load, 80)
            dve.wait_ge(s_const, 6)
            dve.wait_ge(s_prep, 1)
            dve.tensor_tensor(b2lo[:, :], b2f[:, :], b2hi[:, :].bitcast(F32), ALU.subtract).then_inc(s_prep, 1)
            dve.tensor_scalar(eps1[:, :], eps1[:, :], 1.0, None, ALU.add).then_inc(s_prep, 1)
            dve.wait_ge(s_prep, 4)
            dve.tensor_scalar(eye[:, :], g.ident[:, :], eps1[:, 0:1], None, ALU.mult).then_inc(s_prep, 1)
            pairs(dve, GR, 3, 0, body)

        @block.tensor
        def _(pe):
            def sum_edges(T):
                s = T.slot(2)
                pe.wait_ge(s_sel, T.t + 1)
                pe.wait_ge(s_Glo, T.t + 1)
                pe.wait_ge(s_H, T.t + 1)
                wait(pe, s_Zlo, T.t - 1)
                for c in range(C):
                    cols = slice(c * P, (c + 1) * P)
                    pe.matmul(chunk(psum_t[s], c, SEL), Ghi[s][:, cols], sel[s][:, :], start=True, stop=False)
                    pe.matmul(chunk(psum_t[s], c, SEL), Glo[s][:, cols], sel[s][:, :], start=False, stop=False)
                    ins = pe.matmul(chunk(psum_t[s], c, P), H[s][:, cols], eye[:, :], start=False, stop=True)
                ins.then_inc(s_summed, 1)

            def first(T):
                pe.wait_ge(s_Zlo, 2 * T.t + 2)
                wait(pe, s_Ulo, T.t)
                for o in range(C):
                    cols = slice(o * P, (o + 1) * P)
                    for c in range(C):
                        pe.matmul(psum_u[:, o, :], g.Whi[2][:, c, cols], Zhi[:, c, :], start=c == 0, stop=False)
                        pe.matmul(psum_u[:, o, :], g.Whi[2][:, c, cols], Zlo[:, c, :], start=False, stop=False)
                        ins = pe.matmul(psum_u[:, o, :], g.Wlo[2][:, c, cols], Zhi[:, c, :], start=False,
                                        stop=c == C - 1)
                ins.then_inc(s_u, 1)

            def second(T, ring):
                s = T.slot(2)
                pe.wait_ge(s_Ulo, T.k + 1)
                wait(pe, s_rows, T.t - 1)
                half = slice(s * P, (s + 1) * P)
                pe.matmul(psum_o[s][:, :], ones1[:, :], b2hi[:, :], start=True, stop=False)
                pe.matmul(psum_o[s][:, :], ones1[:, :], b2lo[:, :], start=False, stop=False)
                product(pe, psum_o[s][:, :], Uhi[ring][:, :, half], Ulo[ring][:, :, half], g.Whi[3], g.Wlo[3],
                        False, True).then_inc(s_prod, 1)

            def body(i, odd):
                at(i, 0, 1, 1, GR, first)
                for u in range(2):
                    at(i, u, 4, 2, NT, sum_edges)
                for u in range(2):
                    at(i, u, 0, 2, NT, lambda T: second(T, odd))

            pe.wait_ge(s_prep, 5)
            pairs(pe, GR, 3, 0, body)



def layer2(nc, io, g):
    NT, N = g.NT, g.N
    U = 4
    GR = NT // U
    with ExitStack() as ctx:
        e = Env(nc, ctx, "d_")
        src, out = g.xs[1], g.xs[2]
        W = Weights(nc, e, g, [(2, io.L3_W[0:D, :]), (3, io.L3_W[D:2 * D, :])])
        gamma, beta = e.sb("gamma", [P, D], F32), e.sb("beta", [P, D], F32)
        bf, bhi = e.sb("bf", [4, D], F32), e.sb("bhi", [4, D], F32R)
        blo = e.sb("blo", [4, D], F32R)
        has = e.ring("has", 2, [2, P], F32R)
        ones_f = e.sb("onesf", [2, P], F32)
        neg_half = e.sb("neghalf", [P, 1], F32)
        col, colx = e.ring("col", 2, [P, 3], I32), e.ring("colx", 2, [P, 3], I32)
        G, X = e.ring("G", 2, [P, EXT], F32), e.ring("X", 2, [P, EXT], F32)
        gsb = e.ring("gsb", 2, [P, 2], F32)
        H, XB = e.ring("H", 4, [P, D], F32), e.ring("XB", 4, [P, D], F32)
        Ghi, Glo = e.ring("Ghi", 2, [P, D], F32R), e.ring("Glo", 2, [P, D], F32R)
        sel, mask = e.ring("sel", 2, [P, SEL], F32R), e.ring("mask", 2, [P, SEL], F32)
        carry = e.ring("carry", 2, [P, C], F32)
        Thi, Tlo = e.ring("Thi", 2, [P, C, P], F32R), e.ring("Tlo", 2, [P, C, P], F32R)
        Hhi, Hlo = e.ring("Hhi", 2, [P, C, P], F32R), e.ring("Hlo", 2, [P, C, P], F32R)
        rows = e.ring("rows", 2, [P, EXT], F32)
        ylen = e.ring("ylen", 2, [P, 1], F32)
        ln_y, ln_x = Norm(e, "lny"), Norm(e, "lnx")
        psum_t = [e.ps(f"pt{i}", [P, 2, 512]) for i in range(2)]
        psum_h = [e.ps(f"ph{i}", [P, C, P]) for i in range(2)]
        psum_o = [e.ps(f"po{i}", [P, D]) for i in range(2)]

        s_load, s_const, s_prep = e.sem("s_load"), e.sem("s_const"), e.sem("s_prep")
        s_ones, s_has = e.sem("s_ones"), e.sems("s_has", 2)
        s_col, s_colx = e.sem("s_col"), e.sem("s_colx")
        s_G, s_X, s_put = e.sems("s_G", 2), e.sems("s_X", 2), e.sems("s_put", 2)
        s_gsb, s_Gn, s_H, s_Ghi, s_Glo, s_XB = (
            e.sem(n) for n in ("s_gsb", "s_Gn", "s_H", "s_Ghi", "s_Glo", "s_XB"))
        s_sel, s_mask = e.sem("s_sel"), e.sem("s_mask")
        s_summed, s_carried, s_copied = e.sem("s_summed"), e.sem("s_carried"), e.sem("s_copied")
        s_turned = e.sem("s_turned")
        s_Thi, s_Tlo, s_Hhi, s_Hlo = (e.sem(n) for n in ("s_Thi", "s_Tlo", "s_Hhi", "s_Hlo"))
        s_prod, s_y, s_cent, s_rows = (e.sem(n) for n in ("s_prod", "s_y", "s_cent", "s_rows"))
        tick = e.sem("tick")
        block = ctx.enter_context(e.block())

        @block.sync
        def _(sp):
            sp.dma_start(gamma[:, :], io.L2_gamma.partition_broadcast(P)).then_inc(s_load, 16)
            sp.dma_start(beta[:, :], io.L2_beta.partition_broadcast(P)).then_inc(s_load, 16)
            sp.dma_start(bf[0:1, :], row_of(io.L2_bs)).then_inc(s_load, 16)
            sp.dma_start(bf[1:2, :], row_of(io.L2_bn)).then_inc(s_load, 16)
            sp.wait_ge(s_load, 64)
            sp.wait_ge(s_ones, 1)

            def load_has(T):
                s = T.slot(2)
                wait(sp, s_prod, T.t - 1)
                sp.sem_inc(tick, 1)
                sp.dma_start(has[s][1:2, :].bitcast(F32), g.lastdram[bass.ds(T.t, 1), :]).then_inc(s_has[s], 16)

            def body(i):
                for u in range(U):
                    at(i, u, 2, U, NT, load_has)

            pipeline(sp, GR, 1, 0, body, between=lambda n: W.load_one(sp, n))

        @block.gpsimd
        def _(pool):
            def start_fetch(T):
                s = T.slot(2)
                wait(pool, s_Glo, T.t - 1)
                wait(pool, s_H, T.t - 1)
                wait(pool, s_XB, T.t - 1)
                wait(pool, s_X[s], 16 * T.use(2))
                indices(pool, g, "S", T, col, 3, tick, s_col)
                pool.wait_ge(s_col, T.t + 1)
                pool.sem_inc(tick, 1)
                fetch(pool, G[s][:, :], src, col[s][:, 0:1]).then_inc(s_G[s], 16)
                fetch(pool, X[s][:, :], src, col[s][:, 2:3]).then_inc(s_X[s], 16)

            def keep_x(T):
                s = T.slot(2)
                pool.wait_ge(s_X[s], 16 * (T.use(2) + 1))
                wait(pool, s_rows, T.t - 3)
                pool.tensor_tensor(XB[T.slot(4)][:, :], X[s][:, 0:D], beta[:, :], ALU.add).then_inc(s_XB, 1)

            def low(T):
                s = T.slot(2)
                wait(pool, s_summed, T.t - 1)
                pool.wait_ge(s_Ghi, T.t + 1)
                pool.tensor_tensor(Glo[s][:, :], G[s][:, 0:D], Ghi[s][:, :].bitcast(F32), ALU.subtract)\
                    .then_inc(s_Glo, 1)

            def norm_y(T):
                wait(pool, s_rows, T.t - 1)
                ln_y.finish(pool, tick, T, neg_half, ylen[T.slot(2)][:, :])

            def store(T):
                s = T.slot(2)
                wait(pool, s_put[s], 16 * T.use(2))
                indices(pool, g, "S", T, colx, 3, tick, s_colx)
                ln_x.finish(pool, tick, T, neg_half, rows[s][:, SCALE:SCALE + 1], rows[s][:, BIAS:BIAS + 1])
                pool.wait_ge(s_colx, T.t + 1)
                pool.wait_ge(ln_x.s_bias, T.t + 1)
                pool.sem_inc(tick, 1)
                put_rows(pool, out, colx[s][:, 2:3], rows[s][:, :], N - 1).then_inc(s_put[s], 16)

            def body(i):
                for u in range(U):
                    at(i, u, 2, U, NT, keep_x)
                    at(i, u, 2, U, NT, low)
                    at(i, u, 4, U, NT, start_fetch)
                    at(i, u, -1, U, NT, store)
                    at(i, u, 0, U, NT, norm_y)

            pool.memset(neg_half[:, :], -0.5).then_inc(s_const, 1)
            pool.memset(ones_f[:, :], 1.0).then_inc(s_const, 1)
            for s in range(2):
                pool.memset(carry[s][:, :], 0.0).then_inc(s_const, 1)
                pool.memset(rows[s][:, BIAS + 1:EXT], 0.0).then_inc(s_const, 1)
            pool.wait_ge(s_const, 6)
            pool.wait_ge(s_load, 64)
            pipeline(pool, GR, 1, 1, body, between=lambda n: W.split_low(pool, n))
            for s in range(2):
                pool.wait_ge(s_put[s], 16 * (NT // 2))

        @block.scalar
        def _(act):
            def norm_in(T):
                s = T.slot(2)
                act.wait_ge(s_gsb, T.t + 1)
                nc.scalar.activation(G[s][:, 0:D], G[s][:, 0:D], ACT.Relu, bias=gsb[s][:, 1:2],
                                     scale=gsb[s][:, 0:1]).then_inc(s_Gn, 1)
                act.wait_ge(s_X[s], 16 * (T.use(2) + 1))
                wait(act, s_y, T.t - 3)
                nc.scalar.activation(H[T.slot(4)][:, :], X[s][:, 0:D], ACT.Relu, bias=X[s][:, BIAS:BIAS + 1],
                                     scale=X[s][:, SCALE:SCALE + 1]).then_inc(s_H, 1)
                act.wait_ge(s_Gn, T.t + 1)
                wait(act, s_summed, T.t - 1)
                nc.scalar.copy(Ghi[s][:, :], G[s][:, 0:D]).then_inc(s_Ghi, 1)

            def high_sum(T):
                s = T.slot(2)
                act.wait_ge(s_turned, T.t + 1)
                wait(act, s_prod, T.t - 1)
                nc.scalar.copy(Hhi[s][:, :, :], psum_h[s][:, :, :]).then_inc(s_Hhi, 1)
                act.wait_ge(s_copied, T.t + 1)
                nc.scalar.copy(chunks_of(Thi[s]), all_chunks(psum_t[s], 0, P)).then_inc(s_Thi, 1)

            def body(i):
                for u in range(U):
                    at(i, u, 1, U, NT, high_sum)
                    at(i, u, 2, U, NT, norm_in)

            act.wait_ge(s_load, 64)
            nc.scalar.copy(bhi[0:2, :], bf[0:2, :]).then_inc(s_prep, 1)
            act.wait_ge(s_const, 2)
            nc.scalar.copy(has[0][:, :], ones_f[:, :])
            nc.scalar.copy(has[1][:, :], ones_f[:, :]).then_inc(s_ones, 1)
            pipeline(act, GR, 1, 0, body, between=lambda n: W.split_high(act, n))

        @block.vector
        def _(dve):
            def over_degree(T):
                s = T.slot(2)
                dve.wait_ge(s_G[s], 16 * (T.use(2) + 1))
                wait(dve, s_Gn, T.t - 1)
                dve.tensor_scalar(gsb[s][:, :], G[s][:, SCALE:BIAS + 1], g.rdeg[:, bass.ds(T.t, 1)], None, ALU.mult)\
                    .then_inc(s_gsb, 1)

            def carried(T):
                carry_in(dve, T, psum_t, mask, carry, s_summed, s_mask, s_carried, s_copied)

            def low_sum(T):
                s = T.slot(2)
                dve.wait_ge(s_Hhi, T.t + 1)
                dve.tensor_tensor(Hlo[s][:, :, :], psum_h[s][:, :, :], Hhi[s][:, :, :].bitcast(F32),
                                  ALU.subtract).then_inc(s_Hlo, 1)
                dve.wait_ge(s_Thi, T.t + 1)
                dve.tensor_tensor(chunks_of(Tlo[s]), all_chunks(psum_t[s], 0, P), chunks_of(Thi[s]).bitcast(F32),
                                  ALU.subtract).then_inc(s_Tlo, 1)

            def select(T):
                selection(dve, g, "S", T, sel, mask, s_sel, s_mask, s_summed, s_carried)

            def center(T):
                s = T.slot(2)
                dve.wait_ge(s_prod, T.t + 1)
                dve.scalar_tensor_tensor(psum_o[s][:, :], psum_o[s][:, :], 0.0, H[T.slot(4)][:, :],
                                         ALU.max, ALU.add).then_inc(s_y, 1)
                dve.wait_ge(s_y, T.t + 1)
                ln_y.statistics(dve, tick, T, psum_o[s][:, :], ln_y.s_scale)
                dve.wait_ge(ln_y.s_mean, T.t + 1)
                dve.scalar_tensor_tensor(psum_o[s][:, :], psum_o[s][:, :], ln_y.mean_var[s][:, 0:1], gamma[:, :],
                                         ALU.subtract, ALU.mult).then_inc(s_cent, 1)

            def new_rows(T):
                s = T.slot(2)
                dve.wait_ge(s_cent, T.t + 1)
                dve.wait_ge(ln_y.s_scale, T.t + 1)
                wait(dve, s_put[s], 16 * T.use(2))
                dve.scalar_tensor_tensor(rows[s][:, 0:D], psum_o[s][:, :], ylen[s][:, 0:1], XB[T.slot(4)][:, :],
                                         ALU.mult, ALU.add).then_inc(s_rows, 1)
                dve.wait_ge(s_rows, T.t + 1)
                ln_x.statistics(dve, tick, T, rows[s][:, 0:D], ln_x.s_bias)

            def body(i):
                for u in range(U):
                    at(i, u, -1, U, NT, new_rows)
                    at(i, u, 1, U, NT, carried)
                    at(i, u, 1, U, NT, low_sum)
                    at(i, u, 2, U, NT, over_degree)
                    at(i, u, 2, U, NT, select)
                    at(i, u, 0, U, NT, center)

            dve.wait_ge(s_load, 64)
            dve.wait_ge(s_const, 6)
            dve.wait_ge(s_prep, 1)
            dve.tensor_tensor(blo[0:2, :], bf[0:2, :], bhi[0:2, :].bitcast(F32), ALU.subtract).then_inc(s_prep, 1)
            pipeline(dve, GR, 1, 1, body)

        @block.tensor
        def _(pe):
            def sum_edges(T):
                s = T.slot(2)
                pe.wait_ge(s_sel, T.t + 1)
                pe.wait_ge(s_Glo, T.t + 1)
                wait(pe, s_Tlo, T.t - 1)
                for c in range(C):
                    cols = slice(c * P, (c + 1) * P)
                    pe.matmul(chunk(psum_t[s], c, SEL), Ghi[s][:, cols], sel[s][:, :], start=True, stop=False)
                    ins = pe.matmul(chunk(psum_t[s], c, SEL), Glo[s][:, cols], sel[s][:, :], start=False, stop=True)
                ins.then_inc(s_summed, 1)
                pe.wait_ge(s_H, T.t + 1)
                wait(pe, s_Hlo, T.t - 1)
                for c in range(C):
                    ins = pe.transpose(psum_h[s][:, c, :], H[T.slot(4)][:, c * P:(c + 1) * P], g.ident[:, :])
                ins.then_inc(s_turned, 1)

            def multiply(T):
                s = T.slot(2)
                pe.wait_ge(s_has[s], 16 * (T.use(2) + 1))
                wait(pe, s_rows, T.t - 1)
                pe.matmul(psum_o[s][:, :], has[s][:, :], bhi[0:2, :], start=True, stop=False)
                pe.matmul(psum_o[s][:, :], has[s][:, :], blo[0:2, :], start=False, stop=False)
                pe.wait_ge(s_Hlo, T.t + 1)
                product(pe, psum_o[s][:, :], Hhi[s], Hlo[s], g.Whi[1], g.Wlo[1], False, False)
                pe.wait_ge(s_Tlo, T.t + 1)
                product(pe, psum_o[s][:, :], Thi[s], Tlo[s], g.Whi[0], g.Wlo[0], False, True).then_inc(s_prod, 1)

            def body(i):
                for u in range(U):
                    at(i, u, 1, U, NT, sum_edges)
                    at(i, u, 0, U, NT, multiply)

            pe.wait_ge(s_prep, 2)
            pipeline(pe, GR, 1, 0, body)



def layer3(nc, io, g):
    NT, N = g.NT, g.N
    GR = NT // 2
    ENDS = ("src", "dst")
    INDEX = {"src": 1, "dst": 0}
    with ExitStack() as ctx:
        e = Env(nc, ctx, "f_")
        src = g.xs[2]
        b3f, b3hi, b3lo = e.sb("b3f", [1, D], F32), e.sb("b3hi", [1, D], F32R), e.sb("b3lo", [1, D], F32R)
        ones1, ones_f = e.sb("ones1", [1, P], F32R), e.sb("onesf", [P, P], F32)
        col, colx = e.ring("col", 2, [P, 3], I32), e.ring("colx", 2, [P, 3], I32)
        G = {k: e.ring("G" + k, 2, [P, EXT], F32) for k in ENDS}
        X = e.ring("X", 2, [P, EXT], F32)
        Hhi = {k: e.ring("Hhi" + k, 2, [P, C, P], F32R) for k in ENDS}
        Hlo = {k: e.ring("Hlo" + k, 2, [P, C, P], F32R) for k in ENDS}
        sel, lastsel = e.ring("sel", 2, [P, SEL], F32R), e.ring("lastsel", 2, [P, P], F32R)
        Mhi, Mlo = e.ring("Mhi", 2, [P, D], F32R), e.ring("Mlo", 2, [P, D], F32R)
        carry = e.ring("carry", 2, [P, D], F32)
        rows = e.ring("rows", 2, [P, D], F32)
        psum_h = {k: e.ps("ph" + k, [P, C, P]) for k in ENDS}
        psum_m = [e.ps(f"pm{i}", [P, D]) for i in range(2)]
        psum_o = [e.ps(f"po{i}", [P, D]) for i in range(2)]
        psum_c = [e.ps(f"pc{i}", [P, D]) for i in range(2)]

        s_load, s_const, s_prep = e.sem("s_load"), e.sem("s_const"), e.sem("s_prep")
        s_col, s_colx = e.sem("s_col"), e.sem("s_colx")
        s_G = {k: e.sems("s_G" + k, 2) for k in ENDS}
        s_X, s_put = e.sems("s_X", 2), e.sems("s_put", 2)
        s_Gn, s_turned, s_Hhi, s_Hlo = ({k: e.sem(n + k) for k in ENDS} for n in ("s_Gn", "s_turned", "s_Hhi", "s_Hlo"))
        s_sel, s_msg, s_Mhi, s_Mlo, s_sum, s_carry, s_added, s_rows = (
            e.sem(n) for n in ("s_sel", "s_msg", "s_Mhi", "s_Mlo", "s_sum", "s_carry", "s_added", "s_rows"))
        tick = e.sem("tick")
        block = ctx.enter_context(e.block())

        @block.sync
        def _(sp):
            sp.dma_start(b3f[:, :], row_of(io.L3_b)).then_inc(s_load, 16)
            sp.wait_ge(s_load, 16)

        @block.gpsimd
        def _(pool):
            def start_fetch(T):
                s = T.slot(2)
                for k in ENDS:
                    wait(pool, s_turned[k], T.t - 1)
                indices(pool, g, "S", T, col, 3, tick, s_col)
                pool.wait_ge(s_col, T.t + 1)
                pool.sem_inc(tick, 1)
                for k in ENDS:
                    n = INDEX[k]
                    fetch(pool, G[k][s][:, :], src, col[s][:, n:n + 1]).then_inc(s_G[k][s], 16)

            def fetch_x(T):
                s = T.slot(2)
                wait(pool, s_rows, T.t - 1)
                wait(pool, s_put[s], 16 * T.use(2))
                indices(pool, g, "S", T, colx, 3, tick, s_colx)
                pool.wait_ge(s_colx, T.t + 1)
                pool.sem_inc(tick, 1)
                fetch(pool, X[s][:, :], src, colx[s][:, 2:3]).then_inc(s_X[s], 16)

            def store(T):
                s = T.slot(2)
                pool.wait_ge(s_rows, T.t + 1)
                pool.sem_inc(tick, 1)
                put_rows(pool, io.out, colx[s][:, 2:3], rows[s][:, :], N - 1).then_inc(s_put[s], 16)

            def body(i):
                for u in range(2):
                    at(i, u, -1, 2, NT, fetch_x)
                    at(i, u, -2, 2, NT, store)
                    at(i, u, 3, 2, NT, start_fetch)

            pool.memset(ones_f[:, :], 1.0).then_inc(s_const, 1)
            for s in range(2):
                pool.memset(carry[s][:, :], 0.0).then_inc(s_const, 1)
            pipeline(pool, GR, 2, 1, body)
            for s in range(2):
                pool.wait_ge(s_put[s], 16 * GR)

        @block.scalar
        def _(act):
            def norm_in(T):
                s = T.slot(2)
                for k in ENDS:
                    act.wait_ge(s_G[k][s], 16 * (T.use(2) + 1))
                    nc.scalar.activation(G[k][s][:, 0:D], G[k][s][:, 0:D], ACT.Relu, bias=G[k][s][:, BIAS:BIAS + 1],
                                         scale=G[k][s][:, SCALE:SCALE + 1]).then_inc(s_Gn[k], 1)

            def high(T):
                s = T.slot(2)
                for k in ENDS:
                    act.wait_ge(s_turned[k], T.t + 1)
                    wait(act, s_msg, T.t - 1)
                    nc.scalar.copy(Hhi[k][s][:, :, :], psum_h[k][:, :, :]).then_inc(s_Hhi[k], 1)

            def message(T):
                s = T.slot(2)
                act.wait_ge(s_msg, T.t + 1)
                wait(act, s_sum, T.t - 1)
                nc.scalar.activation(Mhi[s][:, :], psum_m[s][:, :], ACT.Relu).then_inc(s_Mhi, 1)

            def body(i):
                for u in range(2):
                    at(i, u, 1, 2, NT, high)
                    at(i, u, 2, 2, NT, norm_in)
                    at(i, u, 0, 2, NT, message)

            act.wait_ge(s_load, 16)
            nc.scalar.copy(b3hi[:, :], b3f[:, :]).then_inc(s_prep, 1)
            act.wait_ge(s_const, 1)
            nc.scalar.copy(ones1[:, :], ones_f[0:1, :]).then_inc(s_prep, 1)
            pipeline(act, GR, 1, 0, body)

        @block.vector
        def _(dve):
            def low(T):
                s = T.slot(2)
                for k in ENDS:
                    dve.wait_ge(s_Hhi[k], T.t + 1)
                    dve.tensor_tensor(Hlo[k][s][:, :, :], psum_h[k][:, :, :], Hhi[k][s][:, :, :].bitcast(F32),
                                      ALU.subtract).then_inc(s_Hlo[k], 1)

            def select(T):
                s = T.slot(2)
                wait(dve, s_sum, T.t - 1)
                dve.tensor_scalar(lastsel[s][:, :], ones_f[:, :], g.in_last[:, bass.ds(T.t, 1)], None, ALU.mult)
                selection(dve, g, "S", T, sel, None, s_sel, None, s_sum, None)

            def message(T):
                s = T.slot(2)
                dve.wait_ge(s_Mhi, T.t + 1)
                dve.scalar_tensor_tensor(Mlo[s][:, :], psum_m[s][:, :], 0.0, Mhi[s][:, :].bitcast(F32),
                                         ALU.max, ALU.subtract).then_inc(s_Mlo, 1)

            def combine(T):
                s, before = T.slot(2), (T.j - 1) % 2
                one = bass.ds(T.t, 1)
                dve.wait_ge(s_sum, T.t + 1)
                wait(dve, s_carry, T.t)
                dve.scalar_tensor_tensor(carry[s][:, :], carry[before][:, :], g.same_last[:, one], psum_c[s][:, :],
                                         ALU.mult, ALU.add).then_inc(s_carry, 1)
                dve.scalar_tensor_tensor(psum_o[s][:, :], carry[before][:, :], g.takes[:, one], psum_o[s][:, :],
                                         ALU.mult, ALU.add).then_inc(s_added, 1)
                dve.wait_ge(s_added, T.t + 1)
                dve.wait_ge(s_X[s], 16 * (T.use(2) + 1))
                wait(dve, s_put[s], 16 * T.use(2))
                dve.tensor_tensor(rows[s][:, :], psum_o[s][:, :], X[s][:, 0:D], ALU.add).then_inc(s_rows, 1)

            def body(i):
                for u in range(2):
                    at(i, u, 1, 2, NT, low)
                    at(i, u, -1, 2, NT, combine)
                    at(i, u, 0, 2, NT, select)
                    at(i, u, 0, 2, NT, message)

            dve.wait_ge(s_const, 3)
            dve.wait_ge(s_prep, 1)
            dve.tensor_tensor(b3lo[:, :], b3f[:, :], b3hi[:, :].bitcast(F32), ALU.subtract).then_inc(s_prep, 1)
            pipeline(dve, GR, 1, 1, body)

        @block.tensor
        def _(pe):
            def turn(T):
                s = T.slot(2)
                for k in ENDS:
                    pe.wait_ge(s_Gn[k], T.t + 1)
                    wait(pe, s_Hlo[k], T.t)
                    for c in range(C):
                        ins = pe.transpose(psum_h[k][:, c, :], G[k][s][:, c * P:(c + 1) * P], g.ident[:, :])
                    ins.then_inc(s_turned[k], 1)

            def multiply(T):
                s = T.slot(2)
                wait(pe, s_Mlo, T.t - 1)
                pe.matmul(psum_m[s][:, :], ones1[:, :], b3hi[:, :], start=True, stop=False)
                pe.matmul(psum_m[s][:, :], ones1[:, :], b3lo[:, :], start=False, stop=False)
                for n, k in enumerate(ENDS):
                    pe.wait_ge(s_Hlo[k], T.t + 1)
                    ins = product(pe, psum_m[s][:, :], Hhi[k][s], Hlo[k][s], g.Whi[2 + n], g.Wlo[2 + n], False, n == 1)
                ins.then_inc(s_msg, 1)

            def sum_edges(T):
                s = T.slot(2)
                pe.wait_ge(s_sel, T.t + 1)
                pe.wait_ge(s_Mlo, T.t + 1)
                wait(pe, s_rows, T.t - 1)
                pe.matmul(psum_o[s][:, :], sel[s][:, 0:P], Mhi[s][:, :], start=True, stop=False)
                pe.matmul(psum_o[s][:, :], sel[s][:, 0:P], Mlo[s][:, :], start=False, stop=True)
                pe.matmul(psum_c[s][:, :], lastsel[s][:, :], Mhi[s][:, :], start=True, stop=False)
                pe.matmul(psum_c[s][:, :], lastsel[s][:, :], Mlo[s][:, :], start=False, stop=True).then_inc(s_sum, 1)

            def body(i):
                for u in range(2):
                    at(i, u, 1, 2, NT, turn)
                    at(i, u, -1, 2, NT, sum_edges)
                    at(i, u, 0, 2, NT, multiply)

            pe.wait_ge(s_prep, 3)
            pipeline(pe, GR, 1, 1, body)


WEIGHTS = {"L0_W1": "L0_gnn_W1", "L0_W2": "L0_gnn_W2", "L1_W1": "L1_gnn_W1", "L1_W2": "L1_gnn_W2",
           "L2_Ws": "L2_gnn_W_self", "L2_Wn": "L2_gnn_W_neigh", "L3_W": "L3_gnn_W"}
VECTORS = {"L0_b1": "L0_gnn_b1", "L0_b2": "L0_gnn_b2", "L1_b1": "L1_gnn_b1", "L1_b2": "L1_gnn_b2",
           "L1_gamma": "L1_gnn_gamma", "L1_beta": "L1_gnn_beta", "L2_bs": "L2_gnn_b_self",
           "L2_bn": "L2_gnn_b_neigh", "L2_gamma": "L2_gnn_ln_gamma", "L2_beta": "L2_gnn_ln_beta",
           "L3_b": "L3_gnn_b"}


class Named:
    pass


def program(nc, io, N):
    NT = N // P
    g = Named()
    g.NT, g.N = NT, N

    def dram(name, shape, dt=F32):
        return nc.dram_tensor(name, shape, dt, kind="Internal").ap()

    g.h0, g.h1 = dram("h0", [N, D]), dram("h1", [N, D])
    g.xs = [dram(f"x{n}", [N, EXT]) for n in range(1, 4)]
    g.seq = {k: dram("seq" + k, [N + 1]) for k in "DS"}
    g.seldram = {k: dram("sel" + k, [NT, SEL], I16) for k in "DS"}
    g.lastdram, g.qdram = dram("lastdram", [NT, P]), dram("qdram", [NT, P], I16)
    with ExitStack() as ctx:
        e = Env(nc, ctx, "")
        parts = e.sb("parts", [P, 8, C, D], F32R)
        g.parts = parts[:, :, :, :].rearrange("p w c n -> p (w c n)")
        g.Whi, g.Wlo = ([parts[:, 2 * slot + half] for slot in range(4)] for half in range(2))
        g.ident = e.sb("ident", [P, P], F32)
        g.selrows = {k: e.sb("selrows" + k, [P, NT, SEL], I16) for k in "DS"}
        g.index = {k: e.sb("index" + k, [P, NT, 3], I32) for k in "DS"}
        g.keycol, g.keylast, g.keyprev = (
            {k: e.sb(n + k, [P, NT], F32) for k in "DS"} for n in ("keycol", "keylast", "keyprev"))
        g.degcol, g.rdeg = e.sb("degcol", [P, NT], F32), e.sb("rdeg", [P, NT], F32)
        g.same_last, g.takes, g.in_last = (e.sb(n, [P, NT], F32) for n in ("samelast", "takes", "inlast"))
        prepare_orders(nc, io, g)
        layer0(nc, io, g, False)
        layer0(nc, io, g, True)
        layer1(nc, io, g)
        layer2(nc, io, g)
        layer3(nc, io, g)


def kernel(**inputs):
    import numpy as np
    import concourse.bacc as bacc
    from concourse.bass_utils import run_bass_kernel_spmd

    x, src, dst = (np.asarray(inputs[n]) for n in ("x", "src", "dst"))
    nodes = x.shape[0]
    N = -(-nodes // (4 * P)) * 4 * P
    loops = np.arange(nodes, N, dtype=src.dtype)
    src, dst = np.concatenate([src, loops]), np.concatenate([dst, loops])
    arrays = {"x": np.concatenate([x, np.zeros((N - nodes, D), x.dtype)]), "src": src, "dst": dst,
              "src_col": np.ascontiguousarray(src.reshape(-1, P).T),
              "dst_col": np.ascontiguousarray(dst.reshape(-1, P).T),
              "eps": np.asarray(inputs["L1_gnn_eps"]).reshape(1)}
    for name, given in WEIGHTS.items():
        arrays[name] = np.ascontiguousarray(np.asarray(inputs[given]).T)
    for name, given in VECTORS.items():
        arrays[name] = np.asarray(inputs[given])
    arrays["L1_b1col"] = np.ascontiguousarray(arrays.pop("L1_b1").reshape(C, P).T)

    nc = bacc.Bacc("TRN2", target_bir_lowering=False, num_devices=1)
    io = Named()
    for name, a in arrays.items():
        io.__dict__[name] = nc.dram_tensor("in_" + name, a.shape, mybir.dt.from_np(a.dtype), kind="ExternalInput").ap()
    io.out = nc.dram_tensor("out_x", (N, D), F32, kind="ExternalOutput").ap()
    program(nc, io, N)
    r = run_bass_kernel_spmd(nc, [{"in_" + name: a for name, a in arrays.items()}], core_ids=[0])
    return r.results[0]["out_x"][0:nodes]
```

```python
from contextlib import ExitStack, contextmanager

import concourse.bass as bass
from concourse import mybir

P = 128
D = 512
C = D // P
EXT = 520
SCALE, BIAS = D, D + 1
SEL = P + 2
LN_EPS = 1e-5
NOWHERE = 1 << 20

F32, F32R, BF16 = mybir.dt.float32, mybir.dt.float32r, mybir.dt.bfloat16
I32, I16 = mybir.dt.int32, mybir.dt.int16
ALU = mybir.AluOpType
ACT = mybir.ActivationFunctionType
AX = mybir.AxisListType


class Tile:

    def __init__(self, k, j, unroll):
        self.k, self.j, self.unroll = k, j, unroll
        self.t = k * unroll + j if j else k * unroll

    def slot(self, ring):
        return self.j % ring

    def use(self, ring):
        each = self.unroll // ring
        n = self.k * each if each > 1 else self.k
        return n + self.j // ring if self.j // ring else n


def at(i, u, off, unroll, tiles, stage):
    tile = Tile(i + (u + off) // unroll, (u + off) % unroll, unroll)
    if not isinstance(i, int) or 0 <= tile.t < tiles:
        stage(tile)


def pipeline(eng, groups, lead, drain, body, ahead=2, between=None):
    first, last = 2, groups - ahead
    for i in range(-lead, first):
        body(i)
        if between and i >= 0:
            between(i)
    with eng.Fori(first, last) as i:
        body(i)
    for i in range(last, groups + drain):
        body(i)


def wait(eng, sem, value):
    if not isinstance(value, int) or value > 0:
        eng.wait_ge(sem, value)


class Env:

    def __init__(self, nc, ctx, prefix):
        self.nc, self.ctx, self.prefix = nc, ctx, prefix
        self.semaphores = []

    def sb(self, name, shape, dt):
        return self.ctx.enter_context(self.nc.sbuf_tensor(self.prefix + name, shape, dt))

    def ring(self, name, n, shape, dt):
        return [self.sb(f"{name}{i}", shape, dt) for i in range(n)]

    def ps(self, name, shape, dt=F32):
        return self.ctx.enter_context(self.nc.psum_tensor(self.prefix + name, shape, dt))

    def sem(self, name):
        self.semaphores.append(self.nc.alloc_semaphore(self.prefix + name))
        return self.semaphores[-1]

    @contextmanager
    def block(self):
        with self.nc.Block() as block:
            yield block
        self.nc.clear_and_free_semaphores(self.semaphores)
        self.nc.all_engine_barrier()
        self.semaphores = []

    def sems(self, name, n):
        return [self.sem(f"{name}{i}") for i in range(n)]


def row_of(vector):
    return vector.rearrange("(a n) -> a n", a=1)



def prepare_orders(nc, io, g):
    NT, N = g.NT, g.N
    KEYS = ("D", "S")
    G4 = NT // 4
    with ExitStack() as ctx:
        e = Env(nc, ctx, "p_")
        sb, ps, sem = e.sb, e.ps, e.sem

        key_i = {k: sb("keyi" + k, [P, NT], I32) for k in KEYS}
        tmp_i = sb("tmpi", [P, NT], I32)
        key_f = {k: sb("keyf" + k, [P, NT], F32) for k in KEYS}
        hi_f = {k: sb("hif" + k, [P, NT], F32) for k in KEYS}
        lo_f = {k: sb("lof" + k, [P, NT], F32) for k in KEYS}
        hirow = {k: g.selrows[k][:, :, :].rearrange("p t c -> p (t c)")[0:NT, 0:N] for k in KEYS}
        iota_i = sb("iotai", [P, P], I32)
        iota_b = sb("iotab", [P, P], BF16)
        iota_f = sb("iotaf", [P, P], F32)
        pidx_i = sb("pidxi", [P, 1], I32)
        pidx = sb("pidx", [P, 1], F32)
        node_i = sb("nodei", [P, NT], I32)
        node_f = sb("nodef", [P, NT], F32)
        ones_f = sb("onesf", [P, P], F32)
        ones_b = sb("onesb", [P, 2], BF16)
        before_f = sb("beforef", [P, P], F32)
        before_b = sb("beforeb", [P, P], BF16)
        neg_half = sb("neghalf", [P, 1], F32)
        count = {k: sb("count" + k, [NT, P], F32) for k in KEYS}
        start = {k: sb("start" + k, [NT, P], F32) for k in KEYS}
        colform = sb("colform", [P, NT], F32)
        total = sb("total", [NT, 1], F32)
        totals = sb("totals", [NT, P], F32)

        pos = {k: sb("pos" + k, [P, NT], F32) for k in KEYS}
        deg = {k: sb("deg" + k, [P, NT], F32) for k in KEYS}
        intile = {k: sb("intile" + k, [P, NT], F32) for k in KEYS}

        c12 = ctx.enter_context(ExitStack())
        first = Env(nc, c12, "q_")
        keyrow = {k: first.sb("keyrow" + k, [P, N], I16) for k in KEYS}
        zero_row = first.sb("zerorow", [P, D], F32)
        spare = g.parts.bitcast(BF16)
        words = NT * P
        OHlo = {k: spare[:, m * words:(m + 1) * words].rearrange("p (t n) -> p t n", n=P)
                for m, k in enumerate(KEYS)}
        OHhi = {"D": spare[:, 2 * words:2 * words + NT * NT].rearrange("p (t n) -> p t n", n=NT),
                "S": first.sb("ohhiS", [P, NT, NT], BF16)}

        s_load = sem("s_load")
        s_rowload = {k: sem("s_rowload" + k) for k in KEYS}
        s_iota = sem("s_iota")
        s_v = sem("s_v")
        s_one = sem("s_one")
        s_cnt = sem("s_cnt")
        s_pe = sem("s_pe")

        with ExitStack() as c1:
            pcount = {k: c1.enter_context(nc.psum_tensor("p_pcount" + k, [P, 512], F32)) for k in KEYS}
            ptr = c1.enter_context(nc.psum_tensor("p_ptr", [P, 512], F32))
            pstart = c1.enter_context(nc.psum_tensor("p_pstart", [P, 512], F32))
            block = c1.enter_context(e.block())

            @block.sync
            def _(sp):
                sp.dma_start(key_i["D"][:, :], io.dst_col).then_inc(s_load, 16)
                sp.dma_start(key_i["S"][:, :], io.src_col).then_inc(s_load, 16)

            @block.gpsimd
            def _(pool):
                pool.dma_start(keyrow["D"][:, :], io.dst.partition_broadcast(P)).then_inc(s_rowload["D"], 16)
                pool.dma_start(keyrow["S"][:, :], io.src.partition_broadcast(P)).then_inc(s_rowload["S"], 16)
                pool.iota(iota_i[:, :], pattern=[[1, P]], base=0, channel_multiplier=0).then_inc(s_iota, 1)
                pool.iota(pidx_i[:, :], pattern=[[0, 1]], base=0, channel_multiplier=1).then_inc(s_iota, 1)
                pool.iota(node_i[:, :], pattern=[[P, NT]], base=0, channel_multiplier=1).then_inc(s_iota, 1)
                pool.memset(g.ident[:, :], 0.0).then_inc(s_iota, 1)
                pool.memset(ones_f[:, :], 1.0)
                pool.memset(ones_b[:, :], 1.0)
                pool.memset(zero_row[:, :], 0.0)
                pool.memset(neg_half[:, :], -0.5)
                pool.wait_ge(s_iota, 4)
                pool.affine_select(out=g.ident[:, :], in_=g.ident[:, :], compare_op=ALU.not_equal, fill=1.0,
                                   base=0, pattern=[[-1, P]], channel_multiplier=1).then_inc(s_iota, 1)

            @block.vector
            def _(dve):
                n = [0]

                def step(ins):
                    ins.then_inc(s_v, 1)
                    n[0] += 1
                    dve.wait_ge(s_v, n[0])

                dve.wait_ge(s_iota, 5)
                step(dve.tensor_copy(iota_b[:, :], iota_i[:, :]))
                step(dve.tensor_copy(iota_f[:, :], iota_i[:, :]))
                step(dve.tensor_copy(pidx[:, :], pidx_i[:, :]))
                step(dve.tensor_copy(node_f[:, :], node_i[:, :]))
                step(dve.tensor_scalar(before_f[:, :], iota_f[:, :], pidx[:, 0:1], None, ALU.is_gt))
                step(dve.tensor_scalar(before_b[:, :], iota_f[:, :], pidx[:, 0:1], None, ALU.is_gt))
                dve.wait_ge(s_load, 32)
                for k in KEYS:
                    step(dve.tensor_copy(key_f[k][:, :], key_i[k][:, :]))
                    step(dve.tensor_scalar(tmp_i[:, :], key_i[k][:, :], 7, None, ALU.logical_shift_right))
                    step(dve.tensor_copy(hi_f[k][:, :], tmp_i[:, :]))
                    step(dve.tensor_scalar(tmp_i[:, :], key_i[k][:, :], P - 1, None, ALU.bitwise_and))
                    step(dve.tensor_copy(lo_f[k][:, :], tmp_i[:, :]))
                with dve.Fori(0, NT) as t:
                    for k in KEYS:
                        dve.tensor_scalar(OHhi[k][:, bass.ds(t, 1), :], iota_b[:, 0:NT],
                                          hi_f[k][:, bass.ds(t, 1)], None, ALU.is_equal)
                        dve.tensor_scalar(OHlo[k][:, bass.ds(t, 1), :], iota_b[:, :],
                                          lo_f[k][:, bass.ds(t, 1)], None, ALU.is_equal).then_inc(s_one, 1)
                for k in KEYS:
                    dve.wait_ge(s_rowload[k], 16)
                    step(dve.tensor_scalar(hirow[k][:, :], keyrow[k][0:NT, :], 7, None, ALU.logical_shift_right))
                for m, k in enumerate(KEYS):
                    dve.wait_ge(s_cnt, m + 1)
                    step(dve.tensor_copy(count[k][:, :], pcount[k][0:NT, 0:P]))
                for m, k in enumerate(KEYS):
                    dve.wait_ge(s_pe, 2 * m + 1)
                    step(dve.tensor_copy(colform[:, :], ptr[:, 0:NT]))
                    step(dve.tensor_reduce(total[:, :], count[k][:, :], AX.X, ALU.add))
                    step(dve.tensor_scalar(totals[:, :], ones_f[0:NT, :], total[:, 0:1], None, ALU.mult))
                    dve.wait_ge(s_pe, 2 * m + 2)
                    step(dve.tensor_copy(start[k][:, :], pstart[0:NT, 0:P]))

            @block.tensor
            def _(pe):
                pe.wait_ge(s_one, 2)
                for k in KEYS:
                    pe.matmul(pcount[k][0:NT, 0:P], OHhi[k][:, 0, :], OHlo[k][:, 0, :], start=True, stop=False)
                with pe.Fori(1, NT - 1) as t:
                    pe.wait_ge(s_one, 2 * t + 2)
                    for k in KEYS:
                        pe.matmul(pcount[k][0:NT, 0:P], OHhi[k][:, bass.ds(t, 1), :], OHlo[k][:, bass.ds(t, 1), :],
                                  start=False, stop=False)
                pe.wait_ge(s_one, 2 * NT)
                for k in KEYS:
                    pe.matmul(pcount[k][0:NT, 0:P], OHhi[k][:, NT - 1, :], OHlo[k][:, NT - 1, :],
                              start=False, stop=True).then_inc(s_cnt, 1)
                pe.wait_ge(s_iota, 5)
                for m, k in enumerate(KEYS):
                    base = 6 + 10 + 2
                    pe.wait_ge(s_v, base + m + 1 if m == 0 else base + 2 + 4)
                    pe.transpose(ptr[:, 0:NT], count[k][:, :], g.ident[0:NT, 0:NT]).then_inc(s_pe, 1)
                    pe.wait_ge(s_v, base + 2 + 4 * m + 3)
                    pe.matmul(pstart[0:NT, 0:P], colform[:, :], before_f[:, :], start=True, stop=False)
                    pe.matmul(pstart[0:NT, 0:P], before_f[0:NT, 0:NT], totals[:, :], start=False, stop=True)\
                        .then_inc(s_pe, 1)

        U = 4
        with ExitStack() as c2:
            f = Env(nc, c2, "r_")
            OHhiT = {k: f.ring("ohhit" + k, 2, [NT, P], F32) for k in KEYS}
            same = {k: f.ring("same" + k, 2, [P, P], BF16) for k in KEYS}
            earlier = {k: f.ring("earlier" + k, 2, [P, P], BF16) for k in KEYS}
            table = {k: f.ring("table" + k, 2, [NT, 2, P], F32) for k in KEYS}
            picked = f.sb("picked", [P, 2, P], F32)
            pair = f.sb("pair", [P, 2], F32)
            xt = f.ring("xt", U, [P, EXT], F32)
            h0 = f.ring("h0", 2, [P, D], F32)
            st = f.ring("st", 2, [P, 6], F32)
            mv = f.ring("mv", 2, [P, 2], F32)
            va = f.ring("va", 2, [P, 1], F32)
            pbase = {k: f.ps("pbase" + k, [P, 512]) for k in KEYS}
            plook = {k: [f.ps(f"plook{k}{j}", [P, 2, P]) for j in range(2)] for k in KEYS}
            pin = f.ps("pin", [P, 512])
            q_tab, q_acc, q_hot, q_eq, q_early, q_look, q_in, q_pick, q_red = (
                {k: f.sem(n + k) for k in KEYS} for n in
                ("q_tab", "q_acc", "q_hot", "q_eq", "q_early", "q_look", "q_in", "q_pick", "q_red"))
            q_x = f.sems("q_x", U)
            q_st, q_mv, q_var, q_a, q_b, q_h = (f.sem(n) for n in ("q_st", "q_mv", "q_var", "q_a", "q_b", "q_h"))
            q_out = f.sems("q_out", 2)
            q_ext = f.sems("q_ext", U)
            q_zero = f.sem("q_zero")
            q_tick = f.sem("q_tick")
            q_done = f.sem("q_done")
            block = c2.enter_context(f.block())
            GR = NT // U

            @block.sync
            def _(sp):
                def load(T):
                    s = T.slot(U)
                    wait(sp, q_h, T.t - U + 1)
                    sp.sem_inc(q_tick, 1)
                    wait(sp, q_ext[s], 16 * T.use(U))
                    sp.sem_inc(q_tick, 1)
                    sp.dma_start(xt[s][:, 0:D], io.x[bass.ds(T.t * P, P), :]).then_inc(q_x[s], 16)

                def store(T):
                    s = T.slot(2)
                    sp.wait_ge(q_h, T.t + 1)
                    sp.sem_inc(q_tick, 1)
                    sp.dma_start(g.h0[bass.ds(T.t * P, P), :], h0[s][:, :]).then_inc(q_out[s], 16)
                    sp.dma_start(g.xs[0][bass.ds(T.t * P, P), :], xt[T.slot(U)][:, :]).then_inc(q_ext[T.slot(U)], 16)
                    sp.dma_start(g.h1[bass.ds(T.t * P, P), :], zero_row[:, :]).then_inc(q_zero, 16)

                def body(i):
                    for u in range(U):
                        at(i, u, 0, U, NT, store)
                        at(i, u, 3, U, NT, load)

                pipeline(sp, GR, 1, 0, body)
                for s in range(2):
                    sp.wait_ge(q_out[s], 16 * (NT // 2))
                for s in range(U):
                    sp.wait_ge(q_ext[s], 16 * GR)
                sp.wait_ge(q_zero, 16 * NT)

            @block.vector
            def _(dve):
                def hot(T):
                    s = T.slot(2)
                    for k in KEYS:
                        wait(dve, q_look[k], T.t - 1)
                        dve.tensor_scalar(OHhiT[k][s][:, :], hirow[k][:, bass.ds(T.t * P, P)], pidx[0:NT, 0:1],
                                          None, ALU.is_equal).then_inc(q_hot[k], 1)
                        wait(dve, q_early[k], T.t - 1)
                        dve.tensor_scalar(same[k][s][:, :], keyrow[k][:, bass.ds(T.t * P, P)],
                                          key_f[k][:, bass.ds(T.t, 1)], None, ALU.is_equal).then_inc(q_eq[k], 1)
                    for k in KEYS:
                        dve.wait_ge(q_eq[k], T.t + 1)
                        wait(dve, q_in[k], T.t - 1)
                        dve.tensor_tensor(earlier[k][s][:, :], same[k][s][:, :], before_b[:, :], ALU.mult)\
                            .then_inc(q_early[k], 1)

                def pick(T):
                    s = T.slot(2)
                    for k in KEYS:
                        dve.wait_ge(q_look[k], T.t + 1)
                        if k == "D":
                            wait(dve, q_red["S"], T.t)
                        else:
                            dve.wait_ge(q_red["D"], T.t + 1)
                        dve.tensor_tensor(picked[:, :, :], plook[k][s][:, :, :],
                                          OHlo[k][:, bass.ds(T.t, 1), :].broadcast_to([P, 2, P]), ALU.mult)\
                            .then_inc(q_pick[k], 1)
                        dve.wait_ge(q_pick[k], T.t + 1)
                        dve.tensor_reduce(pos[k][:, bass.ds(T.t, 1)], picked[:, 0, :], AX.X, ALU.add)
                        dve.tensor_reduce(deg[k][:, bass.ds(T.t, 1)], picked[:, 1, :], AX.X, ALU.add)\
                            .then_inc(q_red[k], 1)

                def norm_x(T):
                    s = T.slot(2)
                    dve.wait_ge(q_x[T.slot(U)], 16 * (T.use(U) + 1))
                    dve.bn_stats(st[s][:, :], xt[T.slot(U)][:, 0:D]).then_inc(q_st, 1)
                    dve.wait_ge(q_st, T.t + 1)
                    wait(dve, q_b, T.t - 1)
                    dve.sem_inc(q_tick, 1)
                    dve.bn_aggr(mv[s][:, :], st[s][:, :]).then_inc(q_mv, 1)

                def body(i):
                    for u in range(U):
                        at(i, u, 1, U, NT, hot)
                        at(i, u, 1, U, NT, norm_x)
                        at(i, u, 0, U, NT, pick)

                pipeline(dve, GR, 1, 0, body)
                for k in KEYS:
                    dve.wait_ge(q_red[k], NT)
                    dve.wait_ge(q_in[k], NT)
                for m, k in enumerate(KEYS):
                    dve.tensor_copy(intile[k][:, :], pin[:, m * P:m * P + NT]).then_inc(q_done, 1)
                    dve.wait_ge(q_done, 2 * m + 1)
                    dve.tensor_tensor(pos[k][:, :], pos[k][:, :], intile[k][:, :], ALU.add).then_inc(q_done, 1)

            @block.gpsimd
            def _(pool):
                def scale(T):
                    s, x = T.slot(2), xt[T.slot(U)]
                    pool.wait_ge(q_mv, T.t + 1)
                    pool.sem_inc(q_tick, 1)
                    pool.tensor_scalar(va[s][:, 0:1], mv[s][:, 1:2], 1.0, LN_EPS, ALU.mult, ALU.add)\
                        .then_inc(q_var, 1)
                    pool.wait_ge(q_var, T.t + 1)
                    pool.tensor_tensor(x[:, SCALE:SCALE + 1], va[s][:, 0:1], neg_half[:, :], ALU.pow).then_inc(q_a, 1)
                    pool.wait_ge(q_a, T.t + 1)
                    pool.sem_inc(q_tick, 1)
                    pool.tensor_scalar(x[:, BIAS:BIAS + 1], mv[s][:, 0:1], x[:, SCALE:SCALE + 1], -1.0,
                                       ALU.mult, ALU.mult)\
                        .then_inc(q_b, 1)

                def body(i):
                    for u in range(U):
                        at(i, u, 0, U, NT, scale)

                for s in range(U):
                    pool.memset(xt[s][:, BIAS + 1:EXT], 0.0)
                pipeline(pool, GR, 0, 0, body)

            @block.scalar
            def _(act):
                def table_of(T):
                    s = T.slot(2)
                    for k in KEYS:
                        act.wait_ge(q_acc[k], T.t + 1)
                        wait(act, q_look[k], T.t - 1)
                        nc.scalar.copy(table[k][s][:, 0, :], pbase[k][0:NT, 0:P]).then_inc(q_tab[k], 1)

                def relu(T):
                    s, x = T.slot(2), xt[T.slot(U)]
                    act.wait_ge(q_b, T.t + 1)
                    wait(act, q_out[s], 16 * T.use(2))
                    nc.scalar.activation(h0[s][:, :], x[:, 0:D], ACT.Relu, bias=x[:, BIAS:BIAS + 1],
                                         scale=x[:, SCALE:SCALE + 1]).then_inc(q_h, 1)

                def body(i):
                    for u in range(U):
                        at(i, u, 0, U, NT, table_of)
                        at(i, u, 0, U, NT, relu)

                for k in KEYS:
                    for s in range(2):
                        nc.scalar.copy(table[k][s][:, 1, :], count[k][:, :])
                pipeline(act, GR, 0, 0, body)

            @block.tensor
            def _(pe):
                for k in KEYS:
                    pe.matmul(pbase[k][0:NT, 0:P], g.ident[0:NT, 0:NT], start[k][:, :], start=True, stop=True,
                              skip_group_check=True).then_inc(q_acc[k], 1)

                def look(T):
                    s = T.slot(2)
                    for m, k in enumerate(KEYS):
                        pe.wait_ge(q_tab[k], T.t + 1)
                        pe.matmul(pbase[k][0:NT, 0:P], OHhi[k][:, bass.ds(T.t, 1), :], OHlo[k][:, bass.ds(T.t, 1), :],
                                  start=False, stop=True, skip_group_check=True).then_inc(q_acc[k], 1)
                        pe.wait_ge(q_hot[k], T.t + 1)
                        wait(pe, q_pick[k], T.t - 1)
                        pe.matmul(plook[k][s][:, :, :], OHhiT[k][s][:, :], table[k][s][:, :, :],
                                  start=True, stop=True).then_inc(q_look[k], 1)
                        pe.wait_ge(q_early[k], T.t + 1)
                        pe.matmul(pin[:, bass.ds(T.t + m * P, 1)], earlier[k][s][:, :], ones_b[:, 0:1],
                                  start=True, stop=True, skip_group_check=True).then_inc(q_in[k], 1)

                def body(i):
                    for u in range(U):
                        at(i, u, 0, U, NT, look)

                pipeline(pe, GR, 0, 0, body)

        c12.close()
        other_f = {"D": key_f["S"], "S": key_f["D"]}
        scol = {k: sb("scol" + k, [P, 3, NT], F32) for k in KEYS}
        with ExitStack() as c3:
            f = Env(nc, c3, "m_")
            pos_i = f.sb("posi", [P, NT], I32)
            row = {k: f.sb("row" + k, [P, NT], F32) for k in KEYS}
            lane = {k: f.sb("lane" + k, [P, NT], F32) for k in KEYS}
            OHlane = {k: f.ring("ohlane" + k, 2, [P, P], F32) for k in KEYS}
            cargo = {k: f.ring("cargo" + k, 2, [P, 3, NT], F32) for k in KEYS}
            pmove = {k: f.ps("pmove" + k, [P, 512]) for k in KEYS}
            m_v, m_made, m_moved, m_out = (f.sem(n) for n in ("m_v", "m_made", "m_moved", "m_out"))
            W = Weights(nc, f, g, [(0, io.L0_W1), (1, io.L0_W2)])
            block = c3.enter_context(f.block())
            GR = NT // 2

            @block.sync
            def _(sp):
                W.load(sp)

            @block.scalar
            def _(act):
                for m in range(2):
                    W.split_high(act, m)

            @block.gpsimd
            def _(pool):
                for m in range(2):
                    W.split_low(pool, m)

            @block.vector
            def _(dve):
                n = [0]

                def step(ins):
                    ins.then_inc(m_v, 1)
                    n[0] += 1
                    dve.wait_ge(m_v, n[0])

                for k in KEYS:
                    step(dve.tensor_copy(pos_i[:, :], pos[k][:, :]))
                    step(dve.tensor_scalar(tmp_i[:, :], pos_i[:, :], 7, None, ALU.logical_shift_right))
                    step(dve.tensor_copy(row[k][:, :], tmp_i[:, :]))
                    step(dve.tensor_scalar(tmp_i[:, :], pos_i[:, :], P - 1, None, ALU.bitwise_and))
                    step(dve.tensor_copy(lane[k][:, :], tmp_i[:, :]))

                def make(T):
                    s = T.slot(2)
                    wait(dve, m_moved, T.t - 1)
                    for k in KEYS:
                        one = bass.ds(T.t, 1)
                        dve.tensor_scalar(OHlane[k][s][:, :], iota_f[:, :], lane[k][:, one], None, ALU.is_equal)
                        for q, value in enumerate((key_f[k], other_f[k], deg[k])):
                            ins = dve.tensor_scalar(cargo[k][s][:, q, :], iota_f[:, 0:NT], row[k][:, one],
                                                    value[:, one], ALU.is_equal, ALU.mult)
                    ins.then_inc(m_made, 1)

                def body(i):
                    for u in range(2):
                        at(i, u, 0, 2, NT, make)

                pipeline(dve, GR, 0, 0, body)
                dve.wait_ge(m_moved, NT)
                for k in KEYS:
                    dve.tensor_copy(scol[k][:, :, :], pmove[k][:, 0:3 * NT]).then_inc(m_out, 1)

            @block.tensor
            def _(pe):
                def move(T):
                    s = T.slot(2)
                    pe.wait_ge(m_made, T.t + 1)
                    for k in KEYS:
                        ins = pe.matmul(pmove[k][:, 0:3 * NT], OHlane[k][s][:, :],
                                        cargo[k][s][:, :, :].rearrange("p a t -> p (a t)"),
                                        start=isinstance(T.t, int) and T.t == 0,
                                        stop=isinstance(T.t, int) and T.t == NT - 1)
                    ins.then_inc(m_moved, 1)

                def body(i):
                    for u in range(2):
                        at(i, u, 0, 2, NT, move)

                pipeline(pe, GR, 0, 0, body)

        rowT = {k: sb("rowT" + k, [NT, P + 1], F32) for k in KEYS}
        last = {k: sb("last" + k, [NT, P], F32) for k in KEYS}
        lastc = {k: sb("lastc" + k, [P, NT], F32) for k in KEYS}
        selrow = {k: sb("selrow" + k, [NT, SEL], I16) for k in KEYS}
        tmp_t = sb("tmpt", [NT, P], F32)
        tmp_c = sb("tmpc", [P, NT], F32)
        tmp_c2 = sb("tmpc2", [P, NT], F32)
        empty = sb("empty", [NT, P], F32)
        free = sb("free", [NT, P], F32)
        emptyc = sb("emptyc", [P, NT], F32)
        zrow = sb("zrow", [NT, P], F32)
        qrow = sb("qrow", [NT, P], F32)
        rank_c = {n: sb("rankc" + n, [P, NT], F32) for n in "zq"}
        rank_hi = {n: sb("rankhi" + n, [P, NT], F32) for n in "zq"}
        rank_lo = {n: sb("ranklo" + n, [P, NT], F32) for n in "zq"}
        qi = sb("qi", [NT, P], I32)
        qhi16 = sb("qhi16", [NT, P], I16)
        sentinel = sb("sentinel", [1, 1], F32)
        with ExitStack() as c4:
            f = Env(nc, c4, "o_")
            ptr = {k: f.ps("ptr" + k, [P, 512]) for k in KEYS}
            plast = {k: f.ps("plast" + k, [P, 512]) for k in KEYS}
            pflag, prank = f.ps("pflag", [P, 512]), f.ps("prank", [P, 512])
            psum = f.ps("psum", [P, 512])
            o_v, o_pe, o_st, o_ld, o_sel, o_bc, o_q = (f.sem(n) for n in ("o_v", "o_pe", "o_st", "o_ld", "o_sel", "o_bc", "o_q"))
            block = c4.enter_context(f.block())
            marks = {}

            @block.vector
            def _(dve):
                n = [0]

                def step(ins, mark=None):
                    ins.then_inc(o_v, 1)
                    n[0] += 1
                    if mark:
                        marks[mark] = n[0]
                    dve.wait_ge(o_v, n[0])

                step(dve.memset(sentinel[:, :], -1.0), "sentinel")
                for m, k in enumerate(KEYS):
                    dve.wait_ge(o_pe, m + 1)
                    step(dve.tensor_copy(rowT[k][:, 0:P], ptr[k][0:NT, 0:P]), "rowT" + k)
                for m, k in enumerate(KEYS):
                    dve.wait_ge(o_ld, 16 * (m + 1))
                    step(dve.tensor_tensor(last[k][:, :], rowT[k][:, 0:P], rowT[k][:, 1:P + 1], ALU.not_equal),
                         "last" + k)
                    step(dve.scalar_tensor_tensor(tmp_t[:, :], rowT[k][:, 0:P], 1.0, last[k][:, :],
                                                  ALU.add, ALU.mult))
                    step(dve.memset(selrow[k][:, P + 1:SEL], -1.0))
                    step(dve.tensor_copy(selrow[k][:, P:P + 1], rowT[k][:, P - 1:P]))
                    step(dve.tensor_scalar(selrow[k][:, 0:P], tmp_t[:, :], -1.0, None, ALU.add), "sel" + k)
                for m, k in enumerate(KEYS):
                    dve.wait_ge(o_pe, 3 + m)
                    step(dve.tensor_copy(lastc[k][:, :], plast[k][:, 0:NT]))
                    step(dve.tensor_copy(g.index[k][:, :, 0], scol[k][:, 1, :]))
                    step(dve.tensor_copy(g.index[k][:, :, 1], scol[k][:, 0, :]))
                    step(dve.tensor_scalar(tmp_c[:, :], lastc[k][:, :], float(-NOWHERE), float(NOWHERE),
                                           ALU.mult, ALU.add))
                    step(dve.tensor_tensor(tmp_c2[:, :], scol[k][:, 0, :], lastc[k][:, :], ALU.mult))
                    step(dve.tensor_tensor(g.index[k][:, :, 2], tmp_c[:, :], tmp_c2[:, :], ALU.add))
                    step(dve.tensor_copy(g.keycol[k][:, :], scol[k][:, 0, :]))
                step(dve.tensor_copy(g.degcol[:, :], scol["D"][:, 2, :]))
                step(dve.tensor_scalar(tmp_c[:, :], scol["S"][:, 2, :], 1.0, None, ALU.max))
                step(dve.reciprocal(g.rdeg[:, :], tmp_c[:, :]))
                for m, k in enumerate(KEYS):
                    dve.wait_ge(o_bc, 16 * (m + 1))
                    step(dve.tensor_copy(g.keylast[k][:, :], g.selrows[k][:, :, P]))
                    step(dve.memset(g.keyprev[k][:, 0:1], -2.0))
                    step(dve.tensor_copy(g.keyprev[k][:, 1:NT], g.keylast[k][:, 0:NT - 1]))
                step(dve.tensor_tensor(g.same_last[:, :], g.keylast["S"][:, :], g.keyprev["S"][:, :], ALU.is_equal))
                step(dve.tensor_tensor(tmp_c[:, :], g.keycol["S"][:, :], g.keyprev["S"][:, :], ALU.is_equal))
                step(dve.tensor_tensor(g.takes[:, :], tmp_c[:, :], lastc["S"][:, :], ALU.mult))
                step(dve.tensor_tensor(g.in_last[:, :], g.keycol["S"][:, :], g.keylast["S"][:, :], ALU.is_equal))
                step(dve.tensor_scalar(empty[:, :], count["S"][:, :], 0.0, None, ALU.is_equal), "empty")
                step(dve.tensor_scalar(free[:, :], last["S"][:, :], -1.0, 1.0, ALU.mult, ALU.add), "free")
                for m, (rows, out_row, name) in enumerate(((empty, zrow, "z"), (free, qrow, "q"))):
                    dve.wait_ge(o_pe, 5 + 3 * m)
                    step(dve.tensor_copy(colform[:, :], pflag[:, 0:NT]))
                    if name == "z":
                        step(dve.tensor_copy(emptyc[:, :], colform[:, :]))
                    step(dve.tensor_reduce(total[:, :], rows[:, :], AX.X, ALU.add))
                    step(dve.tensor_scalar(totals[:, :], ones_f[0:NT, :], total[:, 0:1], None, ALU.mult),
                         "totals" + name)
                    dve.wait_ge(o_pe, 6 + 3 * m)
                    step(dve.tensor_copy(out_row[:, :], psum[0:NT, 0:P]), "row" + name)
                    dve.wait_ge(o_pe, 7 + 3 * m)
                    step(dve.tensor_copy(rank_c[name][:, :], prank[:, 0:NT]), "col" + name)
                    step(dve.tensor_copy(tmp_i[:, :], rank_c[name][:, :]))
                    step(dve.tensor_scalar(node_i[:, :], tmp_i[:, :], 7, None, ALU.logical_shift_right))
                    step(dve.tensor_copy(rank_hi[name][:, :], node_i[:, :]))
                    step(dve.tensor_scalar(node_i[:, :], tmp_i[:, :], P - 1, None, ALU.bitwise_and))
                    step(dve.tensor_copy(rank_lo[name][:, :], node_i[:, :]))
                step(dve.tensor_scalar(tmp_c[:, :], emptyc[:, :], 200.0, -200.0, ALU.mult, ALU.add))
                step(dve.tensor_tensor(rank_hi["z"][:, :], rank_hi["z"][:, :], tmp_c[:, :], ALU.add))
                step(dve.tensor_copy(qi[:, :], qrow[:, :]))
                step(dve.tensor_scalar(qi[:, :], qi[:, :], 7, None, ALU.logical_shift_right))
                step(dve.tensor_copy(qhi16[:, :], qi[:, :]), "qhi16")

            @block.tensor
            def _(pe):
                for k in KEYS:
                    pe.transpose(ptr[k][0:NT, 0:P], scol[k][:, 0, :], g.ident[:, :]).then_inc(o_pe, 1)
                for m, k in enumerate(KEYS):
                    pe.wait_ge(o_v, marks["last" + k])
                    pe.transpose(plast[k][:, 0:NT], last[k][:, :], g.ident[0:NT, 0:NT]).then_inc(o_pe, 1)
                for rows, out_row, name, mark in ((empty, zrow, "z", "empty"), (free, qrow, "q", "colz")):
                    pe.wait_ge(o_v, marks["free"])
                    pe.wait_ge(o_v, marks[mark])
                    pe.transpose(pflag[:, 0:NT], rows[:, :], g.ident[0:NT, 0:NT]).then_inc(o_pe, 1)
                    pe.wait_ge(o_v, marks["totals" + name])
                    pe.matmul(psum[0:NT, 0:P], colform[:, :], before_f[:, :], start=True, stop=False)
                    pe.matmul(psum[0:NT, 0:P], before_f[0:NT, 0:NT], totals[:, :], start=False, stop=True)\
                        .then_inc(o_pe, 1)
                    pe.wait_ge(o_v, marks["row" + name])
                    pe.transpose(prank[:, 0:NT], out_row[:, :], g.ident[0:NT, 0:NT]).then_inc(o_pe, 1)

            @block.sync
            def _(sp):
                sp.wait_ge(o_v, marks["sentinel"])
                for k in KEYS:
                    sp.wait_ge(o_v, marks["rowT" + k])
                    sp.dma_start(g.seq[k][0:N].rearrange("(t j) -> t j", j=P), rowT[k][:, 0:P]).then_inc(o_st, 16)
                    sp.dma_start(row_of(g.seq[k][N:N + 1]), sentinel[:, :]).then_inc(o_st, 16)
                sp.wait_ge(o_st, 64)
                for k in KEYS:
                    sp.dma_start(rowT[k][:, P:P + 1], g.seq[k][1:N + 1].rearrange("(t j) -> t j", j=P)[:, P - 1:P],
                                 allow_slow_non_contiguous=True).then_inc(o_ld, 16)
                    sp.wait_ge(o_ld, 16 if k == "D" else 32)
                for m, k in enumerate(KEYS):
                    sp.wait_ge(o_v, marks["sel" + k])
                    sp.dma_start(g.seldram[k], selrow[k][:, :]).then_inc(o_sel, 16)
                    sp.wait_ge(o_sel, 16 * (m + 1))
                    sp.dma_start(g.selrows[k][:, :, :], g.seldram[k].partition_broadcast(P)).then_inc(o_bc, 16)
                    sp.wait_ge(o_bc, 16 * (m + 1))
                sp.dma_start(g.lastdram, last["S"][:, :]).then_inc(o_q, 16)
                sp.wait_ge(o_v, marks["qhi16"])
                sp.dma_start(g.qdram, qhi16[:, :]).then_inc(o_q, 16)
                sp.wait_ge(o_q, 32)

        with ExitStack() as c5:
            f = Env(nc, c5, "e_")
            qrow16 = f.sb("qrow16", [NT, N], I16)
            hot_hi = f.ring("hothi", 2, [P, NT], F32)
            hot_lo = f.ring("hotlo", 2, [P, P], F32)
            listed = f.sb("listed", [NT, P], F32)
            hotT = f.ring("hott", 2, [NT, P], F32)
            hotq = f.ring("hotq", 2, [P, P], F32)
            picked = f.ring("picked", 2, [P, P], F32)
            found = f.sb("found", [P, NT], F32)
            plist = f.ps("plist", [P, 512])
            pl = [f.ps(f"pl{i}", [P, 512]) for i in range(2)]
            e_ld, e_made, e_put, e_list, e_hot, e_look, e_pick, e_red, e_fin = (
                f.sem(n) for n in ("e_ld", "e_made", "e_put", "e_list", "e_hot", "e_look", "e_pick", "e_red", "e_fin"))
            block = c5.enter_context(f.block())
            GR = NT // 2

            @block.sync
            def _(sp):
                sp.dma_start(qrow16[:, :], g.qdram.rearrange("t j -> (t j)").partition_broadcast(NT)).then_inc(e_ld, 16)
                sp.wait_ge(e_ld, 16)

            @block.vector
            def _(dve):
                def make(T):
                    s = T.slot(2)
                    one = bass.ds(T.t, 1)
                    wait(dve, e_put, T.t - 1)
                    dve.tensor_scalar(hot_hi[s][:, :], iota_f[:, 0:NT], rank_hi["z"][:, one], None, ALU.is_equal)
                    dve.tensor_scalar(hot_lo[s][:, :], iota_f[:, :], rank_lo["z"][:, one], node_f[:, one],
                                      ALU.is_equal, ALU.mult).then_inc(e_made, 1)

                def body(i):
                    for u in range(2):
                        at(i, u, 0, 2, NT, make)

                pipeline(dve, GR, 0, 0, body)
                dve.wait_ge(e_put, NT)
                dve.tensor_copy(listed[:, :], plist[0:NT, 0:P]).then_inc(e_list, 1)
                dve.wait_ge(e_ld, 16)

                def hot(T):
                    s = T.slot(2)
                    wait(dve, e_look, T.t - 1)
                    dve.tensor_scalar(hotT[s][:, :], qrow16[:, bass.ds(T.t * P, P)], pidx[0:NT, 0:1], None,
                                      ALU.is_equal).then_inc(e_hot, 1)
                    wait(dve, e_pick, T.t - 1)
                    dve.tensor_scalar(hotq[s][:, :], iota_f[:, :], rank_lo["q"][:, bass.ds(T.t, 1)], None,
                                      ALU.is_equal).then_inc(e_hot, 1)

                def pick(T):
                    s = T.slot(2)
                    dve.wait_ge(e_look, T.t + 1)
                    dve.wait_ge(e_hot, 2 * T.t + 2)
                    wait(dve, e_red, T.t - 1)
                    dve.tensor_tensor(picked[s][:, :], pl[s][:, 0:P], hotq[s][:, :], ALU.mult).then_inc(e_pick, 1)
                    dve.wait_ge(e_pick, T.t + 1)
                    dve.tensor_reduce(found[:, bass.ds(T.t, 1)], picked[s][:, :], AX.X, ALU.add).then_inc(e_red, 1)

                def body2(i):
                    for u in range(2):
                        at(i, u, 1, 2, NT, hot)
                        at(i, u, 0, 2, NT, pick)

                pipeline(dve, GR, 1, 0, body2)
                dve.wait_ge(e_red, NT)
                n = [0]

                def step(ins):
                    ins.then_inc(e_fin, 1)
                    n[0] += 1
                    dve.wait_ge(e_fin, n[0])

                step(dve.tensor_tensor(tmp_c[:, :], scol["S"][:, 0, :], found[:, :], ALU.subtract))
                step(dve.tensor_tensor(tmp_c[:, :], tmp_c[:, :], lastc["S"][:, :], ALU.mult))
                step(dve.tensor_tensor(g.index["S"][:, :, 2], tmp_c[:, :], found[:, :], ALU.add))

            @block.tensor
            def _(pe):
                def put(T):
                    s = T.slot(2)
                    pe.wait_ge(e_made, T.t + 1)
                    pe.matmul(plist[0:NT, 0:P], hot_hi[s][:, :], hot_lo[s][:, :],
                              start=isinstance(T.t, int) and T.t == 0,
                              stop=isinstance(T.t, int) and T.t == NT - 1).then_inc(e_put, 1)

                def look(T):
                    s = T.slot(2)
                    pe.wait_ge(e_hot, 2 * T.t + 1)
                    wait(pe, e_pick, T.t - 1)
                    pe.matmul(pl[s][:, 0:P], hotT[s][:, :], listed[:, :], start=True, stop=True).then_inc(e_look, 1)

                def body(i):
                    for u in range(2):
                        at(i, u, 0, 2, NT, put)

                def body2(i):
                    for u in range(2):
                        at(i, u, 0, 2, NT, look)

                pipeline(pe, GR, 0, 0, body)
                pe.wait_ge(e_list, 1)
                pipeline(pe, GR, 0, 0, body2)



class Weights:

    def __init__(self, nc, e, g, sources):
        self.nc, self.g, self.sources = nc, g, sources
        self.stage = e.sb("wstage", [P, C, D], F32)
        self.loaded, self.high, self.low = e.sem("w_loaded"), e.sem("w_high"), e.sem("w_low")

    def load(self, sp):
        for n in range(len(self.sources)):
            self.load_one(sp, n)

    def load_one(self, sp, n):
        wait(sp, self.low, n)
        sp.dma_start(self.stage[:, :, :], self.sources[n][1].rearrange("(c p) n -> p c n", p=P))\
            .then_inc(self.loaded, 16)

    def split_high(self, act, n):
        slot = self.sources[n][0]
        act.wait_ge(self.loaded, 16 * (n + 1))
        self.nc.scalar.copy(self.g.Whi[slot][:, :, :], self.stage[:, :, :]).then_inc(self.high, 1)

    def split_low(self, pool, n):
        slot = self.sources[n][0]
        pool.wait_ge(self.high, n + 1)
        pool.tensor_tensor(self.g.Wlo[slot][:, :, :], self.stage[:, :, :],
                           self.g.Whi[slot][:, :, :].bitcast(F32), ALU.subtract).then_inc(self.low, 1)


def selection(dve, g, k, T, sel, mask, sel_sem, mask_sem, sel_free, mask_done):
    s = T.slot(2)
    rows = g.selrows[k][:, bass.ds(T.t, 1), :]
    wait(dve, sel_free, T.t - 1)
    dve.tensor_scalar(sel[s][:, :], rows, g.keycol[k][:, bass.ds(T.t, 1)], None, ALU.is_equal).then_inc(sel_sem, 1)
    if mask is not None:
        wait(dve, mask_done, T.t - 1)
        dve.tensor_scalar(mask[s][:, :], rows, g.keyprev[k][:, bass.ds(T.t, 1)], None, ALU.is_equal)\
            .then_inc(mask_sem, 1)


def chunk(psum, c, cols):
    return psum[:, c // 2, (c % 2) * SEL:(c % 2) * SEL + cols]


def all_chunks(psum, first, cols):
    return psum[:, :, 0:2 * SEL].rearrange("p b (h w) -> p b h w", w=SEL)[:, :, :, first:first + cols]


def chunks_of(t):
    return t.rearrange("p (b h) n -> p b h n", b=2)


def carry_in(dve, T, psum, mask, carry, summed, mask_sem, done, copied):
    s, before = T.slot(2), (T.j - 1) % 2
    dve.wait_ge(summed, T.t + 1)
    dve.wait_ge(mask_sem, T.t + 1)
    wait(dve, copied, T.t)
    for c in range(C):
        ins = dve.scalar_tensor_tensor(chunk(psum[s], c, SEL), mask[s][:, :], carry[before][:, c:c + 1],
                                       chunk(psum[s], c, SEL), ALU.mult, ALU.add)
    ins.then_inc(done, 1)
    dve.wait_ge(done, T.t + 1)
    dve.tensor_copy(carry[s][:, :], all_chunks(psum[s], P, 1)).then_inc(copied, 1)


def product(pe, out, hi, lo, whi, wlo, start, stop):
    for c in range(C):
        ins = pe.matmul(out, hi[:, c, :], whi[:, c, :], start=start and c == 0, stop=False)
        ins = pe.matmul(out, hi[:, c, :], wlo[:, c, :], start=False, stop=False)
        ins = pe.matmul(out, lo[:, c, :], whi[:, c, :], start=False, stop=stop and c == C - 1)
    return ins


def indices(pool, g, k, T, col, n, tick, copied):
    s = T.slot(len(col))
    pool.sem_inc(tick, 1)
    pool.tensor_copy(col[s][:, 0:n], g.index[k][:, bass.ds(T.t, 1), 0:n]).then_inc(copied, 1)


def fetch(pool, out, table, index):
    return pool.indirect_dma_start(out, None, table, bass.IndirectOffsetOnAxis(ap=index, axis=0))


def put_rows(pool, table, index, rows, last_row):
    return pool.indirect_dma_start(table, bass.IndirectOffsetOnAxis(ap=index, axis=0), rows, None,
                                   bounds_check=last_row, oob_is_err=False)


class Norm:

    def __init__(self, e, name):
        self.stats = e.ring(name + "stats", 2, [P, 6], F32)
        self.mean_var = e.ring(name + "mv", 2, [P, 2], F32)
        self.var = e.ring(name + "var", 2, [P, 1], F32)
        self.s_stats, self.s_mean, self.s_var, self.s_scale, self.s_bias = (
            e.sem(name + n) for n in ("_stats", "_mean", "_var", "_scale", "_bias"))

    def statistics(self, dve, T, rows):
        dve.bn_stats(self.stats[T.slot(2)][:, :], rows).then_inc(self.s_stats, 1)

    def finish(self, dve, tick, T):
        s = T.slot(2)
        dve.wait_ge(self.s_stats, T.t + 1)
        dve.sem_inc(tick, 1)
        dve.bn_aggr(self.mean_var[s][:, :], self.stats[s][:, :]).then_inc(self.s_mean, 1)
        dve.wait_ge(self.s_mean, T.t + 1)
        wait(dve, self.s_scale, T.t - 1)
        dve.tensor_scalar(self.var[s][:, :], self.mean_var[s][:, 1:2], LN_EPS, None, ALU.add).then_inc(self.s_var, 1)

    def make_scale(self, pool, T, neg_half, scale):
        pool.wait_ge(self.s_var, T.t + 1)
        pool.tensor_tensor(scale, self.var[T.slot(2)][:, :], neg_half[:, :], ALU.pow).then_inc(self.s_scale, 1)

    def make_bias(self, pool, tick, T, scale, bias):
        pool.wait_ge(self.s_scale, T.t + 1)
        pool.sem_inc(tick, 1)
        pool.tensor_scalar(bias, self.mean_var[T.slot(2)][:, 0:1], scale, -1.0, ALU.mult, ALU.mult)\
            .then_inc(self.s_bias, 1)



def layer0(nc, io, g, second):
    NT, N = g.NT, g.N
    U = 4
    GR = NT // U
    with ExitStack() as ctx:
        e = Env(nc, ctx, "b_" if second else "a_")
        src, slot, bias = (g.h1, 1, io.L0_b2) if second else (g.h0, 0, io.L0_b1)
        brow = e.sb("brow", [P, D], F32)
        neg_half = e.sb("neghalf", [P, 1], F32)
        col, colx = e.ring("col", U, [P, 3], I32), e.ring("colx", U, [P, 3], I32)
        G = e.ring("G", U, [P, D], F32)
        Ghi, Glo = e.ring("Ghi", 2, [P, D], F32R), e.ring("Glo", 2, [P, D], F32R)
        sel, mask = e.ring("sel", 2, [P, SEL], F32R), e.ring("mask", 2, [P, SEL], F32)
        carry = e.ring("carry", 2, [P, C], F32)
        Thi, Tlo = e.ring("Thi", 2, [P, C, P], F32R), e.ring("Tlo", 2, [P, C, P], F32R)
        rows = e.ring("rows", 2, [P, EXT if second else D], F32)
        xr = e.ring("xr", U, [P, D], F32) if second else None
        ln = Norm(e, "ln") if second else None
        W = None if second else Weights(nc, e, g, [(2, io.L1_W1), (3, io.L1_W2)])
        psum_t = [e.ps(f"pt{i}", [P, 2, 512]) for i in range(2)]
        psum_o = [e.ps(f"po{i}", [P, D]) for i in range(2)]

        s_brow, s_const = e.sem("s_brow"), e.sem("s_const")
        s_col, s_colx = e.sem("s_col"), e.sem("s_colx")
        s_G, s_x, s_put = e.sems("s_G", U), e.sems("s_x", U), e.sems("s_put", U)
        s_Ghi, s_Glo = e.sem("s_Ghi"), e.sem("s_Glo")
        s_sel, s_mask = e.sem("s_sel"), e.sem("s_mask")
        s_summed, s_carried, s_copied = e.sem("s_summed"), e.sem("s_carried"), e.sem("s_copied")
        s_Thi, s_Tlo = e.sem("s_Thi"), e.sem("s_Tlo")
        s_prod, s_biased, s_rows = e.sem("s_prod"), e.sem("s_biased"), e.sem("s_rows")
        tick = e.sem("tick")
        block = ctx.enter_context(e.block())

        @block.sync
        def _(sp):
            sp.dma_start(brow[:, :], bias.partition_broadcast(P)).then_inc(s_brow, 16)
            if W:
                W.load(sp)
            sp.wait_ge(s_brow, 16)

        @block.gpsimd
        def _(pool):
            def start_fetch(T):
                s = T.slot(U)
                wait(pool, s_Glo, T.t - 3)
                indices(pool, g, "D", T, col, 1, tick, s_col)
                pool.wait_ge(s_col, T.t + 1)
                pool.sem_inc(tick, 1)
                fetch(pool, G[s][:, :], src, col[s][:, 0:1]).then_inc(s_G[s], 16)

            def low(T):
                s = T.slot(2)
                wait(pool, s_summed, T.t - 1)
                pool.wait_ge(s_Ghi, T.t + 1)
                pool.tensor_tensor(Glo[s][:, :], G[T.slot(U)][:, :], Ghi[s][:, :].bitcast(F32), ALU.subtract)\
                    .then_inc(s_Glo, 1)

            def residual(T):
                s = T.slot(U)
                wait(pool, s_rows, T.t - 3)
                wait(pool, s_put[s], 16 * T.use(U))
                indices(pool, g, "D", T, colx, 3, tick, s_colx)
                if second:
                    pool.wait_ge(s_colx, T.t + 1)
                    pool.sem_inc(tick, 1)
                    fetch(pool, xr[s][:, :], io.x, colx[s][:, 1:2]).then_inc(s_x[s], 16)

            def store(T):
                s = T.slot(U)
                if second:
                    row = rows[T.slot(2)]
                    ln.make_scale(pool, T, neg_half, row[:, SCALE:SCALE + 1])
                    ln.make_bias(pool, tick, T, row[:, SCALE:SCALE + 1], row[:, BIAS:BIAS + 1])
                pool.wait_ge(s_colx, T.t + 1)
                pool.wait_ge(ln.s_bias if second else s_rows, T.t + 1)
                pool.sem_inc(tick, 1)
                put_rows(pool, g.xs[0] if second else g.h1, colx[s][:, 2:3], rows[T.slot(2)][:, :], N - 1)\
                    .then_inc(s_put[s], 16)

            def body(i):
                for u in range(U):
                    at(i, u, -2, U, NT, store)
                    at(i, u, 6, U, NT, start_fetch)
                    at(i, u, 1, U, NT, residual)
                    at(i, u, 3, U, NT, low)

            pool.memset(neg_half[:, :], -0.5).then_inc(s_const, 1)
            for s in range(2):
                pool.memset(carry[s][:, :], 0.0).then_inc(s_const, 1)
                if second:
                    pool.memset(rows[s][:, BIAS + 1:EXT], 0.0).then_inc(s_const, 1)
            pool.wait_ge(s_const, 5 if second else 3)
            pipeline(pool, GR, 2, 1, body, between=W and (lambda n: W.split_low(pool, n)))
            for s in range(U):
                pool.wait_ge(s_put[s], 16 * GR)

        @block.scalar
        def _(act):
            def high(T):
                s = T.slot(2)
                act.wait_ge(s_G[T.slot(U)], 16 * (T.use(U) + 1))
                wait(act, s_summed, T.t - 1)
                nc.scalar.copy(Ghi[s][:, :], G[T.slot(U)][:, :]).then_inc(s_Ghi, 1)

            def high_sum(T):
                s = T.slot(2)
                act.wait_ge(s_copied, T.t + 1)
                wait(act, s_prod, T.t - 1)
                nc.scalar.copy(chunks_of(Thi[s]), all_chunks(psum_t[s], 0, P)).then_inc(s_Thi, 1)

            def relu(T):
                s, store_before = T.slot(2), (T.j - 2) % U
                act.wait_ge(s_biased, T.t + 1)
                wait(act, s_put[store_before], 16 * (T.k + 1 if T.j >= 2 else T.k))
                nc.scalar.activation(rows[s][:, :], psum_o[s][:, :], ACT.Relu).then_inc(s_rows, 1)

            def body(i):
                for u in range(U):
                    if not second:
                        at(i, u, -1, U, NT, relu)
                    at(i, u, 1, U, NT, high_sum)
                    at(i, u, 3, U, NT, high)

            pipeline(act, GR, 1, 1, body, between=W and (lambda n: W.split_high(act, n)))

        @block.vector
        def _(dve):
            def select(T):
                selection(dve, g, "D", T, sel, mask, s_sel, s_mask, s_summed, s_carried)

            def carried(T):
                carry_in(dve, T, psum_t, mask, carry, s_summed, s_mask, s_carried, s_copied)

            def low_sum(T):
                s = T.slot(2)
                dve.wait_ge(s_Thi, T.t + 1)
                dve.tensor_tensor(chunks_of(Tlo[s]), all_chunks(psum_t[s], 0, P), chunks_of(Thi[s]).bitcast(F32),
                                  ALU.subtract).then_inc(s_Tlo, 1)

            def add_bias(T):
                s = T.slot(2)
                dve.wait_ge(s_prod, T.t + 1)
                dve.scalar_tensor_tensor(psum_o[s][:, :], brow[:, :], g.degcol[:, bass.ds(T.t, 1)], psum_o[s][:, :],
                                         ALU.mult, ALU.add).then_inc(s_biased, 1)

            def add_x(T):
                s, store_before = T.slot(2), (T.j - 2) % U
                dve.wait_ge(s_biased, T.t + 1)
                dve.wait_ge(s_x[T.slot(U)], 16 * (T.use(U) + 1))
                wait(dve, s_put[store_before], 16 * (T.k + 1 if T.j >= 2 else T.k))
                dve.scalar_tensor_tensor(rows[s][:, 0:D], psum_o[s][:, :], 0.0, xr[T.slot(U)][:, :],
                                         ALU.max, ALU.add).then_inc(s_rows, 1)

            def norm_rows(T):
                dve.wait_ge(s_rows, T.t + 1)
                ln.statistics(dve, T, rows[T.slot(2)][:, 0:D])

            def finish_rows(T):
                wait(dve, ln.s_bias, T.t - 1)
                ln.finish(dve, tick, T)

            def body(i):
                for u in range(U):
                    at(i, u, -1, U, NT, add_bias)
                    at(i, u, 1, U, NT, carried)
                    if second:
                        at(i, u, -1, U, NT, add_x)
                    at(i, u, 1, U, NT, low_sum)
                    if second:
                        at(i, u, -1, U, NT, norm_rows)
                    at(i, u, 3, U, NT, select)
                    if second:
                        at(i, u, -1, U, NT, finish_rows)

            dve.wait_ge(s_brow, 16)
            dve.wait_ge(s_const, 5 if second else 3)
            pipeline(dve, GR, 1, 1, body)

        @block.tensor
        def _(pe):
            def sum_edges(T):
                s = T.slot(2)
                pe.wait_ge(s_sel, T.t + 1)
                pe.wait_ge(s_Glo, T.t + 1)
                wait(pe, s_Tlo, T.t - 1)
                for c in range(C):
                    pe.matmul(chunk(psum_t[s], c, SEL), Ghi[s][:, c * P:(c + 1) * P], sel[s][:, :],
                              start=True, stop=False)
                    ins = pe.matmul(chunk(psum_t[s], c, SEL), Glo[s][:, c * P:(c + 1) * P], sel[s][:, :],
                                    start=False, stop=True)
                ins.then_inc(s_summed, 1)

            def multiply(T):
                s = T.slot(2)
                pe.wait_ge(s_Tlo, T.t + 1)
                wait(pe, s_rows, T.t - 1)
                product(pe, psum_o[s][:, :], Thi[s], Tlo[s], g.Whi[slot], g.Wlo[slot], True, True)\
                    .then_inc(s_prod, 1)

            def body(i):
                for u in range(U):
                    at(i, u, 1, U, NT, sum_edges)
                    at(i, u, 0, U, NT, multiply)

            pipeline(pe, GR, 1, 0, body)



def layer1(nc, io, g):
    NT, N = g.NT, g.N
    U = 4
    GR = NT // U
    PAIRS = NT // 2
    RX = 8
    with ExitStack() as ctx:
        e = Env(nc, ctx, "c_")
        src, out = g.xs[0], g.xs[1]
        W = Weights(nc, e, g, [(0, io.L2_Wn), (1, io.L2_Ws)])
        gamma, beta = e.sb("gamma", [P, D], F32), e.sb("beta", [P, D], F32)
        neg_half = e.sb("neghalf", [P, 1], F32)
        b1col = e.sb("b1col", [P, C], F32)
        b2f, b2hi, b2lo = e.sb("b2f", [1, D], F32), e.sb("b2hi", [1, D], F32R), e.sb("b2lo", [1, D], F32R)
        ones1 = e.sb("ones1", [1, P], F32R)
        ones_f = e.sb("onesf", [1, P], F32)
        eps1 = e.sb("eps1", [P, 1], F32)
        eye = e.sb("eye", [P, P], F32)
        col, colx = e.ring("col", U, [P, 3], I32), e.ring("colx", 2, [P, 3], I32)
        G, X = e.ring("G", U, [P, EXT], F32), e.ring("X", U, [P, EXT], F32)
        H = e.ring("H", 2, [P, D], F32)
        XB = e.sb("XB", [P, RX, D], F32)
        Ghi, Glo = e.ring("Ghi", 2, [P, D], F32R), e.ring("Glo", 2, [P, D], F32R)
        sel, mask = e.ring("sel", 2, [P, SEL], F32R), e.ring("mask", 2, [P, SEL], F32)
        carry = e.ring("carry", 2, [P, C], F32)
        Zhi, Zlo = e.sb("Zhi", [P, C, 2 * P], F32R), e.sb("Zlo", [P, C, 2 * P], F32R)
        Uhi, Ulo = e.ring("Uhi", 2, [P, C, 2 * P], F32R), e.ring("Ulo", 2, [P, C, 2 * P], F32R)
        rows = e.ring("rows", 2, [P, EXT], F32)
        ylen = e.ring("ylen", 2, [P, 1], F32)
        ln_y, ln_x = Norm(e, "lny"), Norm(e, "lnx")
        psum_t = [e.ps(f"pt{i}", [P, 2, 512]) for i in range(2)]
        psum_u = e.ps("pu", [P, C, 2 * P])
        psum_o = [e.ps(f"po{i}", [P, D]) for i in range(2)]

        s_load, s_const, s_prep = e.sem("s_load"), e.sem("s_const"), e.sem("s_prep")
        s_col, s_colx = e.sem("s_col"), e.sem("s_colx")
        s_G, s_X, s_put = e.sems("s_G", U), e.sems("s_X", U), e.sems("s_put", 2)
        s_Gn, s_H, s_Ghi, s_Glo, s_XB = (e.sem(n) for n in ("s_Gn", "s_H", "s_Ghi", "s_Glo", "s_XB"))
        s_sel, s_mask = e.sem("s_sel"), e.sem("s_mask")
        s_summed, s_carried, s_copied = e.sem("s_summed"), e.sem("s_carried"), e.sem("s_copied")
        s_Zhi, s_Zlo = e.sem("s_Zhi"), e.sem("s_Zlo")
        s_u, s_relu, s_Uhi, s_Ulo = (e.sem(n) for n in ("s_u", "s_relu", "s_Uhi", "s_Ulo"))
        s_prod, s_cent, s_rows = e.sem("s_prod"), e.sem("s_cent"), e.sem("s_rows")
        tick = e.sem("tick")
        block = ctx.enter_context(e.block())

        @block.sync
        def _(sp):
            sp.dma_start(gamma[:, :], io.L1_gamma.partition_broadcast(P)).then_inc(s_load, 16)
            sp.dma_start(beta[:, :], io.L1_beta.partition_broadcast(P)).then_inc(s_load, 16)
            sp.dma_start(b1col[:, :], io.L1_b1col).then_inc(s_load, 16)
            sp.dma_start(b2f[:, :], row_of(io.L1_b2)).then_inc(s_load, 16)
            sp.dma_start(eps1[:, :], io.eps.partition_broadcast(P)).then_inc(s_load, 16)
            W.load(sp)
            sp.wait_ge(s_load, 80)

        @block.gpsimd
        def _(pool):
            def start_fetch(T):
                s = T.slot(U)
                wait(pool, s_Glo, T.t - 3)
                wait(pool, s_H, T.t - 3)
                wait(pool, s_XB, T.t - 3)
                indices(pool, g, "S", T, col, 3, tick, s_col)
                pool.wait_ge(s_col, T.t + 1)
                pool.sem_inc(tick, 1)
                fetch(pool, G[s][:, :], src, col[s][:, 0:1]).then_inc(s_G[s], 16)
                fetch(pool, X[s][:, :], src, col[s][:, 2:3]).then_inc(s_X[s], 16)

            def keep_x(T):
                s = T.slot(U)
                pool.wait_ge(s_X[s], 16 * (T.use(U) + 1))
                wait(pool, s_rows, T.t - RX + 1)
                pool.sem_inc(tick, 1)
                pool.tensor_tensor(XB[:, bass.ds(T.t % RX, 1), :], X[s][:, 0:D], beta[:, :], ALU.add)\
                    .then_inc(s_XB, 1)

            def low(T):
                s = T.slot(2)
                wait(pool, s_summed, T.t - 1)
                pool.wait_ge(s_Ghi, T.t + 1)
                pool.tensor_tensor(Glo[s][:, :], G[T.slot(U)][:, 0:D], Ghi[s][:, :].bitcast(F32), ALU.subtract)\
                    .then_inc(s_Glo, 1)

            def length_y(T):
                wait(pool, s_rows, T.t - 1)
                ln_y.make_scale(pool, T, neg_half, ylen[T.slot(2)][:, :])

            def store(T):
                s = T.slot(2)
                wait(pool, s_put[s], 16 * T.use(2))
                ln_x.make_scale(pool, T, neg_half, rows[s][:, SCALE:SCALE + 1])
                indices(pool, g, "S", T, colx, 3, tick, s_colx)
                ln_x.make_bias(pool, tick, T, rows[s][:, SCALE:SCALE + 1], rows[s][:, BIAS:BIAS + 1])
                pool.wait_ge(s_colx, T.t + 1)
                pool.wait_ge(ln_x.s_bias, T.t + 1)
                pool.sem_inc(tick, 1)
                put_rows(pool, out, colx[s][:, 2:3], rows[s][:, :], N - 1).then_inc(s_put[s], 16)

            def body(i):
                for pair in (0, 2):
                    at(i, pair, 4, U, NT, keep_x)
                    for u in (pair, pair + 1):
                        at(i, u, -2, U, NT, length_y)
                    at(i, pair + 1, 4, U, NT, keep_x)
                    at(i, pair, 8, U, NT, start_fetch)
                    for u in (pair, pair + 1):
                        at(i, u, -2, U, NT, store)
                    at(i, pair + 1, 8, U, NT, start_fetch)
                    for u in (pair, pair + 1):
                        at(i, u, 6, U, NT, low)

            pool.memset(ones_f[:, :], 1.0).then_inc(s_const, 1)
            pool.memset(neg_half[:, :], -0.5).then_inc(s_const, 1)
            for s in range(2):
                pool.memset(carry[s][:, :], 0.0).then_inc(s_const, 1)
                pool.memset(rows[s][:, BIAS + 1:EXT], 0.0).then_inc(s_const, 1)
            pool.wait_ge(s_const, 6)
            pool.wait_ge(s_load, 80)
            pipeline(pool, GR, 2, 1, body, ahead=2, between=lambda n: W.split_low(pool, n))
            for s in range(2):
                pool.wait_ge(s_put[s], 16 * (NT // 2))

        @block.scalar
        def _(act):
            def norm_in(T):
                s = T.slot(U)
                act.wait_ge(s_G[s], 16 * (T.use(U) + 1))
                nc.scalar.activation(G[s][:, 0:D], G[s][:, 0:D], ACT.Relu, bias=G[s][:, BIAS:BIAS + 1],
                                     scale=G[s][:, SCALE:SCALE + 1]).then_inc(s_Gn, 1)
                act.wait_ge(s_X[s], 16 * (T.use(U) + 1))
                wait(act, s_summed, T.t - 1)
                nc.scalar.activation(H[T.slot(2)][:, :], X[s][:, 0:D], ACT.Relu, bias=X[s][:, BIAS:BIAS + 1],
                                     scale=X[s][:, SCALE:SCALE + 1]).then_inc(s_H, 1)
                act.wait_ge(s_Gn, T.t + 1)
                nc.scalar.copy(Ghi[T.slot(2)][:, :], G[s][:, 0:D]).then_inc(s_Ghi, 1)

            def high_sum(T):
                s = T.slot(2)
                act.wait_ge(s_copied, T.t + 1)
                wait(act, s_u, T.use(2))
                nc.scalar.copy(chunks_of(Zhi[:, :, s * P:(s + 1) * P]), all_chunks(psum_t[s], 0, P))\
                    .then_inc(s_Zhi, 1)

            def relu(T):
                act.wait_ge(s_u, T.t + 1)
                for c in range(C):
                    ins = nc.scalar.activation(psum_u[:, c, :], psum_u[:, c, :], ACT.Relu, bias=b1col[:, c:c + 1])
                ins.then_inc(s_relu, 1)
                act.wait_ge(s_relu, T.t + 1)
                wait(act, s_prod, 2 * (T.t - 1))
                nc.scalar.copy(Uhi[T.slot(2)][:, :, :], psum_u[:, :, :]).then_inc(s_Uhi, 1)

            def body(i):
                for pair in (0, 2):
                    at(i, pair // 2, 1, 2, PAIRS, relu)
                    for u in (pair, pair + 1):
                        at(i, u, 4, U, NT, high_sum)
                    for u in (pair, pair + 1):
                        at(i, u, 6, U, NT, norm_in)

            act.wait_ge(s_load, 80)
            nc.scalar.copy(b2hi[:, :], b2f[:, :]).then_inc(s_prep, 1)
            act.wait_ge(s_const, 1)
            nc.scalar.copy(ones1[:, :], ones_f[:, :]).then_inc(s_prep, 1)
            pipeline(act, GR, 2, 0, body, between=lambda n: W.split_high(act, n))

        @block.vector
        def _(dve):
            def low_u(T):
                dve.wait_ge(s_Uhi, T.t + 1)
                dve.tensor_tensor(Ulo[T.slot(2)][:, :, :], psum_u[:, :, :], Uhi[T.slot(2)][:, :, :].bitcast(F32),
                                  ALU.subtract).then_inc(s_Ulo, 1)

            def carried(T):
                carry_in(dve, T, psum_t, mask, carry, s_summed, s_mask, s_carried, s_copied)

            def low_sum(T):
                s = T.slot(2)
                dve.wait_ge(s_Zhi, T.t + 1)
                half = slice(s * P, (s + 1) * P)
                dve.tensor_tensor(chunks_of(Zlo[:, :, half]), all_chunks(psum_t[s], 0, P),
                                  chunks_of(Zhi[:, :, half]).bitcast(F32), ALU.subtract).then_inc(s_Zlo, 1)

            def select(T):
                selection(dve, g, "S", T, sel, mask, s_sel, s_mask, s_summed, s_carried)

            def norm_y(T):
                dve.wait_ge(s_prod, T.t + 1)
                ln_y.statistics(dve, T, psum_o[T.slot(2)][:, :])

            def center(T):
                s = T.slot(2)
                ln_y.finish(dve, tick, T)
                dve.scalar_tensor_tensor(psum_o[s][:, :], psum_o[s][:, :], ln_y.mean_var[s][:, 0:1], gamma[:, :],
                                         ALU.subtract, ALU.mult).then_inc(s_cent, 1)

            def new_rows(T):
                s = T.slot(2)
                dve.wait_ge(s_cent, T.t + 1)
                dve.wait_ge(ln_y.s_scale, T.t + 1)
                dve.wait_ge(s_XB, T.t + 1)
                wait(dve, s_put[s], 16 * T.use(2))
                dve.scalar_tensor_tensor(rows[s][:, 0:D], psum_o[s][:, :], ylen[s][:, 0:1],
                                         XB[:, bass.ds(T.t % RX, 1), :], ALU.mult, ALU.add).then_inc(s_rows, 1)

            def norm_rows(T):
                dve.wait_ge(s_rows, T.t + 1)
                ln_x.statistics(dve, T, rows[T.slot(2)][:, 0:D])

            def finish_rows(T):
                wait(dve, ln_x.s_bias, T.t - 1)
                ln_x.finish(dve, tick, T)

            def body(i):
                for pair in (0, 2):
                    for stage in (norm_y, center, new_rows, norm_rows, finish_rows):
                        for u in (pair, pair + 1):
                            at(i, u, -2, U, NT, stage)
                    at(i, pair, 4, U, NT, carried)
                    at(i, pair // 2, 1, 2, PAIRS, low_u)
                    at(i, pair, 4, U, NT, low_sum)
                    at(i, pair + 1, 4, U, NT, carried)
                    at(i, pair + 1, 4, U, NT, low_sum)
                    for u in (pair, pair + 1):
                        at(i, u, 6, U, NT, select)

            dve.wait_ge(s_load, 80)
            dve.wait_ge(s_const, 6)
            dve.wait_ge(s_prep, 1)
            dve.tensor_tensor(b2lo[:, :], b2f[:, :], b2hi[:, :].bitcast(F32), ALU.subtract).then_inc(s_prep, 1)
            dve.tensor_scalar(eps1[:, :], eps1[:, :], 1.0, None, ALU.add).then_inc(s_prep, 1)
            dve.wait_ge(s_prep, 4)
            dve.tensor_scalar(eye[:, :], g.ident[:, :], eps1[:, 0:1], None, ALU.mult).then_inc(s_prep, 1)
            pipeline(dve, GR, 2, 1, body)

        @block.tensor
        def _(pe):
            def sum_edges(T):
                s = T.slot(2)
                pe.wait_ge(s_sel, T.t + 1)
                pe.wait_ge(s_Glo, T.t + 1)
                pe.wait_ge(s_H, T.t + 1)
                wait(pe, s_Zlo, T.t - 1)
                for c in range(C):
                    cols = slice(c * P, (c + 1) * P)
                    pe.matmul(chunk(psum_t[s], c, SEL), Ghi[s][:, cols], sel[s][:, :], start=True, stop=False)
                    pe.matmul(chunk(psum_t[s], c, SEL), Glo[s][:, cols], sel[s][:, :], start=False, stop=False)
                    ins = pe.matmul(chunk(psum_t[s], c, P), H[s][:, cols], eye[:, :], start=False, stop=True)
                ins.then_inc(s_summed, 1)

            def first(T):
                pe.wait_ge(s_Zlo, 2 * T.t + 2)
                wait(pe, s_Ulo, T.t)
                for o in range(C):
                    cols = slice(o * P, (o + 1) * P)
                    for c in range(C):
                        pe.matmul(psum_u[:, o, :], g.Whi[2][:, c, cols], Zhi[:, c, :], start=c == 0, stop=False)
                        pe.matmul(psum_u[:, o, :], g.Whi[2][:, c, cols], Zlo[:, c, :], start=False, stop=False)
                        ins = pe.matmul(psum_u[:, o, :], g.Wlo[2][:, c, cols], Zhi[:, c, :], start=False,
                                        stop=c == C - 1)
                ins.then_inc(s_u, 1)

            def second(T):
                s, pair = T.slot(2), T.j // 2
                pe.wait_ge(s_Ulo, T.use(2) + 1)
                wait(pe, s_rows, T.t - 1)
                half = slice(s * P, (s + 1) * P)
                pe.matmul(psum_o[s][:, :], ones1[:, :], b2hi[:, :], start=True, stop=False)
                pe.matmul(psum_o[s][:, :], ones1[:, :], b2lo[:, :], start=False, stop=False)
                product(pe, psum_o[s][:, :], Uhi[pair][:, :, half], Ulo[pair][:, :, half], g.Whi[3], g.Wlo[3],
                        False, True).then_inc(s_prod, 1)

            def body(i):
                for pair in (0, 2):
                    at(i, pair // 2, 1, 2, PAIRS, first)
                    for u in (pair, pair + 1):
                        at(i, u, 4, U, NT, sum_edges)
                    for u in (pair, pair + 1):
                        at(i, u, 0, U, NT, second)

            pe.wait_ge(s_prep, 5)
            pipeline(pe, GR, 2, 0, body)



def layer2(nc, io, g):
    NT, N = g.NT, g.N
    U = 4
    GR = NT // U
    with ExitStack() as ctx:
        e = Env(nc, ctx, "d_")
        src, out = g.xs[1], g.xs[2]
        W = Weights(nc, e, g, [(2, io.L3_W[0:D, :]), (3, io.L3_W[D:2 * D, :])])
        gamma, beta = e.sb("gamma", [P, D], F32), e.sb("beta", [P, D], F32)
        neg_half = e.sb("neghalf", [P, 1], F32)
        bf, bhi = e.sb("bf", [4, D], F32), e.sb("bhi", [4, D], F32R)
        blo = e.sb("blo", [4, D], F32R)
        has = e.ring("has", 2, [2, P], F32R)
        ones_f = e.sb("onesf", [2, P], F32)
        col, colx = e.ring("col", U, [P, 3], I32), e.ring("colx", 2, [P, 3], I32)
        G, X = e.ring("G", U, [P, EXT], F32), e.ring("X", U, [P, EXT], F32)
        gsb = e.ring("gsb", 2, [P, 2], F32)
        H, XB = e.ring("H", 4, [P, D], F32), e.ring("XB", 4, [P, D], F32)
        Ghi, Glo = e.ring("Ghi", 2, [P, D], F32R), e.ring("Glo", 2, [P, D], F32R)
        sel, mask = e.ring("sel", 2, [P, SEL], F32R), e.ring("mask", 2, [P, SEL], F32)
        carry = e.ring("carry", 2, [P, C], F32)
        Thi, Tlo = e.ring("Thi", 2, [P, C, P], F32R), e.ring("Tlo", 2, [P, C, P], F32R)
        Hhi, Hlo = e.ring("Hhi", 2, [P, C, P], F32R), e.ring("Hlo", 2, [P, C, P], F32R)
        rows = e.ring("rows", 2, [P, EXT], F32)
        ylen = e.ring("ylen", 2, [P, 1], F32)
        ln_y, ln_x = Norm(e, "lny"), Norm(e, "lnx")
        psum_t = [e.ps(f"pt{i}", [P, 2, 512]) for i in range(2)]
        psum_h = [e.ps(f"ph{i}", [P, C, P]) for i in range(2)]
        psum_o = [e.ps(f"po{i}", [P, D]) for i in range(2)]

        s_load, s_const, s_prep = e.sem("s_load"), e.sem("s_const"), e.sem("s_prep")
        s_ones, s_has = e.sem("s_ones"), e.sems("s_has", 2)
        s_col, s_colx = e.sem("s_col"), e.sem("s_colx")
        s_G, s_X, s_put = e.sems("s_G", U), e.sems("s_X", U), e.sems("s_put", 2)
        s_gsb, s_Gn, s_H, s_Ghi, s_Glo, s_XB = (
            e.sem(n) for n in ("s_gsb", "s_Gn", "s_H", "s_Ghi", "s_Glo", "s_XB"))
        s_sel, s_mask = e.sem("s_sel"), e.sem("s_mask")
        s_summed, s_carried, s_copied = e.sem("s_summed"), e.sem("s_carried"), e.sem("s_copied")
        s_turned = e.sem("s_turned")
        s_Thi, s_Tlo, s_Hhi, s_Hlo = (e.sem(n) for n in ("s_Thi", "s_Tlo", "s_Hhi", "s_Hlo"))
        s_prod, s_y, s_cent, s_rows = (e.sem(n) for n in ("s_prod", "s_y", "s_cent", "s_rows"))
        tick = e.sem("tick")
        block = ctx.enter_context(e.block())

        @block.sync
        def _(sp):
            sp.dma_start(gamma[:, :], io.L2_gamma.partition_broadcast(P)).then_inc(s_load, 16)
            sp.dma_start(beta[:, :], io.L2_beta.partition_broadcast(P)).then_inc(s_load, 16)
            sp.dma_start(bf[0:1, :], row_of(io.L2_bs)).then_inc(s_load, 16)
            sp.dma_start(bf[1:2, :], row_of(io.L2_bn)).then_inc(s_load, 16)
            sp.wait_ge(s_load, 64)
            sp.wait_ge(s_ones, 1)

            def load_has(T):
                s = T.slot(2)
                wait(sp, s_prod, T.t - 1)
                sp.sem_inc(tick, 1)
                sp.dma_start(has[s][1:2, :].bitcast(F32), g.lastdram[bass.ds(T.t, 1), :]).then_inc(s_has[s], 16)

            def body(i):
                for u in range(U):
                    at(i, u, 2, U, NT, load_has)

            pipeline(sp, GR, 1, 0, body, between=lambda n: W.load_one(sp, n))

        @block.gpsimd
        def _(pool):
            def start_fetch(T):
                s = T.slot(U)
                wait(pool, s_Glo, T.t - 3)
                wait(pool, s_H, T.t - 3)
                wait(pool, s_XB, T.t - 3)
                indices(pool, g, "S", T, col, 3, tick, s_col)
                pool.wait_ge(s_col, T.t + 1)
                pool.sem_inc(tick, 1)
                fetch(pool, G[s][:, :], src, col[s][:, 0:1]).then_inc(s_G[s], 16)
                fetch(pool, X[s][:, :], src, col[s][:, 2:3]).then_inc(s_X[s], 16)

            def keep_x(T):
                s = T.slot(U)
                pool.wait_ge(s_X[s], 16 * (T.use(U) + 1))
                wait(pool, s_rows, T.t - 3)
                pool.tensor_tensor(XB[s][:, :], X[s][:, 0:D], beta[:, :], ALU.add).then_inc(s_XB, 1)

            def low(T):
                s = T.slot(2)
                wait(pool, s_summed, T.t - 1)
                pool.wait_ge(s_Ghi, T.t + 1)
                pool.tensor_tensor(Glo[s][:, :], G[T.slot(U)][:, 0:D], Ghi[s][:, :].bitcast(F32), ALU.subtract)\
                    .then_inc(s_Glo, 1)

            def length_y(T):
                wait(pool, s_rows, T.t - 1)
                ln_y.make_scale(pool, T, neg_half, ylen[T.slot(2)][:, :])

            def store(T):
                s = T.slot(2)
                wait(pool, s_put[s], 16 * T.use(2))
                ln_x.make_scale(pool, T, neg_half, rows[s][:, SCALE:SCALE + 1])
                indices(pool, g, "S", T, colx, 3, tick, s_colx)
                ln_x.make_bias(pool, tick, T, rows[s][:, SCALE:SCALE + 1], rows[s][:, BIAS:BIAS + 1])
                pool.wait_ge(s_colx, T.t + 1)
                pool.wait_ge(ln_x.s_bias, T.t + 1)
                pool.sem_inc(tick, 1)
                put_rows(pool, out, colx[s][:, 2:3], rows[s][:, :], N - 1).then_inc(s_put[s], 16)

            def body(i):
                for u in range(U):
                    at(i, u, -2, U, NT, store)
                    at(i, u, -1, U, NT, length_y)
                    at(i, u, 5, U, NT, start_fetch)
                    at(i, u, 2, U, NT, keep_x)
                    at(i, u, 3, U, NT, low)

            pool.memset(ones_f[:, :], 1.0).then_inc(s_const, 1)
            pool.memset(neg_half[:, :], -0.5).then_inc(s_const, 1)
            for s in range(2):
                pool.memset(carry[s][:, :], 0.0).then_inc(s_const, 1)
                pool.memset(rows[s][:, BIAS + 1:EXT], 0.0).then_inc(s_const, 1)
            pool.wait_ge(s_const, 6)
            pool.wait_ge(s_load, 64)
            pipeline(pool, GR, 2, 1, body, between=lambda n: W.split_low(pool, n))
            for s in range(2):
                pool.wait_ge(s_put[s], 16 * (NT // 2))

        @block.scalar
        def _(act):
            def norm_in(T):
                s = T.slot(U)
                act.wait_ge(s_X[s], 16 * (T.use(U) + 1))
                wait(act, s_y, T.t - 3)
                nc.scalar.activation(H[s][:, :], X[s][:, 0:D], ACT.Relu, bias=X[s][:, BIAS:BIAS + 1],
                                     scale=X[s][:, SCALE:SCALE + 1]).then_inc(s_H, 1)
                act.wait_ge(s_gsb, T.t + 1)
                nc.scalar.activation(G[s][:, 0:D], G[s][:, 0:D], ACT.Relu, bias=gsb[T.slot(2)][:, 1:2],
                                     scale=gsb[T.slot(2)][:, 0:1]).then_inc(s_Gn, 1)
                act.wait_ge(s_Gn, T.t + 1)
                wait(act, s_summed, T.t - 1)
                nc.scalar.copy(Ghi[T.slot(2)][:, :], G[s][:, 0:D]).then_inc(s_Ghi, 1)

            def high_own(T):
                s = T.slot(2)
                act.wait_ge(s_turned, T.t + 1)
                wait(act, s_prod, T.t - 1)
                nc.scalar.copy(Hhi[s][:, :, :], psum_h[s][:, :, :]).then_inc(s_Hhi, 1)

            def high_sum(T):
                s = T.slot(2)
                act.wait_ge(s_copied, T.t + 1)
                nc.scalar.copy(chunks_of(Thi[s]), all_chunks(psum_t[s], 0, P)).then_inc(s_Thi, 1)

            def body(i):
                for u in range(U):
                    at(i, u, 1, U, NT, high_own)
                    at(i, u, 1, U, NT, high_sum)
                    at(i, u, 3, U, NT, norm_in)

            act.wait_ge(s_load, 64)
            nc.scalar.copy(bhi[0:2, :], bf[0:2, :]).then_inc(s_prep, 1)
            act.wait_ge(s_const, 1)
            nc.scalar.copy(has[0][:, :], ones_f[:, :])
            nc.scalar.copy(has[1][:, :], ones_f[:, :]).then_inc(s_ones, 1)
            pipeline(act, GR, 1, 0, body, between=lambda n: W.split_high(act, n))

        @block.vector
        def _(dve):
            def over_degree(T):
                s = T.slot(U)
                dve.wait_ge(s_G[s], 16 * (T.use(U) + 1))
                wait(dve, s_Gn, T.t - 1)
                dve.tensor_scalar(gsb[T.slot(2)][:, :], G[s][:, SCALE:BIAS + 1], g.rdeg[:, bass.ds(T.t, 1)],
                                  None, ALU.mult).then_inc(s_gsb, 1)

            def carried(T):
                carry_in(dve, T, psum_t, mask, carry, s_summed, s_mask, s_carried, s_copied)

            def low_own(T):
                s = T.slot(2)
                dve.wait_ge(s_Hhi, T.t + 1)
                dve.tensor_tensor(Hlo[s][:, :, :], psum_h[s][:, :, :], Hhi[s][:, :, :].bitcast(F32),
                                  ALU.subtract).then_inc(s_Hlo, 1)

            def low_sum(T):
                s = T.slot(2)
                dve.wait_ge(s_Thi, T.t + 1)
                dve.tensor_tensor(chunks_of(Tlo[s]), all_chunks(psum_t[s], 0, P), chunks_of(Thi[s]).bitcast(F32),
                                  ALU.subtract).then_inc(s_Tlo, 1)

            def select(T):
                selection(dve, g, "S", T, sel, mask, s_sel, s_mask, s_summed, s_carried)

            def add_own(T):
                s = T.slot(2)
                dve.wait_ge(s_prod, T.t + 1)
                dve.scalar_tensor_tensor(psum_o[s][:, :], psum_o[s][:, :], 0.0, H[T.slot(U)][:, :],
                                         ALU.max, ALU.add).then_inc(s_y, 1)
                dve.wait_ge(s_y, T.t + 1)
                ln_y.statistics(dve, T, psum_o[s][:, :])

            def center(T):
                s = T.slot(2)
                ln_y.finish(dve, tick, T)
                dve.scalar_tensor_tensor(psum_o[s][:, :], psum_o[s][:, :], ln_y.mean_var[s][:, 0:1], gamma[:, :],
                                         ALU.subtract, ALU.mult).then_inc(s_cent, 1)

            def new_rows(T):
                s = T.slot(2)
                dve.wait_ge(s_cent, T.t + 1)
                dve.wait_ge(ln_y.s_scale, T.t + 1)
                dve.wait_ge(s_XB, T.t + 1)
                wait(dve, s_put[s], 16 * T.use(2))
                dve.scalar_tensor_tensor(rows[s][:, 0:D], psum_o[s][:, :], ylen[s][:, 0:1], XB[T.slot(U)][:, :],
                                         ALU.mult, ALU.add).then_inc(s_rows, 1)

            def norm_rows(T):
                dve.wait_ge(s_rows, T.t + 1)
                ln_x.statistics(dve, T, rows[T.slot(2)][:, 0:D])

            def finish_rows(T):
                wait(dve, ln_x.s_bias, T.t - 1)
                ln_x.finish(dve, tick, T)

            def body(i):
                for u in range(U):
                    at(i, u, -1, U, NT, add_own)
                    at(i, u, 1, U, NT, carried)
                    at(i, u, -1, U, NT, center)
                    at(i, u, 1, U, NT, low_own)
                    at(i, u, -1, U, NT, new_rows)
                    at(i, u, 1, U, NT, low_sum)
                    at(i, u, -1, U, NT, norm_rows)
                    at(i, u, 3, U, NT, select)
                    at(i, u, 4, U, NT, over_degree)
                    at(i, u, -1, U, NT, finish_rows)

            dve.wait_ge(s_load, 64)
            dve.wait_ge(s_const, 6)
            dve.wait_ge(s_prep, 1)
            dve.tensor_tensor(blo[0:2, :], bf[0:2, :], bhi[0:2, :].bitcast(F32), ALU.subtract).then_inc(s_prep, 1)
            pipeline(dve, GR, 1, 1, body)

        @block.tensor
        def _(pe):
            def sum_edges(T):
                s = T.slot(2)
                pe.wait_ge(s_sel, T.t + 1)
                pe.wait_ge(s_Glo, T.t + 1)
                wait(pe, s_Tlo, T.t - 1)
                for c in range(C):
                    cols = slice(c * P, (c + 1) * P)
                    pe.matmul(chunk(psum_t[s], c, SEL), Ghi[s][:, cols], sel[s][:, :], start=True, stop=False)
                    ins = pe.matmul(chunk(psum_t[s], c, SEL), Glo[s][:, cols], sel[s][:, :], start=False, stop=True)
                ins.then_inc(s_summed, 1)
                pe.wait_ge(s_H, T.t + 1)
                wait(pe, s_Hlo, T.t - 1)
                for c in range(C):
                    ins = pe.transpose(psum_h[s][:, c, :], H[T.slot(4)][:, c * P:(c + 1) * P], g.ident[:, :])
                ins.then_inc(s_turned, 1)

            def multiply(T):
                s = T.slot(2)
                pe.wait_ge(s_has[s], 16 * (T.use(2) + 1))
                wait(pe, s_rows, T.t - 1)
                pe.matmul(psum_o[s][:, :], has[s][:, :], bhi[0:2, :], start=True, stop=False)
                pe.matmul(psum_o[s][:, :], has[s][:, :], blo[0:2, :], start=False, stop=False)
                pe.wait_ge(s_Hlo, T.t + 1)
                product(pe, psum_o[s][:, :], Hhi[s], Hlo[s], g.Whi[1], g.Wlo[1], False, False)
                pe.wait_ge(s_Tlo, T.t + 1)
                product(pe, psum_o[s][:, :], Thi[s], Tlo[s], g.Whi[0], g.Wlo[0], False, True).then_inc(s_prod, 1)

            def body(i):
                for u in range(U):
                    at(i, u, 1, U, NT, sum_edges)
                    at(i, u, 0, U, NT, multiply)

            pe.wait_ge(s_prep, 2)
            pipeline(pe, GR, 1, 0, body)



def layer3(nc, io, g):
    NT, N = g.NT, g.N
    U = 4
    GR = NT // U
    ENDS = ("src", "dst")
    INDEX = {"src": 1, "dst": 0}
    with ExitStack() as ctx:
        e = Env(nc, ctx, "f_")
        src = g.xs[2]
        b3f, b3hi, b3lo = e.sb("b3f", [1, D], F32), e.sb("b3hi", [1, D], F32R), e.sb("b3lo", [1, D], F32R)
        ones1, ones_f = e.sb("ones1", [1, P], F32R), e.sb("onesf", [P, P], F32)
        col, colx = e.ring("col", U, [P, 3], I32), e.ring("colx", U, [P, 3], I32)
        G = {k: e.ring("G" + k, U, [P, EXT], F32) for k in ENDS}
        X = e.ring("X", U, [P, EXT], F32)
        Hhi = {k: e.ring("Hhi" + k, 2, [P, C, P], F32R) for k in ENDS}
        Hlo = {k: e.ring("Hlo" + k, 2, [P, C, P], F32R) for k in ENDS}
        sel, lastsel = e.ring("sel", 2, [P, SEL], F32R), e.ring("lastsel", 2, [P, P], F32R)
        Mhi, Mlo = e.ring("Mhi", 2, [P, D], F32R), e.ring("Mlo", 2, [P, D], F32R)
        carry = e.ring("carry", 2, [P, D], F32)
        rows = e.ring("rows", 2, [P, D], F32)
        psum_h = {k: e.ps("ph" + k, [P, C, P]) for k in ENDS}
        psum_m = [e.ps(f"pm{i}", [P, D]) for i in range(2)]
        psum_o = [e.ps(f"po{i}", [P, D]) for i in range(2)]
        psum_c = [e.ps(f"pc{i}", [P, D]) for i in range(2)]

        s_load, s_const, s_prep = e.sem("s_load"), e.sem("s_const"), e.sem("s_prep")
        s_col, s_colx = e.sem("s_col"), e.sem("s_colx")
        s_G = {k: e.sems("s_G" + k, U) for k in ENDS}
        s_X, s_put = e.sems("s_X", U), e.sems("s_put", U)
        s_Gn, s_turned, s_Hhi, s_Hlo = ({k: e.sem(n + k) for k in ENDS} for n in ("s_Gn", "s_turned", "s_Hhi", "s_Hlo"))
        s_sel, s_msg, s_Mhi, s_Mlo, s_sum, s_carry, s_added, s_rows = (
            e.sem(n) for n in ("s_sel", "s_msg", "s_Mhi", "s_Mlo", "s_sum", "s_carry", "s_added", "s_rows"))
        tick = e.sem("tick")
        block = ctx.enter_context(e.block())

        @block.sync
        def _(sp):
            sp.dma_start(b3f[:, :], row_of(io.L3_b)).then_inc(s_load, 16)
            sp.wait_ge(s_load, 16)

        @block.gpsimd
        def _(pool):
            def start_fetch(T):
                s = T.slot(U)
                for k in ENDS:
                    wait(pool, s_turned[k], T.t - 3)
                indices(pool, g, "S", T, col, 3, tick, s_col)
                pool.wait_ge(s_col, T.t + 1)
                pool.sem_inc(tick, 1)
                for k in ENDS:
                    n = INDEX[k]
                    fetch(pool, G[k][s][:, :], src, col[s][:, n:n + 1]).then_inc(s_G[k][s], 16)

            def fetch_x(T):
                s = T.slot(U)
                wait(pool, s_rows, T.t - 3)
                wait(pool, s_put[s], 16 * T.use(U))
                indices(pool, g, "S", T, colx, 3, tick, s_colx)
                pool.wait_ge(s_colx, T.t + 1)
                pool.sem_inc(tick, 1)
                fetch(pool, X[s][:, :], src, colx[s][:, 2:3]).then_inc(s_X[s], 16)

            def store(T):
                s = T.slot(U)
                pool.wait_ge(s_rows, T.t + 1)
                pool.sem_inc(tick, 1)
                put_rows(pool, io.out, colx[s][:, 2:3], rows[T.slot(2)][:, :], N - 1).then_inc(s_put[s], 16)

            def body(i):
                for u in range(U):
                    at(i, u, 6, U, NT, start_fetch)
                    at(i, u, 0, U, NT, fetch_x)
                    at(i, u, -3, U, NT, store)

            pool.memset(ones_f[:, :], 1.0).then_inc(s_const, 1)
            for s in range(2):
                pool.memset(carry[s][:, :], 0.0).then_inc(s_const, 1)
            pipeline(pool, GR, 2, 1, body)
            for s in range(U):
                pool.wait_ge(s_put[s], 16 * GR)

        @block.scalar
        def _(act):
            def norm_in(T):
                s = T.slot(U)
                for k in ENDS:
                    act.wait_ge(s_G[k][s], 16 * (T.use(U) + 1))
                    nc.scalar.activation(G[k][s][:, 0:D], G[k][s][:, 0:D], ACT.Relu, bias=G[k][s][:, BIAS:BIAS + 1],
                                         scale=G[k][s][:, SCALE:SCALE + 1]).then_inc(s_Gn[k], 1)

            def high(T):
                s = T.slot(2)
                for k in ENDS:
                    act.wait_ge(s_turned[k], T.t + 1)
                    wait(act, s_msg, T.t - 1)
                    nc.scalar.copy(Hhi[k][s][:, :, :], psum_h[k][:, :, :]).then_inc(s_Hhi[k], 1)

            def message(T):
                s = T.slot(2)
                act.wait_ge(s_msg, T.t + 1)
                wait(act, s_sum, T.t - 1)
                nc.scalar.activation(Mhi[s][:, :], psum_m[s][:, :], ACT.Relu).then_inc(s_Mhi, 1)

            def body(i):
                for u in range(U):
                    at(i, u, -1, U, NT, message)
                    at(i, u, 1, U, NT, high)
                    at(i, u, 3, U, NT, norm_in)

            act.wait_ge(s_load, 16)
            nc.scalar.copy(b3hi[:, :], b3f[:, :]).then_inc(s_prep, 1)
            act.wait_ge(s_const, 1)
            nc.scalar.copy(ones1[:, :], ones_f[0:1, :]).then_inc(s_prep, 1)
            pipeline(act, GR, 1, 1, body)

        @block.vector
        def _(dve):
            def low(T):
                s = T.slot(2)
                for k in ENDS:
                    dve.wait_ge(s_Hhi[k], T.t + 1)
                    dve.tensor_tensor(Hlo[k][s][:, :, :], psum_h[k][:, :, :], Hhi[k][s][:, :, :].bitcast(F32),
                                      ALU.subtract).then_inc(s_Hlo[k], 1)

            def select(T):
                s = T.slot(2)
                wait(dve, s_sum, T.t - 1)
                dve.tensor_scalar(lastsel[s][:, :], ones_f[:, :], g.in_last[:, bass.ds(T.t, 1)], None, ALU.mult)
                selection(dve, g, "S", T, sel, None, s_sel, None, s_sum, None)

            def message(T):
                s = T.slot(2)
                dve.wait_ge(s_Mhi, T.t + 1)
                dve.scalar_tensor_tensor(Mlo[s][:, :], psum_m[s][:, :], 0.0, Mhi[s][:, :].bitcast(F32),
                                         ALU.max, ALU.subtract).then_inc(s_Mlo, 1)

            def combine(T):
                s, before = T.slot(2), (T.j - 1) % 2
                one = bass.ds(T.t, 1)
                dve.wait_ge(s_sum, T.t + 1)
                wait(dve, s_carry, T.t)
                dve.scalar_tensor_tensor(carry[s][:, :], carry[before][:, :], g.same_last[:, one], psum_c[s][:, :],
                                         ALU.mult, ALU.add).then_inc(s_carry, 1)
                dve.scalar_tensor_tensor(psum_o[s][:, :], carry[before][:, :], g.takes[:, one], psum_o[s][:, :],
                                         ALU.mult, ALU.add).then_inc(s_added, 1)
                dve.wait_ge(s_added, T.t + 1)
                dve.wait_ge(s_X[T.slot(U)], 16 * (T.use(U) + 1))
                wait(dve, s_put[(T.j - 2) % U], 16 * (T.k + 1 if T.j >= 2 else T.k))
                dve.tensor_tensor(rows[s][:, :], psum_o[s][:, :], X[T.slot(U)][:, 0:D], ALU.add).then_inc(s_rows, 1)

            def body(i):
                for u in range(U):
                    at(i, u, -1, U, NT, message)
                    at(i, u, 1, U, NT, low)
                    at(i, u, -2, U, NT, combine)
                    at(i, u, 0, U, NT, select)

            dve.wait_ge(s_const, 3)
            dve.wait_ge(s_prep, 1)
            dve.tensor_tensor(b3lo[:, :], b3f[:, :], b3hi[:, :].bitcast(F32), ALU.subtract).then_inc(s_prep, 1)
            pipeline(dve, GR, 1, 1, body)

        @block.tensor
        def _(pe):
            def turn(T):
                for k in ENDS:
                    pe.wait_ge(s_Gn[k], T.t + 1)
                    wait(pe, s_Hlo[k], T.t)
                    for c in range(C):
                        ins = pe.transpose(psum_h[k][:, c, :], G[k][T.slot(U)][:, c * P:(c + 1) * P], g.ident[:, :])
                    ins.then_inc(s_turned[k], 1)

            def multiply(T):
                s = T.slot(2)
                wait(pe, s_Mlo, T.t - 1)
                pe.matmul(psum_m[s][:, :], ones1[:, :], b3hi[:, :], start=True, stop=False)
                pe.matmul(psum_m[s][:, :], ones1[:, :], b3lo[:, :], start=False, stop=False)
                for n, k in enumerate(ENDS):
                    pe.wait_ge(s_Hlo[k], T.t + 1)
                    ins = product(pe, psum_m[s][:, :], Hhi[k][s], Hlo[k][s], g.Whi[2 + n], g.Wlo[2 + n], False, n == 1)
                ins.then_inc(s_msg, 1)

            def sum_edges(T):
                s = T.slot(2)
                pe.wait_ge(s_sel, T.t + 1)
                pe.wait_ge(s_Mlo, T.t + 1)
                wait(pe, s_rows, T.t - 1)
                pe.matmul(psum_o[s][:, :], sel[s][:, 0:P], Mhi[s][:, :], start=True, stop=False)
                pe.matmul(psum_o[s][:, :], sel[s][:, 0:P], Mlo[s][:, :], start=False, stop=True)
                pe.matmul(psum_c[s][:, :], lastsel[s][:, :], Mhi[s][:, :], start=True, stop=False)
                pe.matmul(psum_c[s][:, :], lastsel[s][:, :], Mlo[s][:, :], start=False, stop=True).then_inc(s_sum, 1)

            def body(i):
                for u in range(U):
                    at(i, u, 1, U, NT, turn)
                    at(i, u, -2, U, NT, sum_edges)
                    at(i, u, 0, U, NT, multiply)

            pe.wait_ge(s_prep, 3)
            pipeline(pe, GR, 1, 1, body)


WEIGHTS = {"L0_W1": "L0_gnn_W1", "L0_W2": "L0_gnn_W2", "L1_W1": "L1_gnn_W1", "L1_W2": "L1_gnn_W2",
           "L2_Ws": "L2_gnn_W_self", "L2_Wn": "L2_gnn_W_neigh", "L3_W": "L3_gnn_W"}
VECTORS = {"L0_b1": "L0_gnn_b1", "L0_b2": "L0_gnn_b2", "L1_b1": "L1_gnn_b1", "L1_b2": "L1_gnn_b2",
           "L1_gamma": "L1_gnn_gamma", "L1_beta": "L1_gnn_beta", "L2_bs": "L2_gnn_b_self",
           "L2_bn": "L2_gnn_b_neigh", "L2_gamma": "L2_gnn_ln_gamma", "L2_beta": "L2_gnn_ln_beta",
           "L3_b": "L3_gnn_b"}


class Named:
    pass


def program(nc, io, N):
    NT = N // P
    g = Named()
    g.NT, g.N = NT, N

    def dram(name, shape, dt=F32):
        return nc.dram_tensor(name, shape, dt, kind="Internal").ap()

    g.h0, g.h1 = dram("h0", [N, D]), dram("h1", [N, D])
    g.xs = [dram(f"x{n}", [N, EXT]) for n in range(1, 4)]
    g.seq = {k: dram("seq" + k, [N + 1]) for k in "DS"}
    g.seldram = {k: dram("sel" + k, [NT, SEL], I16) for k in "DS"}
    g.lastdram, g.qdram = dram("lastdram", [NT, P]), dram("qdram", [NT, P], I16)
    with ExitStack() as ctx:
        e = Env(nc, ctx, "")
        parts = e.sb("parts", [P, 8, C, D], F32R)
        g.parts = parts[:, :, :, :].rearrange("p w c n -> p (w c n)")
        g.Whi, g.Wlo = ([parts[:, 2 * slot + half] for slot in range(4)] for half in range(2))
        g.ident = e.sb("ident", [P, P], F32)
        g.selrows = {k: e.sb("selrows" + k, [P, NT, SEL], I16) for k in "DS"}
        g.index = {k: e.sb("index" + k, [P, NT, 3], I32) for k in "DS"}
        g.keycol, g.keylast, g.keyprev = (
            {k: e.sb(n + k, [P, NT], F32) for k in "DS"} for n in ("keycol", "keylast", "keyprev"))
        g.degcol, g.rdeg = e.sb("degcol", [P, NT], F32), e.sb("rdeg", [P, NT], F32)
        g.same_last, g.takes, g.in_last = (e.sb(n, [P, NT], F32) for n in ("samelast", "takes", "inlast"))
        prepare_orders(nc, io, g)
        layer0(nc, io, g, False)
        layer0(nc, io, g, True)
        layer1(nc, io, g)
        layer2(nc, io, g)
        layer3(nc, io, g)


def kernel(**inputs):
    import numpy as np
    import concourse.bacc as bacc
    from concourse.bass_utils import run_bass_kernel_spmd

    x, src, dst = (np.asarray(inputs[n]) for n in ("x", "src", "dst"))
    nodes = x.shape[0]
    N = -(-nodes // (4 * P)) * 4 * P
    loops = np.arange(nodes, N, dtype=src.dtype)
    src, dst = np.concatenate([src, loops]), np.concatenate([dst, loops])
    arrays = {"x": np.concatenate([x, np.zeros((N - nodes, D), x.dtype)]), "src": src, "dst": dst,
              "src_col": np.ascontiguousarray(src.reshape(-1, P).T),
              "dst_col": np.ascontiguousarray(dst.reshape(-1, P).T),
              "eps": np.asarray(inputs["L1_gnn_eps"]).reshape(1)}
    for name, given in WEIGHTS.items():
        arrays[name] = np.ascontiguousarray(np.asarray(inputs[given]).T)
    for name, given in VECTORS.items():
        arrays[name] = np.asarray(inputs[given])
    arrays["L1_b1col"] = np.ascontiguousarray(arrays.pop("L1_b1").reshape(C, P).T)

    nc = bacc.Bacc("TRN2", target_bir_lowering=False, num_devices=1)
    io = Named()
    for name, a in arrays.items():
        io.__dict__[name] = nc.dram_tensor("in_" + name, a.shape, mybir.dt.from_np(a.dtype), kind="ExternalInput").ap()
    io.out = nc.dram_tensor("out_x", (N, D), F32, kind="ExternalOutput").ap()
    program(nc, io, N)
    r = run_bass_kernel_spmd(nc, [{"in_" + name: a for name, a in arrays.items()}], core_ids=[0])
    return r.results[0]["out_x"][0:nodes]
```

```python
from contextlib import ExitStack, contextmanager

import concourse.bass as bass
from concourse import mybir

P = 128
D = 512
C = D // P
EXT = 520
SCALE, BIAS = D, D + 1
SEL = P + 2
LN_EPS = 1e-5
NOWHERE = 1 << 20

F32, F32R, BF16 = mybir.dt.float32, mybir.dt.float32r, mybir.dt.bfloat16
I32, I16 = mybir.dt.int32, mybir.dt.int16
ALU = mybir.AluOpType
ACT = mybir.ActivationFunctionType
AX = mybir.AxisListType


class Tile:

    def __init__(self, k, j, unroll):
        self.k, self.j, self.unroll = k, j, unroll
        self.t = k * unroll + j if j else k * unroll

    def slot(self, ring):
        return self.j % ring

    def use(self, ring):
        each = self.unroll // ring
        n = self.k * each if each > 1 else self.k
        return n + self.j // ring if self.j // ring else n


def at(i, u, off, unroll, tiles, stage):
    tile = Tile(i + (u + off) // unroll, (u + off) % unroll, unroll)
    if not isinstance(i, int) or 0 <= tile.t < tiles:
        stage(tile)


def pipeline(eng, groups, lead, drain, body, ahead=2, between=None):
    first, last = 2, groups - ahead
    for i in range(-lead, first):
        body(i)
        if between and i >= 0:
            between(i)
    with eng.Fori(first, last) as i:
        body(i)
    for i in range(last, groups + drain):
        body(i)


def wait(eng, sem, value):
    if not isinstance(value, int) or value > 0:
        eng.wait_ge(sem, value)


class Env:

    def __init__(self, nc, ctx, prefix):
        self.nc, self.ctx, self.prefix = nc, ctx, prefix
        self.semaphores = []

    def sb(self, name, shape, dt):
        return self.ctx.enter_context(self.nc.sbuf_tensor(self.prefix + name, shape, dt))

    def ring(self, name, n, shape, dt):
        return [self.sb(f"{name}{i}", shape, dt) for i in range(n)]

    def ps(self, name, shape, dt=F32):
        return self.ctx.enter_context(self.nc.psum_tensor(self.prefix + name, shape, dt))

    def sem(self, name):
        self.semaphores.append(self.nc.alloc_semaphore(self.prefix + name))
        return self.semaphores[-1]

    @contextmanager
    def block(self):
        with self.nc.Block() as block:
            yield block
        self.nc.clear_and_free_semaphores(self.semaphores)
        self.nc.all_engine_barrier()
        self.semaphores = []

    def sems(self, name, n):
        return [self.sem(f"{name}{i}") for i in range(n)]



def prepare_orders(nc, io, g):
    NT, N = g.NT, g.N
    KEYS = ("D", "S")
    with ExitStack() as ctx:
        e = Env(nc, ctx, "p_")
        sb, ps, sem = e.sb, e.ps, e.sem

        key_i = {k: sb("keyi" + k, [P, NT], I32) for k in KEYS}
        tmp_i = sb("tmpi", [P, NT], I32)
        key_f = {k: sb("keyf" + k, [P, NT], F32) for k in KEYS}
        ends = sb("ends", [P, NT, 3], F32)
        hi_f = {k: sb("hif" + k, [P, NT], F32) for k in KEYS}
        lo_f = {k: sb("lof" + k, [P, NT], F32) for k in KEYS}
        hirow = {k: g.parts.bitcast(I16)[0:NT, m * N:(m + 1) * N] for m, k in enumerate(KEYS)}
        iota_i = sb("iotai", [P, P], I32)
        iota_b = sb("iotab", [P, P], BF16)
        pidx_i = sb("pidxi", [P, 1], I32)
        node_i = sb("nodei", [P, NT], I32)
        ones_f = sb("onesf", [P, P], F32)
        ones_b = sb("onesb", [P, 2], BF16)
        before_f = sb("beforef", [P, P], F32)
        before_b = sb("beforeb", [P, P], BF16)
        neg_half = sb("neghalf", [P, 1], F32)
        count = {k: sb("count" + k, [NT, P], F32) for k in KEYS}
        start = {k: sb("start" + k, [NT, P], F32) for k in KEYS}
        colform = sb("colform", [P, NT], F32)
        total = sb("total", [NT, 1], F32)
        totals = sb("totals", [NT, P], F32)
        sentinel = sb("sentinel", [1, 1], F32)

        c12 = ctx.enter_context(ExitStack())
        first = Env(nc, c12, "q_")
        keyrow = {k: first.sb("keyrow" + k, [P, N], I16) for k in KEYS}
        zero_row = first.sb("zerorow", [P, D], F32)
        OHhi = {k: first.sb("ohhi" + k, [P, NT, NT], BF16) for k in KEYS}
        OHlo = {k: g.selrows[k][:, :, :].rearrange("p t c -> p (t c)").bitcast(BF16)[:, 0:N]
                .rearrange("p (t n) -> p t n", n=P) for k in KEYS}

        s_load = sem("s_load")
        s_rowload = {k: sem("s_rowload" + k) for k in KEYS}
        s_iota = sem("s_iota")
        s_v = sem("s_v")
        s_one = sem("s_one")
        s_cnt = sem("s_cnt")
        s_pe = sem("s_pe")

        with ExitStack() as c1:
            pcount = {k: c1.enter_context(nc.psum_tensor("p_pcount" + k, [P, 512], F32)) for k in KEYS}
            ptr = c1.enter_context(nc.psum_tensor("p_ptr", [P, 512], F32))
            pstart = c1.enter_context(nc.psum_tensor("p_pstart", [P, 512], F32))
            R = 8
            ln = Env(nc, c1, "n_")
            xt = ln.ring("xt", R, [P, EXT], F32)
            st = ln.ring("st", 2, [P, 6], F32)
            mv = ln.ring("mv", 2, [P, 2], F32)
            va = ln.ring("va", 2, [P, 1], F32)
            q_x = e.sems("q_x", R)
            q_st, q_mv, q_var, q_a, q_b = (e.sem(n) for n in ("q_st", "q_mv", "q_var", "q_a", "q_b"))
            q_ext, q_tick, q_const = e.sems("q_ext", R), e.sem("q_tick"), e.sem("q_const")
            GR = NT // R
            block = c1.enter_context(e.block())

            @block.sync
            def _(sp):
                sp.dma_start(key_i["D"][:, :], io.dst_col).then_inc(s_load, 16)
                sp.dma_start(key_i["S"][:, :], io.src_col).then_inc(s_load, 16)

                def load(T):
                    s = T.slot(R)
                    wait(sp, q_ext[s], 16 * T.use(R))
                    sp.sem_inc(q_tick, 1)
                    sp.dma_start(xt[s][:, 0:D], io.x[bass.ds(T.t * P, P), :]).then_inc(q_x[s], 16)

                def store(T):
                    s = T.slot(R)
                    if isinstance(T.t, int) and T.t == 0:
                        sp.wait_ge(q_const, 1)
                    sp.wait_ge(q_b, T.t + 1)
                    sp.sem_inc(q_tick, 1)
                    sp.dma_start(g.xs[0][bass.ds(T.t * P, P), :], xt[s][:, :]).then_inc(q_ext[s], 16)

                def body(i):
                    for u in range(R):
                        at(i, u, 0, R, NT, store)
                        at(i, u, 6, R, NT, load)

                pipeline(sp, GR, 1, 0, body)
                for s in range(R):
                    sp.wait_ge(q_ext[s], 16 * GR)

            @block.gpsimd
            def _(pool):
                pool.iota(iota_i[:, :], pattern=[[1, P]], base=0, channel_multiplier=0).then_inc(s_iota, 1)
                pool.iota(pidx_i[:, :], pattern=[[0, 1]], base=0, channel_multiplier=1).then_inc(s_iota, 1)
                pool.iota(node_i[:, :], pattern=[[P, NT]], base=0, channel_multiplier=1).then_inc(s_iota, 1)
                pool.memset(g.ident[:, :], 0.0).then_inc(s_iota, 1)
                pool.memset(ones_f[:, :], 1.0)
                pool.memset(ones_b[:, :], 1.0)
                pool.memset(zero_row[:, :], 0.0)
                pool.memset(neg_half[:, :], -0.5)
                pool.memset(sentinel[:, :], -1.0)
                for s in range(R):
                    ins = pool.memset(xt[s][:, BIAS + 1:EXT], 0.0)
                ins.then_inc(q_const, 1)
                pool.wait_ge(s_iota, 4)
                pool.dma_start(keyrow["D"][:, :], io.dst.partition_broadcast(P)).then_inc(s_rowload["D"], 16)
                pool.dma_start(keyrow["S"][:, :], io.src.partition_broadcast(P)).then_inc(s_rowload["S"], 16)
                pool.affine_select(out=g.ident[:, :], in_=g.ident[:, :], compare_op=ALU.not_equal, fill=1.0,
                                   base=0, pattern=[[-1, P]], channel_multiplier=1).then_inc(s_iota, 1)

                def scale(T):
                    s, x = T.slot(2), xt[T.slot(R)]
                    pool.wait_ge(q_mv, T.t + 1)
                    pool.sem_inc(q_tick, 1)
                    pool.tensor_scalar(va[s][:, 0:1], mv[s][:, 1:2], 1.0, LN_EPS, ALU.mult, ALU.add)\
                        .then_inc(q_var, 1)
                    pool.wait_ge(q_var, T.t + 1)
                    pool.tensor_tensor(x[:, SCALE:SCALE + 1], va[s][:, 0:1], neg_half[:, :], ALU.pow).then_inc(q_a, 1)
                    pool.wait_ge(q_a, T.t + 1)
                    pool.sem_inc(q_tick, 1)
                    pool.tensor_scalar(x[:, BIAS:BIAS + 1], mv[s][:, 0:1], x[:, SCALE:SCALE + 1], -1.0,
                                       ALU.mult, ALU.mult)\
                        .then_inc(q_b, 1)

                def body(i):
                    for u in range(R):
                        at(i, u, 0, R, NT, scale)

                pipeline(pool, GR, 0, 0, body)

            @block.vector
            def _(dve):
                n = [0]

                def step(ins):
                    ins.then_inc(s_v, 1)
                    n[0] += 1
                    dve.wait_ge(s_v, n[0])

                dve.wait_ge(s_iota, 5)
                dve.tensor_tensor(g.hilo[:, :], g.ident[0:4, 0:2], g.ident[0:4, 2:4], ALU.add)
                step(dve.tensor_copy(iota_b[:, :], iota_i[:, :]))
                step(dve.tensor_copy(g.iota_f[:, :], iota_i[:, :]))
                step(dve.tensor_copy(g.pidx[:, :], pidx_i[:, :]))
                step(dve.tensor_scalar(g.minus_p[:, :], g.pidx[:, :], -1.0, None, ALU.mult))
                step(dve.tensor_copy(g.node_f[:, :], node_i[:, :]))
                step(dve.tensor_scalar(before_f[:, :], g.iota_f[:, :], g.pidx[:, 0:1], None, ALU.is_gt))
                step(dve.tensor_scalar(before_b[:, :], g.iota_f[:, :], g.pidx[:, 0:1], None, ALU.is_gt))
                dve.wait_ge(s_load, 32)
                for k in KEYS:
                    step(dve.tensor_copy(key_f[k][:, :], key_i[k][:, :]))
                    step(dve.tensor_scalar(tmp_i[:, :], key_i[k][:, :], 7, None, ALU.logical_shift_right))
                    step(dve.tensor_copy(hi_f[k][:, :], tmp_i[:, :]))
                    step(dve.tensor_scalar(tmp_i[:, :], key_i[k][:, :], P - 1, None, ALU.bitwise_and))
                    step(dve.tensor_copy(lo_f[k][:, :], tmp_i[:, :]))
                for m, k in enumerate(("D", "S", "D")):
                    dve.tensor_copy(ends[:, :, m], key_i[k][:, :])

                def hot(T):
                    one = bass.ds(T.t, 1)
                    for k in KEYS:
                        dve.tensor_scalar(OHhi[k][:, one, :], iota_b[:, 0:NT], hi_f[k][:, one], None, ALU.is_equal)
                        dve.tensor_scalar(OHlo[k][:, one, :], iota_b[:, :], lo_f[k][:, one], None, ALU.is_equal)\
                            .then_inc(s_one, 1)

                def statistics_x(T):
                    s = T.slot(2)
                    dve.wait_ge(q_x[T.slot(R)], 16 * (T.use(R) + 1))
                    dve.bn_stats(st[s][:, :], xt[T.slot(R)][:, 0:D]).then_inc(q_st, 1)

                def aggregate_x(T):
                    s = T.slot(2)
                    dve.wait_ge(q_st, T.t + 1)
                    wait(dve, q_b, T.t - 1)
                    dve.sem_inc(q_tick, 1)
                    dve.bn_aggr(mv[s][:, :], st[s][:, :]).then_inc(q_mv, 1)

                def body(i):
                    for u in range(R):
                        at(i, u, 0, R, NT, statistics_x)
                        at(i, u, 0, R, NT, hot)
                        at(i, u, 0, R, NT, aggregate_x)

                pipeline(dve, GR, 0, 0, body)
                for k in KEYS:
                    dve.wait_ge(s_rowload[k], 16)
                    with dve.Fori(0, 4) as quarter:
                        part = bass.ds(quarter * (N // 4), N // 4)
                        dve.tensor_scalar(hirow[k][:, part], keyrow[k][0:NT, part], 7, None, ALU.logical_shift_right)
                for m, k in enumerate(KEYS):
                    dve.wait_ge(s_cnt, m + 1)
                    step(dve.tensor_copy(count[k][:, :], pcount[k][0:NT, 0:P]))
                for m, k in enumerate(KEYS):
                    dve.wait_ge(s_pe, 2 * m + 1)
                    step(dve.tensor_copy(colform[:, :], ptr[:, 0:NT]))
                    step(dve.tensor_reduce(total[:, :], count[k][:, :], AX.X, ALU.add))
                    step(dve.tensor_scalar(totals[:, :], ones_f[0:NT, :], total[:, 0:1], None, ALU.mult))
                    dve.wait_ge(s_pe, 2 * m + 2)
                    step(dve.tensor_copy(start[k][:, :], pstart[0:NT, 0:P]))

            @block.tensor
            def _(pe):
                pe.wait_ge(s_one, 2)
                for k in KEYS:
                    pe.matmul(pcount[k][0:NT, 0:P], OHhi[k][:, 0, :], OHlo[k][:, 0, :], start=True, stop=False)
                with pe.Fori(1, NT - 1) as t:
                    pe.wait_ge(s_one, 2 * t + 2)
                    for k in KEYS:
                        pe.matmul(pcount[k][0:NT, 0:P], OHhi[k][:, bass.ds(t, 1), :], OHlo[k][:, bass.ds(t, 1), :],
                                  start=False, stop=False)
                pe.wait_ge(s_one, 2 * NT)
                for k in KEYS:
                    pe.matmul(pcount[k][0:NT, 0:P], OHhi[k][:, NT - 1, :], OHlo[k][:, NT - 1, :],
                              start=False, stop=True).then_inc(s_cnt, 1)
                pe.wait_ge(s_iota, 5)
                for m, k in enumerate(KEYS):
                    base = 7 + 10
                    pe.wait_ge(s_v, base + m + 1 if m == 0 else base + 2 + 4)
                    pe.transpose(ptr[:, 0:NT], count[k][:, :], g.ident[0:NT, 0:NT]).then_inc(s_pe, 1)
                    pe.wait_ge(s_v, base + 2 + 4 * m + 3)
                    pe.matmul(pstart[0:NT, 0:P], colform[:, :], before_f[:, :], start=True, stop=False)
                    pe.matmul(pstart[0:NT, 0:P], before_f[0:NT, 0:NT], totals[:, :], start=False, stop=True)\
                        .then_inc(s_pe, 1)

        U = 4
        with ExitStack() as c2:
            f = Env(nc, c2, "r_")
            square = {k: f.sb("square" + k, [NT, P], F32) for k in KEYS}
            OHhiT = {k: f.ring("ohhit" + k, 2, [NT, P], F32) for k in KEYS}
            earlier = {k: f.ring("earlier" + k, 2, [P, P], BF16) for k in KEYS}
            table = {k: f.ring("table" + k, 2, [NT, 2, P], F32) for k in KEYS}
            picked = f.sb("picked", [P, P], F32)
            posf = {k: f.ring("posf" + k, 2, [P, 1], F32) for k in KEYS}
            posi = {k: f.ring("posi" + k, U, [P, 1], I32) for k in KEYS}
            cargo = {k: f.ring("cargo" + k, U, [P, 4], F32) for k in KEYS}
            pbase = {k: f.ps("pbase" + k, [P, 512]) for k in KEYS}
            plook = {k: [f.ps(f"plook{k}{j}", [P, 512]) for j in range(2)] for k in KEYS}
            q_tab, q_acc, q_square, q_hot, q_early, q_look, q_pos, q_ends = (
                {k: f.sem(n + k) for k in KEYS} for n in
                ("q_tab", "q_acc", "q_square", "q_hot", "q_early", "q_look", "q_pos", "q_ends"))
            q_moved = {k: f.sems("q_moved" + k, U) for k in KEYS}
            q_pick, q_tick, q_const, q_end = (f.sem(n) for n in ("q_pick", "q_tick", "q_const", "q_end"))
            GR = NT // U
            block = c2.enter_context(f.block())

            @block.sync
            def _(sp):
                for k in KEYS:
                    sp.dma_start(g.sorted[k][N:N + 1, 0:1], sentinel[:, :]).then_inc(q_end, 16)
                with sp.Fori(0, NT) as t:
                    sp.dma_start(g.h1[bass.ds(t * P, P), :], zero_row[:, :]).then_inc(q_end, 16)
                sp.wait_ge(q_end, 16 * (2 + NT))

            @block.vector
            def _(dve):
                def before(T):
                    s = T.slot(2)
                    for k in KEYS:
                        wait(dve, q_look[k], T.t - 1)
                        dve.scalar_tensor_tensor(earlier[k][s][:, :], keyrow[k][:, bass.ds(T.t * P, P)],
                                                 key_f[k][:, bass.ds(T.t, 1)], before_b[:, :],
                                                 ALU.is_equal, ALU.mult).then_inc(q_early[k], 1)

                def pick(T):
                    s, r = T.slot(2), T.slot(U)
                    for m, k in enumerate(KEYS):
                        dve.wait_ge(q_look[k], T.t + 1)
                        wait(dve, q_moved[k][r], 16 * T.use(U))
                        n = T.t * 4 + 2 * m
                        wait(dve, q_pick, n)
                        dve.scalar_tensor_tensor(picked[:, :], plook[k][s][:, 0:P], 1.0, OHlo[k][:, bass.ds(T.t, 1), :],
                                                 ALU.mult, ALU.mult, accum_out=posf[k][s][:, :])\
                            .then_inc(q_pick, 1)
                        dve.wait_ge(q_pick, n + 1)
                        dve.scalar_tensor_tensor(picked[:, :], plook[k][s][:, P:2 * P], 1.0,
                                                 OHlo[k][:, bass.ds(T.t, 1), :],
                                                 ALU.mult, ALU.mult, accum_out=cargo[k][r][:, 2:3])\
                            .then_inc(q_pick, 1)
                    for k in KEYS:
                        dve.tensor_tensor(posi[k][r][:, :], plook[k][s][:, 2 * P:2 * P + 1], posf[k][s][:, :], ALU.add)\
                            .then_inc(q_pos[k], 1)

                def body(i):
                    for u in range(U):
                        at(i, u, 1, U, NT, before)
                        at(i, u, 0, U, NT, pick)

                pipeline(dve, GR, 1, 0, body)

            @block.gpsimd
            def _(pool):
                def move(T):
                    r = T.slot(U)
                    for k in KEYS:
                        pool.wait_ge(q_pos[k], T.t + 1)
                        pool.wait_ge(q_ends[k], T.t + 1)
                        pool.sem_inc(q_tick, 1)
                        pool.indirect_dma_start(g.sorted[k], bass.IndirectOffsetOnAxis(ap=posi[k][r][:, 0:1], axis=0),
                                                cargo[k][r][:, :], None).then_inc(q_moved[k][r], 16)

                def body(i):
                    for u in range(U):
                        at(i, u, -1, U, NT, move)

                for k in KEYS:
                    for s in range(U):
                        pool.memset(cargo[k][s][:, 3:4], 0.0).then_inc(q_const, 1)
                pool.wait_ge(q_const, 2 * U)
                pipeline(pool, GR, 0, 1, body)
                for k in KEYS:
                    for s in range(U):
                        pool.wait_ge(q_moved[k][s], 16 * GR)

            @block.scalar
            def _(act):
                def table_of(T):
                    s = T.slot(2)
                    for k in KEYS:
                        act.wait_ge(q_acc[k], T.t + 1)
                        wait(act, q_look[k], T.t - 1)
                        nc.scalar.copy(table[k][s][:, 0, :], pbase[k][0:NT, 0:P]).then_inc(q_tab[k], 1)

                def hot(T):
                    s = T.slot(2)
                    for k in KEYS:
                        wait(act, q_hot[k], T.t)
                        act.sem_inc(q_tick, 1)
                        nc.scalar.activation(square[k][:, :], hirow[k][:, bass.ds(T.t * P, P)], ACT.Square,
                                             bias=g.minus_p[0:NT, 0:1]).then_inc(q_square[k], 1)
                    for k in KEYS:
                        act.wait_ge(q_square[k], T.t + 1)
                        wait(act, q_look[k], T.t - 1)
                        nc.scalar.activation(OHhiT[k][s][:, :], square[k][:, :], ACT.Relu, bias=ones_f[0:NT, 0:1],
                                             scale=-1.0).then_inc(q_hot[k], 1)

                def name_ends(T):
                    r = T.slot(U)
                    for m, k in enumerate(KEYS):
                        wait(act, q_moved[k][r], 16 * T.use(U))
                        act.sem_inc(q_tick, 1)
                        nc.scalar.copy(cargo[k][r][:, 0:2], ends[:, bass.ds(T.t, 1), m:m + 2]).then_inc(q_ends[k], 1)

                def body(i):
                    for u in range(U):
                        at(i, u, 0, U, NT, table_of)
                        at(i, u, 1, U, NT, hot)
                        at(i, u, 0, U, NT, name_ends)

                for k in KEYS:
                    for s in range(2):
                        nc.scalar.copy(table[k][s][:, 1, :], count[k][:, :])
                pipeline(act, GR, 1, 0, body)

            @block.tensor
            def _(pe):
                for k in KEYS:
                    pe.matmul(pbase[k][0:NT, 0:P], g.ident[0:NT, 0:NT], start[k][:, :], start=True, stop=True,
                              skip_group_check=True).then_inc(q_acc[k], 1)

                def look(T):
                    s = T.slot(2)
                    for k in KEYS:
                        pe.wait_ge(q_tab[k], T.t + 1)
                        pe.matmul(pbase[k][0:NT, 0:P], OHhi[k][:, bass.ds(T.t, 1), :], OHlo[k][:, bass.ds(T.t, 1), :],
                                  start=False, stop=True, skip_group_check=True).then_inc(q_acc[k], 1)
                    for k in KEYS:
                        pe.wait_ge(q_hot[k], T.t + 1)
                        wait(pe, q_pos[k], T.t - 1)
                        pe.matmul(plook[k][s][:, 0:2 * P], OHhiT[k][s][:, :],
                                  table[k][s][:, :, :].rearrange("h q l -> h (q l)"), start=True, stop=True)
                        pe.wait_ge(q_early[k], T.t + 1)
                        pe.matmul(plook[k][s][:, 2 * P:2 * P + 1], earlier[k][s][:, :], ones_b[:, 0:1],
                                  start=True, stop=True, skip_group_check=True).then_inc(q_look[k], 1)

                def body(i):
                    for u in range(U):
                        at(i, u, 0, U, NT, look)

                pipeline(pe, GR, 0, 0, body)

        c12.close()
        scol = {k: sb("scol" + k, [P, 3, NT], F32) for k in KEYS}

        record = {k: sb("record" + k, [NT, P, 4], F32) for k in KEYS}
        rowT = {k: sb("rowT" + k, [NT, P + 1], F32) for k in KEYS}
        last = {k: sb("last" + k, [NT, P], F32) for k in KEYS}
        lastc = {"D": sb("lastcD", [P, NT], F32), "S": g.lastc}
        selrow = {k: sb("selrow" + k, [NT, SEL], I16) for k in KEYS}
        tmp_t = sb("tmpt", [NT, P], F32)
        deg_hi, deg_lo = sb("deghi", [NT, P], F32), sb("deglo", [NT, P], F32)
        tmp_c = sb("tmpc", [P, NT], F32)
        tmp_c2 = sb("tmpc2", [P, NT], F32)
        empty = sb("empty", [NT, P], F32)
        free = sb("free", [NT, P], F32)
        emptyc = sb("emptyc", [P, NT], F32)
        zrow = sb("zrow", [NT, P], F32)
        qrow = sb("qrow", [NT, P], F32)
        rank_c = {n: sb("rankc" + n, [P, NT], F32) for n in "zq"}
        rank_hi, rank_lo = g.rank_hi, g.rank_lo
        qi = sb("qi", [NT, P], I32)
        qhi16 = sb("qhi16", [NT, P], I16)
        with ExitStack() as c4:
            f = Env(nc, c4, "o_")
            ptr = {k: f.ps("ptr" + k, [P, 512]) for k in KEYS}
            plast = {k: f.ps("plast" + k, [P, 512]) for k in KEYS}
            pflag, prank = f.ps("pflag", [P, 512]), f.ps("prank", [P, 512])
            psum = f.ps("psum", [P, 512])
            o_v, o_pe, o_q = (f.sem(n) for n in ("o_v", "o_pe", "o_q"))
            o_sel, o_bc = ({k: f.sem(n + k) for k in KEYS} for n in ("o_sel", "o_bc"))
            o_ld = {k: f.sem("o_ld" + k) for k in KEYS}
            W = Weights(nc, f, g, [(0, io.L0_W1), (1, io.L0_W2)])
            block = c4.enter_context(f.block())
            marks = {}

            @block.vector
            def _(dve):
                n = [0]

                def step(ins, mark=None):
                    ins.then_inc(o_v, 1)
                    n[0] += 1
                    if mark:
                        marks[mark] = n[0]
                    dve.wait_ge(o_v, n[0])

                for m, k in enumerate(KEYS):
                    dve.wait_ge(o_ld[k], 32)
                    step(dve.tensor_copy(rowT[k][:, 0:P], record[k][:, :, 0]))
                    step(dve.tensor_tensor(last[k][:, :], rowT[k][:, 0:P], rowT[k][:, 1:P + 1], ALU.not_equal),
                         "last" + k)
                    step(dve.scalar_tensor_tensor(tmp_t[:, :], rowT[k][:, 0:P], 1.0, last[k][:, :],
                                                  ALU.add, ALU.mult))
                    step(dve.memset(selrow[k][:, P + 1:SEL], -1.0))
                    step(dve.tensor_copy(selrow[k][:, P:P + 1], rowT[k][:, P - 1:P]))
                    step(dve.tensor_scalar(selrow[k][:, 0:P], tmp_t[:, :], -1.0, None, ALU.add), "sel" + k)
                step(dve.tensor_copy(qi[:, :], record["D"][:, :, 2]))
                step(dve.tensor_scalar(qi[:, :], qi[:, :], P - 1, None, ALU.bitwise_and))
                step(dve.tensor_copy(deg_lo[:, :], qi[:, :]))
                step(dve.tensor_tensor(deg_hi[:, :], record["D"][:, :, 2], deg_lo[:, :], ALU.subtract), "degrees")
                for m, k in enumerate(KEYS):
                    dve.wait_ge(o_pe, m + 1)
                    step(dve.tensor_copy(scol[k][:, :, :], ptr[k][:, 0:3 * NT]))
                for m, k in enumerate(KEYS):
                    dve.wait_ge(o_pe, 3 + m)
                    step(dve.tensor_copy(lastc[k][:, :], plast[k][:, 0:NT]))
                    step(dve.tensor_copy(g.index[k][:, :, 0], scol[k][:, 1, :]))
                    step(dve.tensor_copy(g.index[k][:, :, 1], scol[k][:, 0, :]))
                    step(dve.tensor_scalar(tmp_c[:, :], lastc[k][:, :], float(-NOWHERE), float(NOWHERE),
                                           ALU.mult, ALU.add))
                    step(dve.tensor_tensor(tmp_c2[:, :], scol[k][:, 0, :], lastc[k][:, :], ALU.mult))
                    step(dve.tensor_tensor(g.index[k][:, :, 2], tmp_c[:, :], tmp_c2[:, :], ALU.add))
                    step(dve.tensor_copy(g.keycol[k][:, :], scol[k][:, 0, :]))
                step(dve.tensor_copy(g.degcol[:, :], scol["D"][:, 2, :]))
                step(dve.tensor_scalar(tmp_c[:, :], scol["S"][:, 2, :], 1.0, None, ALU.max))
                step(dve.reciprocal(g.rdeg[:, :], tmp_c[:, :]))
                step(dve.tensor_scalar(empty[:, :], count["S"][:, :], 0.0, None, ALU.is_equal), "empty")
                step(dve.tensor_scalar(free[:, :], last["S"][:, :], -1.0, 1.0, ALU.mult, ALU.add), "free")
                for m, (rows, out_row, name) in enumerate(((empty, zrow, "z"), (free, qrow, "q"))):
                    dve.wait_ge(o_pe, 5 + 3 * m)
                    step(dve.tensor_copy(colform[:, :], pflag[:, 0:NT]))
                    if name == "z":
                        step(dve.tensor_copy(emptyc[:, :], colform[:, :]))
                    step(dve.tensor_reduce(total[:, :], rows[:, :], AX.X, ALU.add))
                    step(dve.tensor_scalar(totals[:, :], ones_f[0:NT, :], total[:, 0:1], None, ALU.mult),
                         "totals" + name)
                    dve.wait_ge(o_pe, 6 + 3 * m)
                    step(dve.tensor_copy(out_row[:, :], psum[0:NT, 0:P]), "row" + name)
                    dve.wait_ge(o_pe, 7 + 3 * m)
                    step(dve.tensor_copy(rank_c[name][:, :], prank[:, 0:NT]), "col" + name)
                    step(dve.tensor_copy(tmp_i[:, :], rank_c[name][:, :]))
                    step(dve.tensor_scalar(node_i[:, :], tmp_i[:, :], 7, None, ALU.logical_shift_right))
                    step(dve.tensor_copy(rank_hi[name][:, :], node_i[:, :]))
                    step(dve.tensor_scalar(node_i[:, :], tmp_i[:, :], P - 1, None, ALU.bitwise_and))
                    step(dve.tensor_copy(rank_lo[name][:, :], node_i[:, :]))
                step(dve.tensor_scalar(g.minus_q[:, :], rank_lo["q"][:, :], -1.0, None, ALU.mult))
                step(dve.tensor_scalar(tmp_c[:, :], emptyc[:, :], 200.0, -200.0, ALU.mult, ALU.add))
                step(dve.tensor_tensor(rank_hi["z"][:, :], rank_hi["z"][:, :], tmp_c[:, :], ALU.add))
                step(dve.tensor_copy(qi[:, :], qrow[:, :]))
                step(dve.tensor_scalar(qi[:, :], qi[:, :], 7, None, ALU.logical_shift_right))
                step(dve.tensor_copy(qhi16[:, :], qi[:, :]), "qhi16")
                for m, k in enumerate(KEYS):
                    dve.wait_ge(o_bc[k], 16)
                    step(dve.tensor_copy(g.keylast[k][:, :], g.selrows[k][:, :, P]))
                    step(dve.memset(g.keyprev[k][:, 0:1], -2.0))
                    step(dve.tensor_copy(g.keyprev[k][:, 1:NT], g.keylast[k][:, 0:NT - 1]))
                for out, value in ((g.minus_prev, g.keyprev), (g.minus_key, g.keycol)):
                    step(dve.tensor_scalar(out[:, :], value["D"][:, :], -1.0, None, ALU.mult))
                step(dve.tensor_tensor(g.same_last[:, :], g.keylast["S"][:, :], g.keyprev["S"][:, :], ALU.is_equal))
                step(dve.tensor_tensor(tmp_c[:, :], g.keycol["S"][:, :], g.keyprev["S"][:, :], ALU.is_equal))
                step(dve.tensor_tensor(g.takes[:, :], tmp_c[:, :], lastc["S"][:, :], ALU.mult))
                step(dve.tensor_tensor(g.in_last[:, :], g.keycol["S"][:, :], g.keylast["S"][:, :], ALU.is_equal))

            @block.scalar
            def _(act):
                for m in range(2):
                    W.load_one(act, m)
                    W.split_high(act, m)

            @block.gpsimd
            def _(pool):
                for m in range(2):
                    W.split_low(pool, m)

            @block.tensor
            def _(pe):
                for k in KEYS:
                    pe.wait_ge(o_ld[k], 32)
                    for q in range(3):
                        ins = pe.transpose(ptr[k][:, q * NT:(q + 1) * NT], record[k][:, :, q], g.ident[0:NT, 0:NT])
                    ins.then_inc(o_pe, 1)
                for m, k in enumerate(KEYS):
                    pe.wait_ge(o_v, marks["last" + k])
                    pe.transpose(plast[k][:, 0:NT], last[k][:, :], g.ident[0:NT, 0:NT]).then_inc(o_pe, 1)
                for rows, out_row, name, mark in ((empty, zrow, "z", "empty"), (free, qrow, "q", "colz")):
                    pe.wait_ge(o_v, marks["free"])
                    pe.wait_ge(o_v, marks[mark])
                    pe.transpose(pflag[:, 0:NT], rows[:, :], g.ident[0:NT, 0:NT]).then_inc(o_pe, 1)
                    pe.wait_ge(o_v, marks["totals" + name])
                    pe.matmul(psum[0:NT, 0:P], colform[:, :], before_f[:, :], start=True, stop=False)
                    pe.matmul(psum[0:NT, 0:P], before_f[0:NT, 0:NT], totals[:, :], start=False, stop=True)\
                        .then_inc(o_pe, 1)
                    pe.wait_ge(o_v, marks["row" + name])
                    pe.transpose(prank[:, 0:NT], out_row[:, :], g.ident[0:NT, 0:NT]).then_inc(o_pe, 1)

            @block.sync
            def _(sp):
                for k in KEYS:
                    sp.dma_start(record[k][:, :, :], g.sorted[k][0:N, :].rearrange("(t j) q -> t j q", j=P))\
                        .then_inc(o_ld[k], 16)
                    sp.dma_start(rowT[k][:, P:P + 1], g.sorted[k][P:N + P, 0:1].rearrange("(t j) q -> t j q", j=P)[:, 0, :],
                                 allow_slow_non_contiguous=True).then_inc(o_ld[k], 16)
                for k in KEYS:
                    sp.wait_ge(o_ld[k], 32)
                for m, k in enumerate(KEYS):
                    sp.wait_ge(o_v, marks["sel" + k])
                    sp.dma_start(g.seldram[k], selrow[k][:, :]).then_inc(o_sel[k], 16)
                for k in KEYS:
                    sp.wait_ge(o_sel[k], 16)
                    sp.dma_start(g.selrows[k][:, :, :], g.seldram[k].partition_broadcast(P)).then_inc(o_bc[k], 16)
                sp.wait_ge(o_v, marks["degrees"])
                for copy in range(2):
                    sp.dma_start(g.lastdram[copy], last["S"][:, :]).then_inc(o_q, 16)
                    sp.dma_start(g.degdram[copy], deg_hi[:, :]).then_inc(o_q, 16)
                    sp.dma_start(g.degdram[2 + copy], deg_lo[:, :]).then_inc(o_q, 16)
                sp.wait_ge(o_v, marks["qhi16"])
                sp.dma_start(g.qdram, qhi16[:, :]).then_inc(o_q, 16)
                sp.wait_ge(o_q, 7 * 16)



class Weights:

    def __init__(self, nc, e, g, sources):
        self.nc, self.g, self.sources = nc, g, sources
        self.stage = e.sb("wstage", [P, C, D], F32)
        self.loaded, self.high, self.low = e.sem("w_loaded"), e.sem("w_high"), e.sem("w_low")

    def load(self, sp):
        for n in range(len(self.sources)):
            self.load_one(sp, n)

    def load_one(self, sp, n):
        wait(sp, self.low, n)
        sp.dma_start(self.stage[:, :, :], self.sources[n][1].rearrange("(c p) n -> p c n", p=P))\
            .then_inc(self.loaded, 16)

    def split_high(self, act, n):
        slot = self.sources[n][0]
        act.wait_ge(self.loaded, 16 * (n + 1))
        self.nc.scalar.copy(self.g.Whi[slot][:, :, :], self.stage[:, :, :]).then_inc(self.high, 1)

    def split_low(self, pool, n):
        slot = self.sources[n][0]
        pool.wait_ge(self.high, n + 1)
        pool.tensor_tensor(self.g.Wlo[slot][:, :, :], self.stage[:, :, :],
                           self.g.Whi[slot][:, :, :].bitcast(F32), ALU.subtract).then_inc(self.low, 1)


def selection(dve, g, k, T, sel, mask, sel_sem, mask_sem, sel_free, mask_done):
    s = T.slot(2)
    rows = g.selrows[k][:, bass.ds(T.t, 1), :]
    wait(dve, sel_free, T.t - 1)
    dve.tensor_scalar(sel[s][:, :], rows, g.keycol[k][:, bass.ds(T.t, 1)], None, ALU.is_equal).then_inc(sel_sem, 1)
    if mask is not None:
        wait(dve, mask_done, T.t - 1)
        dve.tensor_scalar(mask[s][:, :], rows, g.keyprev[k][:, bass.ds(T.t, 1)], None, ALU.is_equal)\
            .then_inc(mask_sem, 1)


def chunk(psum, c, cols):
    return psum[:, c // 2, (c % 2) * SEL:(c % 2) * SEL + cols]


def all_chunks(psum, first, cols):
    return psum[:, :, 0:2 * SEL].rearrange("p b (h w) -> p b h w", w=SEL)[:, :, :, first:first + cols]


def chunks_of(t):
    return t.rearrange("p (b h) n -> p b h n", b=2)


def carry_in(dve, T, psum, mask, carry, summed, mask_sem, done, copied):
    s, before = T.slot(2), (T.j - 1) % 2
    dve.wait_ge(summed, T.t + 1)
    dve.wait_ge(mask_sem, T.t + 1)
    wait(dve, copied, T.t)
    for c in range(C):
        ins = dve.scalar_tensor_tensor(chunk(psum[s], c, SEL), mask[s][:, :], carry[before][:, c:c + 1],
                                       chunk(psum[s], c, SEL), ALU.mult, ALU.add)
    ins.then_inc(done, 1)
    dve.wait_ge(done, T.t + 1)
    dve.tensor_copy(carry[s][:, :], all_chunks(psum[s], P, 1)).then_inc(copied, 1)


def product(pe, out, hi, lo, whi, wlo, start, stop):
    for c in range(C):
        ins = pe.matmul(out, hi[:, c, :], whi[:, c, :], start=start and c == 0, stop=False)
        ins = pe.matmul(out, hi[:, c, :], wlo[:, c, :], start=False, stop=False)
        ins = pe.matmul(out, lo[:, c, :], whi[:, c, :], start=False, stop=stop and c == C - 1)
    return ins


def indices(pool, g, k, T, col, n, tick, copied):
    s = T.slot(len(col))
    pool.sem_inc(tick, 1)
    pool.tensor_copy(col[s][:, 0:n], g.index[k][:, bass.ds(T.t, 1), 0:n]).then_inc(copied, 1)


def fetch(pool, out, table, index):
    return pool.indirect_dma_start(out, None, table, bass.IndirectOffsetOnAxis(ap=index, axis=0))


def put_rows(pool, table, index, rows, last_row):
    return pool.indirect_dma_start(table, bass.IndirectOffsetOnAxis(ap=index, axis=0), rows, None,
                                   bounds_check=last_row, oob_is_err=False)


class Norm:

    def __init__(self, e, name):
        self.stats = e.ring(name + "stats", 2, [P, 6], F32)
        self.mean_var = e.ring(name + "mv", 2, [P, 2], F32)
        self.var = e.ring(name + "var", 2, [P, 1], F32)
        self.s_stats, self.s_mean, self.s_var, self.s_scale, self.s_bias = (
            e.sem(name + n) for n in ("_stats", "_mean", "_var", "_scale", "_bias"))

    def statistics(self, dve, T, rows):
        dve.bn_stats(self.stats[T.slot(2)][:, :], rows).then_inc(self.s_stats, 1)

    def finish(self, dve, tick, T):
        s = T.slot(2)
        dve.wait_ge(self.s_stats, T.t + 1)
        dve.sem_inc(tick, 1)
        dve.bn_aggr(self.mean_var[s][:, :], self.stats[s][:, :]).then_inc(self.s_mean, 1)
        dve.wait_ge(self.s_mean, T.t + 1)
        wait(dve, self.s_scale, T.t - 1)
        dve.tensor_scalar(self.var[s][:, :], self.mean_var[s][:, 1:2], LN_EPS, None, ALU.add).then_inc(self.s_var, 1)

    def make_scale(self, pool, T, neg_half, scale):
        pool.wait_ge(self.s_var, T.t + 1)
        pool.tensor_tensor(scale, self.var[T.slot(2)][:, :], neg_half[:, :], ALU.pow).then_inc(self.s_scale, 1)

    def make_bias(self, pool, tick, T, scale, bias):
        pool.wait_ge(self.s_scale, T.t + 1)
        pool.sem_inc(tick, 1)
        pool.tensor_scalar(bias, self.mean_var[T.slot(2)][:, 0:1], scale, -1.0, ALU.mult, ALU.mult)\
            .then_inc(self.s_bias, 1)


def stack_bias(dve, g, wide, hi, out, prep, n):
    rows = wide.shape[0]
    pick = g.hilo[0:rows, :]
    dve.tensor_tensor(wide[:, :], wide[:, :], hi[:, :], ALU.subtract).then_inc(prep, 1)
    dve.wait_ge(prep, n + 1)
    dve.tensor_scalar(wide[:, :], wide[:, :], pick[:, 1:2], None, ALU.mult).then_inc(prep, 1)
    dve.wait_ge(prep, n + 2)
    dve.scalar_tensor_tensor(out[:, :], hi[:, :], pick[:, 0:1], wide[:, :], ALU.mult, ALU.add).then_inc(prep, 1)



def layer0(nc, io, g, second):
    NT, N = g.NT, g.N
    U = 4
    GR = NT // U
    with ExitStack() as ctx:
        e = Env(nc, ctx, "b_" if second else "a_")
        src, slot, bias = (g.h1, 1, io.L0_b2) if second else (g.xs[0], 0, io.L0_b1)
        if second:
            bf, br, bstack = e.sb("bf", [4, D], F32), e.sb("br", [4, D], F32R), e.sb("bstack", [4, D], F32R)
            degrees = e.ring("degrees", 2, [4, P], F32R)
            s_deg, s_hi, s_prep = e.sems("s_deg", 2), e.sem("s_hi"), e.sem("s_prep")
        else:
            brow = e.sb("brow", [P, D], F32)
        neg_half = e.sb("neghalf", [P, 1], F32)
        col, colx = e.ring("col", U, [P, 3], I32), e.ring("colx", U, [P, 3], I32)
        G = e.ring("G", U, [P, D if second else EXT], F32)
        sel, mask = e.ring("sel", 2, [P, SEL], F32), e.ring("mask", 2, [P, SEL], F32)
        carry = e.ring("carry", 2, [P, C], F32)
        Thi, Tlo = e.ring("Thi", 2, [P, C, P], F32R), e.ring("Tlo", 2, [P, C, P], F32R)
        rows = e.ring("rows", 2, [P, EXT if second else D], F32)
        xr = e.ring("xr", U, [P, D], F32) if second else None
        ln = Norm(e, "ln") if second else None
        W = None if second else Weights(nc, e, g, [(2, io.L1_W1), (3, io.L1_W2)])
        psum_t = [e.ps(f"pt{i}", [P, 2, 512]) for i in range(2)]
        psum_o = [e.ps(f"po{i}", [P, D]) for i in range(2)]
        if second:
            qrow16 = e.sb("qrow16", [NT, N], I16)
            one_f = e.sb("onef", [P, 1], F32)
            square, column_square = e.sb("square", [NT, P], F32), e.sb("columnsquare", [P, P], F32)
            hotT, hotq = e.ring("hott", 2, [NT, P], F32), e.ring("hotq", 2, [P, P], F32)
            picked, found = e.sb("picked", [P, P], F32), e.sb("found", [P, NT], F32)
            psum_l = [e.ps(f"pl{i}", [P, 512]) for i in range(2)]
            e_ld, e_square, e_column, e_hot, e_hotq, e_look, e_pick, e_fin = (
                e.sem(n) for n in ("e_ld", "e_square", "e_column", "e_hot", "e_hotq", "e_look", "e_pick", "e_fin"))
        else:
            hot_hi, hot_lo = e.ring("hothi", 2, [P, NT], F32), e.ring("hotlo", 2, [P, P], F32)
            psum_list = e.ps("plist", [P, 512])
            e_made, e_put = e.sem("e_made"), e.sem("e_put")

        s_brow, s_const = e.sem("s_brow"), e.sem("s_const")
        s_col, s_colx = e.sem("s_col"), e.sem("s_colx")
        s_Gn = e.sem("s_Gn")
        s_G, s_x, s_put = e.sems("s_G", U), e.sems("s_x", U), e.sems("s_put", U)
        s_sel, s_mask = e.sem("s_sel"), e.sem("s_mask")
        s_summed, s_carried, s_copied = e.sem("s_summed"), e.sem("s_carried"), e.sem("s_copied")
        s_Thi, s_Tlo = e.sem("s_Thi"), e.sem("s_Tlo")
        s_prod, s_biased, s_rows = e.sem("s_prod"), e.sem("s_biased"), e.sem("s_rows")
        if second:
            row_square = {s_sel: e.sb("selsquare", [P, SEL], F32), s_mask: e.sb("masksquare", [P, SEL], F32)}
            e_square_of = {s_sel: e.sem("e_selsquare"), s_mask: e.sem("e_masksquare")}
        tick = e.sem("tick")
        block = ctx.enter_context(e.block())

        @block.sync
        def _(sp):
            b, rows_of_b = (bf, 4) if second else (brow, P)
            sp.dma_start(b[:, :], bias.partition_broadcast(rows_of_b)).then_inc(s_brow, 16)
            if W:
                W.load(sp)
            else:
                sp.dma_start(qrow16[:, :], g.qdram.rearrange("t j -> (t j)").partition_broadcast(NT)).then_inc(e_ld, 16)
                sp.wait_ge(e_ld, 16)
            sp.wait_ge(s_brow, 16)

            def load_degrees(T):
                s = T.slot(2)
                wait(sp, s_prod, T.t - 1)
                sp.sem_inc(tick, 1)
                sp.dma_start(degrees[s][:, :].bitcast(F32), g.degdram[:, bass.ds(T.t, 1), :]).then_inc(s_deg[s], 16)

            def body(i):
                for u in range(U):
                    at(i, u, 2, U, NT, load_degrees)

            if second:
                pipeline(sp, GR, 1, 0, body)

        @block.gpsimd
        def _(pool):
            def start_fetch(T):
                s = T.slot(U)
                wait(pool, s_summed, T.t - 3)
                indices(pool, g, "D", T, col, 1, tick, s_col)
                pool.wait_ge(s_col, T.t + 1)
                pool.sem_inc(tick, 1)
                fetch(pool, G[s][:, :], src, col[s][:, 0:1]).then_inc(s_G[s], 16)

            def residual(T):
                s = T.slot(U)
                wait(pool, s_rows, T.t - 3)
                wait(pool, s_put[s], 16 * T.use(U))
                indices(pool, g, "D", T, colx, 3, tick, s_colx)
                if second:
                    pool.wait_ge(s_colx, T.t + 1)
                    pool.sem_inc(tick, 1)
                    fetch(pool, xr[s][:, :], io.x, colx[s][:, 1:2]).then_inc(s_x[s], 16)

            def store(T):
                s = T.slot(U)
                if second:
                    row = rows[T.slot(2)]
                    ln.make_scale(pool, T, neg_half, row[:, SCALE:SCALE + 1])
                    ln.make_bias(pool, tick, T, row[:, SCALE:SCALE + 1], row[:, BIAS:BIAS + 1])
                pool.wait_ge(s_colx, T.t + 1)
                pool.wait_ge(ln.s_bias if second else s_rows, T.t + 1)
                pool.sem_inc(tick, 1)
                put_rows(pool, g.xs[0] if second else g.h1, colx[s][:, 2:3], rows[T.slot(2)][:, :], N - 1)\
                    .then_inc(s_put[s], 16)

            def body(i):
                for u in range(U):
                    at(i, u, -2, U, NT, store)
                    at(i, u, 4, U, NT, start_fetch)
                    at(i, u, 1, U, NT, residual)

            if second:
                pool.memset(one_f[:, :], 1.0)
            pool.memset(neg_half[:, :], -0.5).then_inc(s_const, 1)
            for s in range(2):
                pool.memset(carry[s][:, :], 0.0).then_inc(s_const, 1)
                if second:
                    pool.memset(rows[s][:, BIAS + 1:EXT], 0.0).then_inc(s_const, 1)
            pool.wait_ge(s_const, 5 if second else 3)
            pipeline(pool, GR, 1, 1, body, between=W and (lambda n: W.split_low(pool, n)))
            for s in range(U):
                pool.wait_ge(s_put[s], 16 * GR)

        @block.scalar
        def _(act):
            def norm_in(T):
                s = T.slot(U)
                act.wait_ge(s_G[s], 16 * (T.use(U) + 1))
                nc.scalar.activation(G[s][:, 0:D], G[s][:, 0:D], ACT.Relu, bias=G[s][:, BIAS:BIAS + 1],
                                     scale=G[s][:, SCALE:SCALE + 1]).then_inc(s_Gn, 1)

            def high_sum(T):
                s = T.slot(2)
                act.wait_ge(s_copied, T.t + 1)
                wait(act, s_prod, T.t - 1)
                nc.scalar.copy(chunks_of(Thi[s]), all_chunks(psum_t[s], 0, P)).then_inc(s_Thi, 1)

            def hot_row(T):
                s = T.slot(2)
                wait(act, e_hot, T.t)
                act.sem_inc(tick, 1)
                nc.scalar.activation(square[:, :], qrow16[:, bass.ds(T.t * P, P)], ACT.Square,
                                     bias=g.minus_p[0:NT, 0:1]).then_inc(e_square, 1)
                act.wait_ge(e_square, T.t + 1)
                wait(act, e_look, T.t - 1)
                nc.scalar.activation(hotT[s][:, :], square[:, :], ACT.Relu, bias=one_f[0:NT, 0:1], scale=-1.0)\
                    .then_inc(e_hot, 1)

            def select_row(T, minus, out, used, made):
                s, one = T.slot(2), bass.ds(T.t, 1)
                wait(act, made, T.t)
                act.sem_inc(tick, 1)
                nc.scalar.activation(row_square[made][:, :], g.selrows["D"][:, one, :], ACT.Square,
                                     bias=minus[:, one]).then_inc(e_square_of[made], 1)
                act.wait_ge(e_square_of[made], T.t + 1)
                wait(act, used, T.t - 1)
                nc.scalar.activation(out[s][:, :], row_square[made][:, :], ACT.Relu, bias=one_f[:, 0:1],
                                     scale=-1.0).then_inc(made, 1)

            def mask_row(T):
                select_row(T, g.minus_prev, mask, s_carried, s_mask)

            def sel_row(T):
                select_row(T, g.minus_key, sel, s_summed, s_sel)

            def hot_column(T):
                s = T.slot(2)
                wait(act, e_hotq, T.t)
                act.sem_inc(tick, 1)
                nc.scalar.activation(column_square[:, :], g.iota_f[:, :], ACT.Square,
                                     bias=g.minus_q[:, bass.ds(T.t, 1)]).then_inc(e_column, 1)
                act.wait_ge(e_column, T.t + 1)
                wait(act, e_pick, T.t - 1)
                nc.scalar.activation(hotq[s][:, :], column_square[:, :], ACT.Relu, bias=one_f[:, 0:1], scale=-1.0)\
                    .then_inc(e_hotq, 1)

            def relu(T):
                s, store_before = T.slot(2), (T.j - 2) % U
                act.wait_ge(s_biased, T.t + 1)
                wait(act, s_put[store_before], 16 * (T.k + 1 if T.j >= 2 else T.k))
                nc.scalar.activation(rows[s][:, :], psum_o[s][:, :], ACT.Relu).then_inc(s_rows, 1)

            def body(i):
                for u in range(U):
                    if not second:
                        at(i, u, -1, U, NT, relu)
                    at(i, u, 1, U, NT, high_sum)
                    if second:
                        at(i, u, 1, U, NT, hot_row)
                        at(i, u, 2, U, NT, mask_row)
                        at(i, u, 3, U, NT, sel_row)
                        at(i, u, 0, U, NT, hot_column)
                    else:
                        at(i, u, 3, U, NT, norm_in)

            if second:
                act.wait_ge(s_brow, 16)
                nc.scalar.copy(br[:, :], bf[:, :]).then_inc(s_hi, 1)
                act.wait_ge(e_ld, 16)
                act.wait_ge(s_const, 5)
            pipeline(act, GR, 1, 1, body, between=W and (lambda n: W.split_high(act, n)))

        @block.vector
        def _(dve):
            def select(T):
                selection(dve, g, "D", T, sel, mask, s_sel, s_mask, s_summed, s_carried)

            def carried(T):
                carry_in(dve, T, psum_t, mask, carry, s_summed, s_mask, s_carried, s_copied)

            def low_sum(T):
                s = T.slot(2)
                dve.wait_ge(s_Thi, T.t + 1)
                dve.tensor_tensor(chunks_of(Tlo[s]), all_chunks(psum_t[s], 0, P), chunks_of(Thi[s]).bitcast(F32),
                                  ALU.subtract).then_inc(s_Tlo, 1)

            def add_bias(T):
                s = T.slot(2)
                dve.wait_ge(s_prod, T.t + 1)
                dve.scalar_tensor_tensor(psum_o[s][:, :], brow[:, :], g.degcol[:, bass.ds(T.t, 1)], psum_o[s][:, :],
                                         ALU.mult, ALU.add).then_inc(s_biased, 1)

            def add_x(T):
                s, store_before = T.slot(2), (T.j - 2) % U
                dve.wait_ge(s_prod, T.t + 1)
                dve.wait_ge(s_x[T.slot(U)], 16 * (T.use(U) + 1))
                wait(dve, s_put[store_before], 16 * (T.k + 1 if T.j >= 2 else T.k))
                dve.scalar_tensor_tensor(rows[s][:, 0:D], psum_o[s][:, :], 0.0, xr[T.slot(U)][:, :],
                                         ALU.max, ALU.add).then_inc(s_rows, 1)

            def norm_rows(T):
                dve.wait_ge(s_rows, T.t + 1)
                ln.statistics(dve, T, rows[T.slot(2)][:, 0:D])

            def finish_rows(T):
                wait(dve, ln.s_bias, T.t - 1)
                ln.finish(dve, tick, T)

            def list_nodes(T):
                s, one = T.slot(2), bass.ds(T.t, 1)
                wait(dve, e_put, T.t - 1)
                dve.tensor_scalar(hot_hi[s][:, :], g.iota_f[:, 0:NT], g.rank_hi["z"][:, one], None, ALU.is_equal)
                dve.tensor_scalar(hot_lo[s][:, :], g.iota_f[:, :], g.rank_lo["z"][:, one], g.node_f[:, one],
                                  ALU.is_equal, ALU.mult).then_inc(e_made, 1)

            def pick_node(T):
                s = T.slot(2)
                dve.wait_ge(e_look, T.t + 1)
                dve.wait_ge(e_hotq, T.t + 1)
                wait(dve, e_pick, T.t)
                dve.scalar_tensor_tensor(picked[:, :], psum_l[s][:, 0:P], 1.0, hotq[s][:, :], ALU.mult, ALU.mult,
                                         accum_out=found[:, bass.ds(T.t, 1)]).then_inc(e_pick, 1)

            def body(i):
                for u in range(U):
                    if not second:
                        at(i, u, -1, U, NT, add_bias)
                    at(i, u, 1, U, NT, carried)
                    if second:
                        at(i, u, -1, U, NT, add_x)
                    else:
                        at(i, u, 1, U, NT, list_nodes)
                        at(i, u, 3, U, NT, select)
                    at(i, u, 1, U, NT, low_sum)
                    if second:
                        at(i, u, -1, U, NT, norm_rows)
                    if second:
                        at(i, u, -1, U, NT, finish_rows)
                        at(i, u, -1, U, NT, pick_node)

            dve.wait_ge(s_brow, 16)
            dve.wait_ge(s_const, 5 if second else 3)
            if second:
                dve.wait_ge(s_hi, 1)
                stack_bias(dve, g, bf, br[:, :].bitcast(F32), bstack, s_prep, 0)
            pipeline(dve, GR, 1, 1, body)
            if not second:
                dve.wait_ge(e_put, NT)
                dve.tensor_copy(g.listed[:, :], psum_list[0:NT, 0:P])
            else:
                n = [0]

                def step(ins):
                    ins.then_inc(e_fin, 1)
                    n[0] += 1
                    dve.wait_ge(e_fin, n[0])

                dve.wait_ge(e_pick, NT)
                key = g.keycol["S"]
                step(dve.tensor_tensor(picked[:, 0:NT], key[:, :], found[:, :], ALU.subtract))
                step(dve.tensor_tensor(picked[:, 0:NT], picked[:, 0:NT], g.lastc[:, :], ALU.mult))
                step(dve.tensor_tensor(g.index["S"][:, :, 2], picked[:, 0:NT], found[:, :], ALU.add))

        @block.tensor
        def _(pe):
            def sum_edges(T):
                s = T.slot(2)
                pe.wait_ge(s_sel, T.t + 1)
                if second:
                    pe.wait_ge(s_G[T.slot(U)], 16 * (T.use(U) + 1))
                else:
                    pe.wait_ge(s_Gn, T.t + 1)
                wait(pe, s_Tlo, T.t - 1)
                for c in range(C):
                    ins = pe.matmul(chunk(psum_t[s], c, SEL), G[T.slot(U)][:, c * P:(c + 1) * P], sel[s][:, :],
                                    start=True, stop=True)
                ins.then_inc(s_summed, 1)

            def multiply(T):
                s = T.slot(2)
                pe.wait_ge(s_Tlo, T.t + 1)
                wait(pe, s_rows, T.t - 1)
                if second:
                    pe.wait_ge(s_deg[s], 16 * (T.use(2) + 1))
                    pe.matmul(psum_o[s][:, :], degrees[s][:, :], bstack[:, :], start=True, stop=False)
                product(pe, psum_o[s][:, :], Thi[s], Tlo[s], g.Whi[slot], g.Wlo[slot], not second, True)\
                    .then_inc(s_prod, 1)

            def put(T):
                s = T.slot(2)
                pe.wait_ge(e_made, T.t + 1)
                pe.matmul(psum_list[0:NT, 0:P], hot_hi[s][:, :], hot_lo[s][:, :],
                          start=isinstance(T.t, int) and T.t == 0,
                          stop=isinstance(T.t, int) and T.t == NT - 1).then_inc(e_put, 1)

            def look(T):
                s = T.slot(2)
                pe.wait_ge(e_hot, T.t + 1)
                wait(pe, e_pick, T.t - 1)
                pe.matmul(psum_l[s][:, 0:P], hotT[s][:, :], g.listed[:, :], start=True, stop=True).then_inc(e_look, 1)

            def body(i):
                for u in range(U):
                    at(i, u, 1, U, NT, sum_edges)
                    at(i, u, 0, U, NT, multiply)
                    at(i, u, 0, U, NT, look if second else put)

            if second:
                pe.wait_ge(s_prep, 3)
            pipeline(pe, GR, 1, 0, body)



def layer1(nc, io, g):
    NT, N = g.NT, g.N
    U = 4
    GR = NT // U
    PAIRS = NT // 2
    RX = 8
    with ExitStack() as ctx:
        e = Env(nc, ctx, "c_")
        src, out = g.xs[0], g.xs[1]
        W = Weights(nc, e, g, [(0, io.L2_Wn), (1, io.L2_Ws)])
        gamma, beta = e.sb("gamma", [P, D], F32), e.sb("beta", [P, D], F32)
        neg_half = e.sb("neghalf", [P, 1], F32)
        b1col = e.sb("b1col", [P, C], F32)
        b2f, b2r, b2 = e.sb("b2f", [2, D], F32), e.sb("b2r", [2, D], F32R), e.sb("b2", [2, D], F32R)
        ones1 = e.sb("ones1", [2, P], F32R)
        ones_f = e.sb("onesf", [2, P], F32)
        eps1 = e.sb("eps1", [P, 1], F32)
        eye = e.sb("eye", [P, P], F32)
        col, colx = e.ring("col", U, [P, 3], I32), e.ring("colx", 2, [P, 3], I32)
        G, X = e.ring("G", U, [P, EXT], F32), e.ring("X", U, [P, EXT], F32)
        H = e.ring("H", 2, [P, D], F32)
        XB = e.sb("XB", [P, RX, D], F32)
        sel, mask = e.ring("sel", 2, [P, SEL], F32), e.ring("mask", 2, [P, SEL], F32)
        carry = e.ring("carry", 2, [P, C], F32)
        Zhi, Zlo = e.sb("Zhi", [P, C, 2 * P], F32R), e.sb("Zlo", [P, C, 2 * P], F32R)
        Uhi, Ulo = e.ring("Uhi", 2, [P, C, 2 * P], F32R), e.ring("Ulo", 2, [P, C, 2 * P], F32R)
        rows = e.ring("rows", 2, [P, EXT], F32)
        ylen = e.ring("ylen", 2, [P, 1], F32)
        ln_y, ln_x = Norm(e, "lny"), Norm(e, "lnx")
        psum_t = [e.ps(f"pt{i}", [P, 2, 512]) for i in range(2)]
        psum_u = e.ps("pu", [P, C, 2 * P])
        psum_o = [e.ps(f"po{i}", [P, D]) for i in range(2)]

        s_load, s_const, s_hi, s_prep = (e.sem(n) for n in ("s_load", "s_const", "s_hi", "s_prep"))
        s_col, s_colx = e.sem("s_col"), e.sem("s_colx")
        s_G, s_X, s_put = e.sems("s_G", U), e.sems("s_X", U), e.sems("s_put", 2)
        s_Gn, s_H, s_XB = (e.sem(n) for n in ("s_Gn", "s_H", "s_XB"))
        s_sel, s_mask = e.sem("s_sel"), e.sem("s_mask")
        s_summed, s_carried, s_copied = e.sem("s_summed"), e.sem("s_carried"), e.sem("s_copied")
        s_Zhi, s_Zlo = e.sem("s_Zhi"), e.sem("s_Zlo")
        s_u, s_relu, s_Uhi, s_Ulo = (e.sem(n) for n in ("s_u", "s_relu", "s_Uhi", "s_Ulo"))
        s_prod, s_cent, s_rows = e.sem("s_prod"), e.sem("s_cent"), e.sem("s_rows")
        tick = e.sem("tick")
        block = ctx.enter_context(e.block())

        @block.sync
        def _(sp):
            sp.dma_start(gamma[:, :], io.L1_gamma.partition_broadcast(P)).then_inc(s_load, 16)
            sp.dma_start(beta[:, :], io.L1_beta.partition_broadcast(P)).then_inc(s_load, 16)
            sp.dma_start(b1col[:, :], io.L1_b1col).then_inc(s_load, 16)
            sp.dma_start(b2f[:, :], io.L1_b2.partition_broadcast(2)).then_inc(s_load, 16)
            sp.dma_start(eps1[:, :], io.eps.partition_broadcast(P)).then_inc(s_load, 16)
            W.load(sp)
            sp.wait_ge(s_load, 80)

        @block.gpsimd
        def _(pool):
            def start_fetch(T):
                s = T.slot(U)
                wait(pool, s_summed, T.t - 3)
                wait(pool, s_H, T.t - 3)
                wait(pool, s_XB, T.t - 3)
                indices(pool, g, "S", T, col, 3, tick, s_col)
                pool.wait_ge(s_col, T.t + 1)
                pool.sem_inc(tick, 1)
                fetch(pool, G[s][:, :], src, col[s][:, 0:1]).then_inc(s_G[s], 16)
                fetch(pool, X[s][:, :], src, col[s][:, 2:3]).then_inc(s_X[s], 16)

            def keep_x(T):
                s = T.slot(U)
                pool.wait_ge(s_X[s], 16 * (T.use(U) + 1))
                wait(pool, s_rows, T.t - RX + 1)
                pool.sem_inc(tick, 1)
                pool.tensor_tensor(XB[:, bass.ds(T.t % RX, 1), :], X[s][:, 0:D], beta[:, :], ALU.add)\
                    .then_inc(s_XB, 1)

            def length_y(T):
                wait(pool, s_rows, T.t - 1)
                ln_y.make_scale(pool, T, neg_half, ylen[T.slot(2)][:, :])

            def store(T):
                s = T.slot(2)
                wait(pool, s_put[s], 16 * T.use(2))
                ln_x.make_scale(pool, T, neg_half, rows[s][:, SCALE:SCALE + 1])
                indices(pool, g, "S", T, colx, 3, tick, s_colx)
                ln_x.make_bias(pool, tick, T, rows[s][:, SCALE:SCALE + 1], rows[s][:, BIAS:BIAS + 1])
                pool.wait_ge(s_colx, T.t + 1)
                pool.wait_ge(ln_x.s_bias, T.t + 1)
                pool.sem_inc(tick, 1)
                put_rows(pool, out, colx[s][:, 2:3], rows[s][:, :], N - 1).then_inc(s_put[s], 16)

            def body(i):
                for pair in (0, 2):
                    at(i, pair, 4, U, NT, keep_x)
                    for u in (pair, pair + 1):
                        at(i, u, -2, U, NT, length_y)
                    at(i, pair + 1, 4, U, NT, keep_x)
                    for u in (pair, pair + 1):
                        at(i, u, -2, U, NT, store)
                    for u in (pair, pair + 1):
                        at(i, u, 8, U, NT, start_fetch)

            pool.memset(ones_f[:, :], 1.0).then_inc(s_const, 1)
            pool.memset(neg_half[:, :], -0.5).then_inc(s_const, 1)
            for s in range(2):
                pool.memset(carry[s][:, :], 0.0).then_inc(s_const, 1)
                pool.memset(rows[s][:, BIAS + 1:EXT], 0.0).then_inc(s_const, 1)
            pool.wait_ge(s_const, 6)
            pool.wait_ge(s_load, 80)
            pipeline(pool, GR, 2, 1, body, ahead=2, between=lambda n: W.split_low(pool, n))
            for s in range(2):
                pool.wait_ge(s_put[s], 16 * (NT // 2))

        @block.scalar
        def _(act):
            def norm_in(T):
                s = T.slot(U)
                act.wait_ge(s_G[s], 16 * (T.use(U) + 1))
                nc.scalar.activation(G[s][:, 0:D], G[s][:, 0:D], ACT.Relu, bias=G[s][:, BIAS:BIAS + 1],
                                     scale=G[s][:, SCALE:SCALE + 1]).then_inc(s_Gn, 1)
                act.wait_ge(s_X[s], 16 * (T.use(U) + 1))
                wait(act, s_summed, T.t - 1)
                nc.scalar.activation(H[T.slot(2)][:, :], X[s][:, 0:D], ACT.Relu, bias=X[s][:, BIAS:BIAS + 1],
                                     scale=X[s][:, SCALE:SCALE + 1]).then_inc(s_H, 1)

            def high_sum(T):
                s = T.slot(2)
                act.wait_ge(s_copied, T.t + 1)
                wait(act, s_u, T.use(2))
                nc.scalar.copy(chunks_of(Zhi[:, :, s * P:(s + 1) * P]), all_chunks(psum_t[s], 0, P))\
                    .then_inc(s_Zhi, 1)

            def relu(T):
                act.wait_ge(s_u, T.t + 1)
                for c in range(C):
                    ins = nc.scalar.activation(psum_u[:, c, :], psum_u[:, c, :], ACT.Relu, bias=b1col[:, c:c + 1])
                ins.then_inc(s_relu, 1)
                act.wait_ge(s_relu, T.t + 1)
                wait(act, s_prod, 2 * (T.t - 1))
                nc.scalar.copy(Uhi[T.slot(2)][:, :, :], psum_u[:, :, :]).then_inc(s_Uhi, 1)

            def body(i):
                for pair in (0, 2):
                    at(i, pair // 2, 1, 2, PAIRS, relu)
                    for u in (pair, pair + 1):
                        at(i, u, 4, U, NT, high_sum)
                    for u in (pair, pair + 1):
                        at(i, u, 6, U, NT, norm_in)

            act.wait_ge(s_load, 80)
            nc.scalar.copy(b2r[:, :], b2f[:, :]).then_inc(s_hi, 1)
            act.wait_ge(s_const, 1)
            nc.scalar.copy(ones1[:, :], ones_f[:, :]).then_inc(s_hi, 1)
            pipeline(act, GR, 2, 0, body, between=lambda n: W.split_high(act, n))

        @block.vector
        def _(dve):
            def low_u(T):
                dve.wait_ge(s_Uhi, T.t + 1)
                dve.tensor_tensor(Ulo[T.slot(2)][:, :, :], psum_u[:, :, :], Uhi[T.slot(2)][:, :, :].bitcast(F32),
                                  ALU.subtract).then_inc(s_Ulo, 1)

            def carried(T):
                carry_in(dve, T, psum_t, mask, carry, s_summed, s_mask, s_carried, s_copied)

            def low_sum(T):
                s = T.slot(2)
                dve.wait_ge(s_Zhi, T.t + 1)
                half = slice(s * P, (s + 1) * P)
                dve.tensor_tensor(chunks_of(Zlo[:, :, half]), all_chunks(psum_t[s], 0, P),
                                  chunks_of(Zhi[:, :, half]).bitcast(F32), ALU.subtract).then_inc(s_Zlo, 1)

            def select(T):
                selection(dve, g, "S", T, sel, mask, s_sel, s_mask, s_summed, s_carried)

            def norm_y(T):
                dve.wait_ge(s_prod, T.t + 1)
                ln_y.statistics(dve, T, psum_o[T.slot(2)][:, :])

            def center(T):
                s = T.slot(2)
                ln_y.finish(dve, tick, T)
                dve.scalar_tensor_tensor(psum_o[s][:, :], psum_o[s][:, :], ln_y.mean_var[s][:, 0:1], gamma[:, :],
                                         ALU.subtract, ALU.mult).then_inc(s_cent, 1)

            def new_rows(T):
                s = T.slot(2)
                dve.wait_ge(s_cent, T.t + 1)
                dve.wait_ge(ln_y.s_scale, T.t + 1)
                dve.wait_ge(s_XB, T.t + 1)
                wait(dve, s_put[s], 16 * T.use(2))
                dve.scalar_tensor_tensor(rows[s][:, 0:D], psum_o[s][:, :], ylen[s][:, 0:1],
                                         XB[:, bass.ds(T.t % RX, 1), :], ALU.mult, ALU.add).then_inc(s_rows, 1)

            def norm_rows(T):
                dve.wait_ge(s_rows, T.t + 1)
                ln_x.statistics(dve, T, rows[T.slot(2)][:, 0:D])

            def finish_rows(T):
                wait(dve, ln_x.s_bias, T.t - 1)
                ln_x.finish(dve, tick, T)

            def body(i):
                for pair in (0, 2):
                    for stage in (norm_y, center, new_rows, norm_rows, finish_rows):
                        for u in (pair, pair + 1):
                            at(i, u, -2, U, NT, stage)
                    at(i, pair, 4, U, NT, carried)
                    at(i, pair // 2, 1, 2, PAIRS, low_u)
                    at(i, pair, 4, U, NT, low_sum)
                    at(i, pair + 1, 4, U, NT, carried)
                    at(i, pair + 1, 4, U, NT, low_sum)
                    for u in (pair, pair + 1):
                        at(i, u, 6, U, NT, select)

            dve.wait_ge(s_load, 80)
            dve.wait_ge(s_const, 6)
            dve.wait_ge(s_hi, 1)
            stack_bias(dve, g, b2f, b2r[:, :].bitcast(F32), b2, s_prep, 0)
            dve.tensor_scalar(eps1[:, :], eps1[:, :], 1.0, None, ALU.add).then_inc(s_prep, 1)
            dve.wait_ge(s_prep, 4)
            dve.tensor_scalar(eye[:, :], g.ident[:, :], eps1[:, 0:1], None, ALU.mult).then_inc(s_prep, 1)
            pipeline(dve, GR, 2, 1, body)

        @block.tensor
        def _(pe):
            def sum_edges(T):
                s = T.slot(2)
                pe.wait_ge(s_sel, T.t + 1)
                pe.wait_ge(s_Gn, T.t + 1)
                pe.wait_ge(s_H, T.t + 1)
                wait(pe, s_Zlo, T.t - 1)
                for c in range(C):
                    cols = slice(c * P, (c + 1) * P)
                    pe.matmul(chunk(psum_t[s], c, SEL), G[T.slot(U)][:, cols], sel[s][:, :], start=True, stop=False)
                    ins = pe.matmul(chunk(psum_t[s], c, P), H[s][:, cols], eye[:, :], start=False, stop=True)
                ins.then_inc(s_summed, 1)

            def first(T):
                pe.wait_ge(s_Zlo, 2 * T.t + 2)
                wait(pe, s_Ulo, T.t)
                for o in range(C):
                    cols = slice(o * P, (o + 1) * P)
                    for c in range(C):
                        pe.matmul(psum_u[:, o, :], g.Whi[2][:, c, cols], Zhi[:, c, :], start=c == 0, stop=False)
                        pe.matmul(psum_u[:, o, :], g.Whi[2][:, c, cols], Zlo[:, c, :], start=False, stop=False)
                        ins = pe.matmul(psum_u[:, o, :], g.Wlo[2][:, c, cols], Zhi[:, c, :], start=False,
                                        stop=c == C - 1)
                ins.then_inc(s_u, 1)

            def second(T):
                s, pair = T.slot(2), T.j // 2
                pe.wait_ge(s_Ulo, T.use(2) + 1)
                wait(pe, s_rows, T.t - 1)
                half = slice(s * P, (s + 1) * P)
                pe.matmul(psum_o[s][:, :], ones1[:, :], b2[:, :], start=True, stop=False)
                product(pe, psum_o[s][:, :], Uhi[pair][:, :, half], Ulo[pair][:, :, half], g.Whi[3], g.Wlo[3],
                        False, True).then_inc(s_prod, 1)

            def body(i):
                for pair in (0, 2):
                    at(i, pair // 2, 1, 2, PAIRS, first)
                    for u in (pair, pair + 1):
                        at(i, u, 4, U, NT, sum_edges)
                    for u in (pair, pair + 1):
                        at(i, u, 0, U, NT, second)

            pe.wait_ge(s_hi, 2)
            pe.wait_ge(s_prep, 5)
            pipeline(pe, GR, 2, 0, body)



def layer2(nc, io, g):
    NT, N = g.NT, g.N
    U = 4
    GR = NT // U
    with ExitStack() as ctx:
        e = Env(nc, ctx, "d_")
        src, out = g.xs[1], g.xs[2]
        W = Weights(nc, e, g, [(2, io.L3_W[0:D, :]), (3, io.L3_W[D:2 * D, :])])
        gamma, beta = e.sb("gamma", [P, D], F32), e.sb("beta", [P, D], F32)
        neg_half = e.sb("neghalf", [P, 1], F32)
        bf, br, bias = e.sb("bf", [4, D], F32), e.sb("br", [4, D], F32R), e.sb("bias", [4, D], F32R)
        has = e.ring("has", 2, [4, P], F32R)
        ones_f = e.sb("onesf", [4, P], F32)
        col, colx = e.ring("col", U, [P, 3], I32), e.ring("colx", 2, [P, 3], I32)
        G, X = e.ring("G", U, [P, EXT], F32), e.ring("X", U, [P, EXT], F32)
        gsb = e.ring("gsb", 2, [P, 2], F32)
        H, XB = e.ring("H", 4, [P, D], F32), e.ring("XB", 4, [P, D], F32)
        sel, mask = e.ring("sel", 2, [P, SEL], F32), e.ring("mask", 2, [P, SEL], F32)
        carry = e.ring("carry", 2, [P, C], F32)
        Thi, Tlo = e.ring("Thi", 2, [P, C, P], F32R), e.ring("Tlo", 2, [P, C, P], F32R)
        Hhi, Hlo = e.ring("Hhi", 2, [P, C, P], F32R), e.ring("Hlo", 2, [P, C, P], F32R)
        rows = e.ring("rows", 2, [P, EXT], F32)
        ylen = e.ring("ylen", 2, [P, 1], F32)
        ln_y, ln_x = Norm(e, "lny"), Norm(e, "lnx")
        psum_t = [e.ps(f"pt{i}", [P, 2, 512]) for i in range(2)]
        psum_h = [e.ps(f"ph{i}", [P, C, P]) for i in range(2)]
        psum_o = [e.ps(f"po{i}", [P, D]) for i in range(2)]

        s_load, s_const, s_hi, s_prep = (e.sem(n) for n in ("s_load", "s_const", "s_hi", "s_prep"))
        s_ones, s_has = e.sem("s_ones"), e.sems("s_has", 2)
        s_col, s_colx = e.sem("s_col"), e.sem("s_colx")
        s_G, s_X, s_put = e.sems("s_G", U), e.sems("s_X", U), e.sems("s_put", 2)
        s_gsb, s_Gn, s_H, s_XB = (e.sem(n) for n in ("s_gsb", "s_Gn", "s_H", "s_XB"))
        s_sel, s_mask = e.sem("s_sel"), e.sem("s_mask")
        s_summed, s_carried, s_copied = e.sem("s_summed"), e.sem("s_carried"), e.sem("s_copied")
        s_turned = e.sem("s_turned")
        s_Thi, s_Tlo, s_Hhi, s_Hlo = (e.sem(n) for n in ("s_Thi", "s_Tlo", "s_Hhi", "s_Hlo"))
        s_prod, s_y, s_cent, s_rows = (e.sem(n) for n in ("s_prod", "s_y", "s_cent", "s_rows"))
        tick = e.sem("tick")
        block = ctx.enter_context(e.block())

        @block.sync
        def _(sp):
            sp.dma_start(gamma[:, :], io.L2_gamma.partition_broadcast(P)).then_inc(s_load, 16)
            sp.dma_start(beta[:, :], io.L2_beta.partition_broadcast(P)).then_inc(s_load, 16)
            sp.dma_start(bf[0:2, :], io.L2_bs.partition_broadcast(2)).then_inc(s_load, 16)
            sp.dma_start(bf[2:4, :], io.L2_bn.partition_broadcast(2)).then_inc(s_load, 16)
            sp.wait_ge(s_load, 64)
            sp.wait_ge(s_ones, 1)

            def load_has(T):
                s = T.slot(2)
                wait(sp, s_prod, T.t - 1)
                sp.sem_inc(tick, 1)
                sp.dma_start(has[s][2:4, :].bitcast(F32), g.lastdram[:, bass.ds(T.t, 1), :]).then_inc(s_has[s], 16)

            def body(i):
                for u in range(U):
                    at(i, u, 2, U, NT, load_has)

            pipeline(sp, GR, 1, 0, body, between=lambda n: W.load_one(sp, n))

        @block.gpsimd
        def _(pool):
            def start_fetch(T):
                s = T.slot(U)
                wait(pool, s_summed, T.t - 3)
                wait(pool, s_H, T.t - 3)
                wait(pool, s_XB, T.t - 3)
                indices(pool, g, "S", T, col, 3, tick, s_col)
                pool.wait_ge(s_col, T.t + 1)
                pool.sem_inc(tick, 1)
                fetch(pool, G[s][:, :], src, col[s][:, 0:1]).then_inc(s_G[s], 16)
                fetch(pool, X[s][:, :], src, col[s][:, 2:3]).then_inc(s_X[s], 16)

            def keep_x(T):
                s = T.slot(U)
                pool.wait_ge(s_X[s], 16 * (T.use(U) + 1))
                wait(pool, s_rows, T.t - 3)
                pool.tensor_tensor(XB[s][:, :], X[s][:, 0:D], beta[:, :], ALU.add).then_inc(s_XB, 1)

            def length_y(T):
                wait(pool, s_rows, T.t - 1)
                ln_y.make_scale(pool, T, neg_half, ylen[T.slot(2)][:, :])

            def store(T):
                s = T.slot(2)
                wait(pool, s_put[s], 16 * T.use(2))
                ln_x.make_scale(pool, T, neg_half, rows[s][:, SCALE:SCALE + 1])
                indices(pool, g, "S", T, colx, 3, tick, s_colx)
                ln_x.make_bias(pool, tick, T, rows[s][:, SCALE:SCALE + 1], rows[s][:, BIAS:BIAS + 1])
                pool.wait_ge(s_colx, T.t + 1)
                pool.wait_ge(ln_x.s_bias, T.t + 1)
                pool.sem_inc(tick, 1)
                put_rows(pool, out, colx[s][:, 2:3], rows[s][:, :], N - 1).then_inc(s_put[s], 16)

            def body(i):
                for u in range(U):
                    at(i, u, -2, U, NT, store)
                    at(i, u, -1, U, NT, length_y)
                    at(i, u, 5, U, NT, start_fetch)
                    at(i, u, 2, U, NT, keep_x)

            pool.memset(ones_f[:, :], 1.0).then_inc(s_const, 1)
            pool.memset(neg_half[:, :], -0.5).then_inc(s_const, 1)
            for s in range(2):
                pool.memset(carry[s][:, :], 0.0).then_inc(s_const, 1)
                pool.memset(rows[s][:, BIAS + 1:EXT], 0.0).then_inc(s_const, 1)
            pool.wait_ge(s_const, 6)
            pool.wait_ge(s_load, 64)
            pipeline(pool, GR, 2, 1, body, between=lambda n: W.split_low(pool, n))
            for s in range(2):
                pool.wait_ge(s_put[s], 16 * (NT // 2))

        @block.scalar
        def _(act):
            def norm_in(T):
                s = T.slot(U)
                act.wait_ge(s_X[s], 16 * (T.use(U) + 1))
                wait(act, s_y, T.t - 3)
                nc.scalar.activation(H[s][:, :], X[s][:, 0:D], ACT.Relu, bias=X[s][:, BIAS:BIAS + 1],
                                     scale=X[s][:, SCALE:SCALE + 1]).then_inc(s_H, 1)
                act.wait_ge(s_gsb, T.t + 1)
                nc.scalar.activation(G[s][:, 0:D], G[s][:, 0:D], ACT.Relu, bias=gsb[T.slot(2)][:, 1:2],
                                     scale=gsb[T.slot(2)][:, 0:1]).then_inc(s_Gn, 1)

            def high_own(T):
                s = T.slot(2)
                act.wait_ge(s_turned, T.t + 1)
                wait(act, s_prod, T.t - 1)
                nc.scalar.copy(Hhi[s][:, :, :], psum_h[s][:, :, :]).then_inc(s_Hhi, 1)

            def high_sum(T):
                s = T.slot(2)
                act.wait_ge(s_copied, T.t + 1)
                nc.scalar.copy(chunks_of(Thi[s]), all_chunks(psum_t[s], 0, P)).then_inc(s_Thi, 1)

            def body(i):
                for u in range(U):
                    at(i, u, 1, U, NT, high_own)
                    at(i, u, 1, U, NT, high_sum)
                    at(i, u, 3, U, NT, norm_in)

            act.wait_ge(s_load, 64)
            nc.scalar.copy(br[:, :], bf[:, :]).then_inc(s_hi, 1)
            act.wait_ge(s_const, 1)
            nc.scalar.copy(has[0][:, :], ones_f[:, :])
            nc.scalar.copy(has[1][:, :], ones_f[:, :]).then_inc(s_ones, 1)
            pipeline(act, GR, 1, 0, body, between=lambda n: W.split_high(act, n))

        @block.vector
        def _(dve):
            def over_degree(T):
                s = T.slot(U)
                dve.wait_ge(s_G[s], 16 * (T.use(U) + 1))
                wait(dve, s_Gn, T.t - 1)
                dve.tensor_scalar(gsb[T.slot(2)][:, :], G[s][:, SCALE:BIAS + 1], g.rdeg[:, bass.ds(T.t, 1)],
                                  None, ALU.mult).then_inc(s_gsb, 1)

            def carried(T):
                carry_in(dve, T, psum_t, mask, carry, s_summed, s_mask, s_carried, s_copied)

            def low_own(T):
                s = T.slot(2)
                dve.wait_ge(s_Hhi, T.t + 1)
                dve.tensor_tensor(Hlo[s][:, :, :], psum_h[s][:, :, :], Hhi[s][:, :, :].bitcast(F32),
                                  ALU.subtract).then_inc(s_Hlo, 1)

            def low_sum(T):
                s = T.slot(2)
                dve.wait_ge(s_Thi, T.t + 1)
                dve.tensor_tensor(chunks_of(Tlo[s]), all_chunks(psum_t[s], 0, P), chunks_of(Thi[s]).bitcast(F32),
                                  ALU.subtract).then_inc(s_Tlo, 1)

            def select(T):
                selection(dve, g, "S", T, sel, mask, s_sel, s_mask, s_summed, s_carried)

            def add_own(T):
                s = T.slot(2)
                dve.wait_ge(s_prod, T.t + 1)
                dve.scalar_tensor_tensor(psum_o[s][:, :], psum_o[s][:, :], 0.0, H[T.slot(U)][:, :],
                                         ALU.max, ALU.add).then_inc(s_y, 1)
                dve.wait_ge(s_y, T.t + 1)
                ln_y.statistics(dve, T, psum_o[s][:, :])

            def center(T):
                s = T.slot(2)
                ln_y.finish(dve, tick, T)
                dve.scalar_tensor_tensor(psum_o[s][:, :], psum_o[s][:, :], ln_y.mean_var[s][:, 0:1], gamma[:, :],
                                         ALU.subtract, ALU.mult).then_inc(s_cent, 1)

            def new_rows(T):
                s = T.slot(2)
                dve.wait_ge(s_cent, T.t + 1)
                dve.wait_ge(ln_y.s_scale, T.t + 1)
                dve.wait_ge(s_XB, T.t + 1)
                wait(dve, s_put[s], 16 * T.use(2))
                dve.scalar_tensor_tensor(rows[s][:, 0:D], psum_o[s][:, :], ylen[s][:, 0:1], XB[T.slot(U)][:, :],
                                         ALU.mult, ALU.add).then_inc(s_rows, 1)

            def norm_rows(T):
                dve.wait_ge(s_rows, T.t + 1)
                ln_x.statistics(dve, T, rows[T.slot(2)][:, 0:D])

            def finish_rows(T):
                wait(dve, ln_x.s_bias, T.t - 1)
                ln_x.finish(dve, tick, T)

            def body(i):
                for u in range(U):
                    at(i, u, -1, U, NT, add_own)
                    at(i, u, 1, U, NT, carried)
                    at(i, u, -1, U, NT, center)
                    at(i, u, 1, U, NT, low_own)
                    at(i, u, -1, U, NT, new_rows)
                    at(i, u, 1, U, NT, low_sum)
                    at(i, u, -1, U, NT, norm_rows)
                    at(i, u, 3, U, NT, select)
                    at(i, u, 4, U, NT, over_degree)
                    at(i, u, -1, U, NT, finish_rows)

            dve.wait_ge(s_load, 64)
            dve.wait_ge(s_const, 6)
            dve.wait_ge(s_hi, 1)
            stack_bias(dve, g, bf, br[:, :].bitcast(F32), bias, s_prep, 0)
            pipeline(dve, GR, 1, 1, body)

        @block.tensor
        def _(pe):
            def sum_edges(T):
                s = T.slot(2)
                pe.wait_ge(s_sel, T.t + 1)
                pe.wait_ge(s_Gn, T.t + 1)
                wait(pe, s_Tlo, T.t - 1)
                for c in range(C):
                    cols = slice(c * P, (c + 1) * P)
                    ins = pe.matmul(chunk(psum_t[s], c, SEL), G[T.slot(U)][:, cols], sel[s][:, :],
                                    start=True, stop=True)
                ins.then_inc(s_summed, 1)
                pe.wait_ge(s_H, T.t + 1)
                wait(pe, s_Hlo, T.t - 1)
                for c in range(C):
                    ins = pe.transpose(psum_h[s][:, c, :], H[T.slot(4)][:, c * P:(c + 1) * P], g.ident[:, :])
                ins.then_inc(s_turned, 1)

            def multiply(T):
                s = T.slot(2)
                pe.wait_ge(s_has[s], 16 * (T.use(2) + 1))
                wait(pe, s_rows, T.t - 1)
                pe.matmul(psum_o[s][:, :], has[s][:, :], bias[:, :], start=True, stop=False)
                pe.wait_ge(s_Hlo, T.t + 1)
                product(pe, psum_o[s][:, :], Hhi[s], Hlo[s], g.Whi[1], g.Wlo[1], False, False)
                pe.wait_ge(s_Tlo, T.t + 1)
                product(pe, psum_o[s][:, :], Thi[s], Tlo[s], g.Whi[0], g.Wlo[0], False, True).then_inc(s_prod, 1)

            def body(i):
                for u in range(U):
                    at(i, u, 1, U, NT, sum_edges)
                    at(i, u, 0, U, NT, multiply)

            pe.wait_ge(s_prep, 3)
            pipeline(pe, GR, 1, 0, body)



def layer3(nc, io, g):
    NT, N = g.NT, g.N
    U = 4
    GR = NT // U
    ENDS = ("src", "dst")
    INDEX = {"src": 1, "dst": 0}
    with ExitStack() as ctx:
        e = Env(nc, ctx, "f_")
        src = g.xs[2]
        b3f, b3r, b3 = e.sb("b3f", [2, D], F32), e.sb("b3r", [2, D], F32R), e.sb("b3", [2, D], F32R)
        ones1, ones_f = e.sb("ones1", [2, P], F32R), e.sb("onesf", [P, P], F32)
        col, colx = e.ring("col", U, [P, 3], I32), e.ring("colx", U, [P, 3], I32)
        G = {k: e.ring("G" + k, U, [P, EXT], F32) for k in ENDS}
        X = e.ring("X", U, [P, EXT], F32)
        Hhi = {k: e.ring("Hhi" + k, 2, [P, C, P], F32R) for k in ENDS}
        Hlo = {k: e.ring("Hlo" + k, 2, [P, C, P], F32R) for k in ENDS}
        sel, lastsel = e.ring("sel", 2, [P, SEL], F32R), e.ring("lastsel", 2, [P, P], F32R)
        Mhi, Mlo = e.ring("Mhi", 2, [P, D], F32R), e.ring("Mlo", 2, [P, D], F32R)
        carry = e.ring("carry", 2, [P, D], F32)
        rows = e.ring("rows", 2, [P, D], F32)
        psum_h = {k: e.ps("ph" + k, [P, C, P]) for k in ENDS}
        psum_m = [e.ps(f"pm{i}", [P, D]) for i in range(2)]
        psum_o = [e.ps(f"po{i}", [P, D]) for i in range(2)]
        psum_c = [e.ps(f"pc{i}", [P, D]) for i in range(2)]

        s_load, s_const, s_hi, s_prep = (e.sem(n) for n in ("s_load", "s_const", "s_hi", "s_prep"))
        s_col, s_colx = e.sem("s_col"), e.sem("s_colx")
        s_G = {k: e.sems("s_G" + k, U) for k in ENDS}
        s_X, s_put = e.sems("s_X", U), e.sems("s_put", U)
        s_Gn, s_turned, s_Hhi, s_Hlo = ({k: e.sem(n + k) for k in ENDS} for n in ("s_Gn", "s_turned", "s_Hhi", "s_Hlo"))
        s_sel, s_msg, s_Mhi, s_Mlo, s_sum, s_carry, s_added, s_rows = (
            e.sem(n) for n in ("s_sel", "s_msg", "s_Mhi", "s_Mlo", "s_sum", "s_carry", "s_added", "s_rows"))
        tick = e.sem("tick")
        block = ctx.enter_context(e.block())

        @block.sync
        def _(sp):
            sp.dma_start(b3f[:, :], io.L3_b.partition_broadcast(2)).then_inc(s_load, 16)
            sp.wait_ge(s_load, 16)

        @block.gpsimd
        def _(pool):
            def start_fetch(T):
                s = T.slot(U)
                for k in ENDS:
                    wait(pool, s_turned[k], T.t - 3)
                indices(pool, g, "S", T, col, 3, tick, s_col)
                pool.wait_ge(s_col, T.t + 1)
                pool.sem_inc(tick, 1)
                for k in ENDS:
                    n = INDEX[k]
                    fetch(pool, G[k][s][:, :], src, col[s][:, n:n + 1]).then_inc(s_G[k][s], 16)

            def fetch_x(T):
                s = T.slot(U)
                wait(pool, s_rows, T.t - 3)
                wait(pool, s_put[s], 16 * T.use(U))
                indices(pool, g, "S", T, colx, 3, tick, s_colx)
                pool.wait_ge(s_colx, T.t + 1)
                pool.sem_inc(tick, 1)
                fetch(pool, X[s][:, :], src, colx[s][:, 2:3]).then_inc(s_X[s], 16)

            def store(T):
                s = T.slot(U)
                pool.wait_ge(s_rows, T.t + 1)
                pool.sem_inc(tick, 1)
                put_rows(pool, io.out, colx[s][:, 2:3], rows[T.slot(2)][:, :], N - 1).then_inc(s_put[s], 16)

            def body(i):
                for u in range(U):
                    at(i, u, 6, U, NT, start_fetch)
                    at(i, u, 0, U, NT, fetch_x)
                    at(i, u, -3, U, NT, store)

            pool.memset(ones_f[:, :], 1.0).then_inc(s_const, 1)
            for s in range(2):
                pool.memset(carry[s][:, :], 0.0).then_inc(s_const, 1)
            pipeline(pool, GR, 2, 1, body)
            for s in range(U):
                pool.wait_ge(s_put[s], 16 * GR)

        @block.scalar
        def _(act):
            def norm_in(T):
                s = T.slot(U)
                for k in ENDS:
                    act.wait_ge(s_G[k][s], 16 * (T.use(U) + 1))
                    nc.scalar.activation(G[k][s][:, 0:D], G[k][s][:, 0:D], ACT.Relu, bias=G[k][s][:, BIAS:BIAS + 1],
                                         scale=G[k][s][:, SCALE:SCALE + 1]).then_inc(s_Gn[k], 1)

            def high(T):
                s = T.slot(2)
                for k in ENDS:
                    act.wait_ge(s_turned[k], T.t + 1)
                    wait(act, s_msg, T.t - 1)
                    nc.scalar.copy(Hhi[k][s][:, :, :], psum_h[k][:, :, :]).then_inc(s_Hhi[k], 1)

            def message(T):
                s = T.slot(2)
                act.wait_ge(s_msg, T.t + 1)
                wait(act, s_sum, T.t - 1)
                nc.scalar.activation(Mhi[s][:, :], psum_m[s][:, :], ACT.Relu).then_inc(s_Mhi, 1)

            def body(i):
                for u in range(U):
                    at(i, u, -1, U, NT, message)
                    at(i, u, 1, U, NT, high)
                    at(i, u, 3, U, NT, norm_in)

            act.wait_ge(s_load, 16)
            nc.scalar.copy(b3r[:, :], b3f[:, :]).then_inc(s_hi, 1)
            act.wait_ge(s_const, 1)
            nc.scalar.copy(ones1[:, :], ones_f[0:2, :]).then_inc(s_hi, 1)
            pipeline(act, GR, 1, 1, body)

        @block.vector
        def _(dve):
            def low(T):
                s = T.slot(2)
                for k in ENDS:
                    dve.wait_ge(s_Hhi[k], T.t + 1)
                    dve.tensor_tensor(Hlo[k][s][:, :, :], psum_h[k][:, :, :], Hhi[k][s][:, :, :].bitcast(F32),
                                      ALU.subtract).then_inc(s_Hlo[k], 1)

            def select(T):
                s = T.slot(2)
                wait(dve, s_sum, T.t - 1)
                dve.tensor_scalar(lastsel[s][:, :], ones_f[:, :], g.in_last[:, bass.ds(T.t, 1)], None, ALU.mult)
                selection(dve, g, "S", T, sel, None, s_sel, None, s_sum, None)

            def message(T):
                s = T.slot(2)
                dve.wait_ge(s_Mhi, T.t + 1)
                dve.scalar_tensor_tensor(Mlo[s][:, :], psum_m[s][:, :], 0.0, Mhi[s][:, :].bitcast(F32),
                                         ALU.max, ALU.subtract).then_inc(s_Mlo, 1)

            def combine(T):
                s, before = T.slot(2), (T.j - 1) % 2
                one = bass.ds(T.t, 1)
                dve.wait_ge(s_sum, T.t + 1)
                wait(dve, s_carry, T.t)
                dve.scalar_tensor_tensor(carry[s][:, :], carry[before][:, :], g.same_last[:, one], psum_c[s][:, :],
                                         ALU.mult, ALU.add).then_inc(s_carry, 1)
                dve.scalar_tensor_tensor(psum_o[s][:, :], carry[before][:, :], g.takes[:, one], psum_o[s][:, :],
                                         ALU.mult, ALU.add).then_inc(s_added, 1)
                dve.wait_ge(s_added, T.t + 1)
                dve.wait_ge(s_X[T.slot(U)], 16 * (T.use(U) + 1))
                wait(dve, s_put[(T.j - 2) % U], 16 * (T.k + 1 if T.j >= 2 else T.k))
                dve.tensor_tensor(rows[s][:, :], psum_o[s][:, :], X[T.slot(U)][:, 0:D], ALU.add).then_inc(s_rows, 1)

            def body(i):
                for u in range(U):
                    at(i, u, -1, U, NT, message)
                    at(i, u, 1, U, NT, low)
                    at(i, u, -2, U, NT, combine)
                    at(i, u, 0, U, NT, select)

            dve.wait_ge(s_const, 3)
            dve.wait_ge(s_hi, 1)
            stack_bias(dve, g, b3f, b3r[:, :].bitcast(F32), b3, s_prep, 0)
            pipeline(dve, GR, 1, 1, body)

        @block.tensor
        def _(pe):
            def turn(T):
                for k in ENDS:
                    pe.wait_ge(s_Gn[k], T.t + 1)
                    wait(pe, s_Hlo[k], T.t)
                    for c in range(C):
                        ins = pe.transpose(psum_h[k][:, c, :], G[k][T.slot(U)][:, c * P:(c + 1) * P], g.ident[:, :])
                    ins.then_inc(s_turned[k], 1)

            def multiply(T):
                s = T.slot(2)
                wait(pe, s_Mlo, T.t - 1)
                pe.matmul(psum_m[s][:, :], ones1[:, :], b3[:, :], start=True, stop=False)
                for n, k in enumerate(ENDS):
                    pe.wait_ge(s_Hlo[k], T.t + 1)
                    ins = product(pe, psum_m[s][:, :], Hhi[k][s], Hlo[k][s], g.Whi[2 + n], g.Wlo[2 + n], False, n == 1)
                ins.then_inc(s_msg, 1)

            def sum_edges(T):
                s = T.slot(2)
                pe.wait_ge(s_sel, T.t + 1)
                pe.wait_ge(s_Mlo, T.t + 1)
                wait(pe, s_rows, T.t - 1)
                pe.matmul(psum_o[s][:, :], sel[s][:, 0:P], Mhi[s][:, :], start=True, stop=False)
                pe.matmul(psum_o[s][:, :], sel[s][:, 0:P], Mlo[s][:, :], start=False, stop=True)
                pe.matmul(psum_c[s][:, :], lastsel[s][:, :], Mhi[s][:, :], start=True, stop=False)
                pe.matmul(psum_c[s][:, :], lastsel[s][:, :], Mlo[s][:, :], start=False, stop=True).then_inc(s_sum, 1)

            def body(i):
                for u in range(U):
                    at(i, u, 1, U, NT, turn)
                    at(i, u, -2, U, NT, sum_edges)
                    at(i, u, 0, U, NT, multiply)

            pe.wait_ge(s_hi, 2)
            pe.wait_ge(s_prep, 3)
            pipeline(pe, GR, 1, 1, body)


WEIGHTS = {"L0_W1": "L0_gnn_W1", "L0_W2": "L0_gnn_W2", "L1_W1": "L1_gnn_W1", "L1_W2": "L1_gnn_W2",
           "L2_Ws": "L2_gnn_W_self", "L2_Wn": "L2_gnn_W_neigh", "L3_W": "L3_gnn_W"}
VECTORS = {"L0_b1": "L0_gnn_b1", "L0_b2": "L0_gnn_b2", "L1_b1": "L1_gnn_b1", "L1_b2": "L1_gnn_b2",
           "L1_gamma": "L1_gnn_gamma", "L1_beta": "L1_gnn_beta", "L2_bs": "L2_gnn_b_self",
           "L2_bn": "L2_gnn_b_neigh", "L2_gamma": "L2_gnn_ln_gamma", "L2_beta": "L2_gnn_ln_beta",
           "L3_b": "L3_gnn_b"}


class Named:
    pass


def program(nc, io, N):
    NT = N // P
    g = Named()
    g.NT, g.N = NT, N

    def dram(name, shape, dt=F32):
        return nc.dram_tensor(name, shape, dt, kind="Internal").ap()

    g.h1 = dram("h1", [N, D])
    g.xs = [dram(f"x{n}", [N, EXT]) for n in range(1, 4)]
    g.sorted = {k: dram("sorted" + k, [N + P, 4]) for k in "DS"}
    g.seldram = {k: dram("sel" + k, [NT, SEL], I16) for k in "DS"}
    g.degdram = dram("degdram", [4, NT, P])
    g.lastdram, g.qdram = dram("lastdram", [2, NT, P]), dram("qdram", [NT, P], I16)
    with ExitStack() as ctx:
        e = Env(nc, ctx, "")
        parts = e.sb("parts", [P, 8, C, D], F32R)
        g.parts = parts[:, :, :, :].rearrange("p w c n -> p (w c n)")
        g.Whi, g.Wlo = ([parts[:, 2 * slot + half] for slot in range(4)] for half in range(2))
        g.ident = e.sb("ident", [P, P], F32)
        g.hilo = e.sb("hilo", [4, 2], F32)
        g.selrows = {k: e.sb("selrows" + k, [P, NT, SEL], I16) for k in "DS"}
        g.index = {k: e.sb("index" + k, [P, NT, 3], I32) for k in "DS"}
        g.keycol, g.keylast, g.keyprev = (
            {k: e.sb(n + k, [P, NT], F32) for k in "DS"} for n in ("keycol", "keylast", "keyprev"))
        g.degcol, g.rdeg = e.sb("degcol", [P, NT], F32), e.sb("rdeg", [P, NT], F32)
        g.same_last, g.takes, g.in_last = (e.sb(n, [P, NT], F32) for n in ("samelast", "takes", "inlast"))
        g.iota_f, g.node_f = e.sb("iotaf", [P, P], F32), e.sb("nodef", [P, NT], F32)
        g.pidx, g.minus_p = e.sb("pidx", [P, 1], F32), e.sb("minusp", [P, 1], F32)
        g.rank_hi = {n: e.sb("rankhi" + n, [P, NT], F32) for n in "zq"}
        g.rank_lo = {n: e.sb("ranklo" + n, [P, NT], F32) for n in "zq"}
        g.minus_prev, g.minus_key, g.minus_q = (e.sb(n, [P, NT], F32) for n in ("minusprev", "minuskey", "minusq"))
        g.lastc, g.listed = e.sb("lastc", [P, NT], F32), e.sb("listed", [NT, P], F32)
        prepare_orders(nc, io, g)
        layer0(nc, io, g, False)
        layer0(nc, io, g, True)
        layer1(nc, io, g)
        layer2(nc, io, g)
        layer3(nc, io, g)


def kernel(**inputs):
    import numpy as np
    import concourse.bacc as bacc
    from concourse.bass_utils import run_bass_kernel_spmd

    x, src, dst = (np.asarray(inputs[n]) for n in ("x", "src", "dst"))
    nodes = x.shape[0]
    N = -(-nodes // (8 * P)) * 8 * P
    loops = np.arange(nodes, N, dtype=src.dtype)
    src, dst = np.concatenate([src, loops]), np.concatenate([dst, loops])
    arrays = {"x": np.concatenate([x, np.zeros((N - nodes, D), x.dtype)]), "src": src, "dst": dst,
              "src_col": np.ascontiguousarray(src.reshape(-1, P).T),
              "dst_col": np.ascontiguousarray(dst.reshape(-1, P).T),
              "eps": np.asarray(inputs["L1_gnn_eps"]).reshape(1)}
    for name, given in WEIGHTS.items():
        arrays[name] = np.ascontiguousarray(np.asarray(inputs[given]).T)
    for name, given in VECTORS.items():
        arrays[name] = np.asarray(inputs[given])
    arrays["L1_b1col"] = np.ascontiguousarray(arrays.pop("L1_b1").reshape(C, P).T)

    nc = bacc.Bacc("TRN2", target_bir_lowering=False, num_devices=1)
    io = Named()
    for name, a in arrays.items():
        io.__dict__[name] = nc.dram_tensor("in_" + name, a.shape, mybir.dt.from_np(a.dtype), kind="ExternalInput").ap()
    io.out = nc.dram_tensor("out_x", (N, D), F32, kind="ExternalOutput").ap()
    program(nc, io, N)
    r = run_bass_kernel_spmd(nc, [{"in_" + name: a for name, a in arrays.items()}], core_ids=[0])
    return r.results[0]["out_x"][0:nodes]
```
